# Optimizing a Trainium2 kernel written in Bass

```python
import numpy as np
import jax
import jax.numpy as jnp

def _softmax(x, axis=-1):
    return jax.nn.softmax(x, axis=axis)

def _gelu(x):
    return jax.nn.gelu(x, approximate=True)

def _silu(x):
    return jax.nn.silu(x)

def _sigmoid(x):
    return jax.nn.sigmoid(x)

def _layernorm(x, axis=-1, eps=1e-05):
    m = jnp.mean(x, axis=axis, keepdims=True)
    v = jnp.var(x, axis=axis, keepdims=True)
    return (x - m) / jnp.sqrt(v + eps)

def _scatter_add(tgt, idx, src, axis=0):
    return tgt.at[idx].add(src)

def _segment_sum(src, seg, n):
    return jax.ops.segment_sum(src, seg, n)
kernel_name = 'mk_audio_tower_d2_tok_audfeat4096_r4_3700bc'

def setup_inputs(seed: int=0):
    np.random.seed(seed)
    _w = jnp.asarray

    def _rec_inputs():
        import jax
        import jax.numpy as jnp
        _rk = jax.random.key(seed)
        x = 7.22013e-05 + 1.00017 * jax.random.normal(jax.random.fold_in(_rk, 1), (16, 64, 2048), jnp.float32)
        return x
    x = _rec_inputs()

    def _L0_tok_setup():
        import jax, jax.numpy as jnp
        import numpy as np
        EPS = 1e-05

        def conv1d(x, w, stride=1, pad=0, groups=1):
            return jax.lax.conv_general_dilated(x, w, window_strides=(stride,), padding=[(pad, pad)], dimension_numbers=('NCH', 'OIH', 'NCH'), feature_group_count=groups)

        def groupnorm1(x, gamma, beta):
            m = jnp.mean(x, axis=(1, 2), keepdims=True)
            v = jnp.mean((x - m) ** 2, axis=(1, 2), keepdims=True)
            xn = (x - m) * jax.lax.rsqrt(v + EPS)
            return xn * gamma[None, :, None] + beta[None, :, None]
        key = jax.random.key(seed)
        ks = jax.random.split(key, 8)
        B, C_IN, T, H = (16, 64, 2048, 128)
        x = jax.random.normal(ks[0], (B, C_IN, T), dtype=jnp.float32)
        conv_in_w = jax.random.normal(ks[1], (H, C_IN, 7), dtype=jnp.float32) * 0.05
        dw_w = jax.random.normal(ks[2], (H, 1, 5), dtype=jnp.float32) * 0.1
        dw_b = jax.random.normal(ks[3], (H,), dtype=jnp.float32) * 0.01
        pw_w = jax.random.normal(ks[4], (H, H, 1), dtype=jnp.float32) * 0.04
        gn1_w = jnp.ones((H,), jnp.float32)
        gn1_b = jnp.zeros((H,), jnp.float32)
        gn2_w = jnp.ones((H,), jnp.float32)
        gn2_b = jnp.zeros((H,), jnp.float32)
        return {'x': x, 'conv_in_w': conv_in_w, 'dw_w': dw_w, 'dw_b': dw_b, 'pw_w': pw_w, 'gn1_w': gn1_w, 'gn1_b': gn1_b, 'gn2_w': gn2_w, 'gn2_b': gn2_b}
    _L0_tok_all = _L0_tok_setup()
    _L0_tok_in = {k: v for k, v in _L0_tok_all.items() if k in ('conv_in_w', 'dw_w', 'dw_b', 'pw_w', 'gn1_w', 'gn1_b', 'gn2_w', 'gn2_b')}
    del _L0_tok_all

    def _L0_attn_setup():
        import jax, jax.numpy as jnp
        import numpy as np
        B, S, H = (2, 512, 1024)
        NH, NKV, HD = (32, 8, 128)
        GROUPS = NH // NKV
        ROPE_BASE = 500000.0

        def _rope_tables(seq_len, dim, dtype):
            inv_freq = 1.0 / ROPE_BASE ** (jnp.arange(0, dim, 2, dtype=jnp.float32) / dim)
            t = jnp.arange(seq_len, dtype=jnp.float32)
            freqs = jnp.einsum('i,j->ij', t, inv_freq)
            emb = jnp.concatenate([freqs, freqs], axis=-1)
            return (jnp.cos(emb).astype(dtype), jnp.sin(emb).astype(dtype))

        def _rotate_half(x):
            x1, x2 = jnp.split(x, 2, axis=-1)
            return jnp.concatenate([-x2, x1], axis=-1)
        key = jax.random.key(seed)
        ks = jax.random.split(key, 5)
        sc = 0.02
        return {'hidden_states': jax.random.normal(ks[0], (B, S, H), jnp.float32), 'Wq': jax.random.normal(ks[1], (NH * HD, H), jnp.float32) * sc, 'Wk': jax.random.normal(ks[2], (NKV * HD, H), jnp.float32) * sc, 'Wv': jax.random.normal(ks[3], (NKV * HD, H), jnp.float32) * sc, 'Wo': jax.random.normal(ks[4], (H, NH * HD), jnp.float32) * sc}
    _L0_attn_all = _L0_attn_setup()
    _L0_attn_in = {k: v for k, v in _L0_attn_all.items() if k in ('Wq', 'Wk', 'Wv', 'Wo')}
    del _L0_attn_all

    def _L0_ffn_setup():
        import jax, jax.numpy as jnp
        import numpy as np
        R = 16
        LORA_ALPHA = 16
        SCALING = LORA_ALPHA / R
        key = jax.random.key(seed)
        kx, kr, ka = jax.random.split(key, 3)
        B, S, D, DO, E = (4, 512, 1024, 1024, 8)
        x = jax.random.normal(kx, (B, S, D), dtype=jnp.float32)
        bound_r = 1.0 / np.sqrt(D)
        route_w = jax.random.uniform(kr, (E, D), jnp.float32, -bound_r, bound_r)
        bound_a = 1.0 / np.sqrt(D)
        A = jax.random.uniform(ka, (E, R, D), jnp.float32, -bound_a, bound_a)
        kb = jax.random.fold_in(key, 7)
        Bw = jax.random.normal(kb, (E, DO, R), dtype=jnp.float32) * 0.02
        return {'x': x, 'route_w': route_w, 'A': A, 'Bw': Bw}
    _L0_ffn_all = _L0_ffn_setup()
    _L0_ffn_in = {k: v for k, v in _L0_ffn_all.items() if k in ('route_w', 'A', 'Bw')}
    del _L0_ffn_all

    def _L1_attn_setup():
        import jax, jax.numpy as jnp
        import numpy as np
        import math
        FACTOR = 1
        key = jax.random.key(seed)
        x = jax.random.normal(key, (8, 128, 1024), dtype=jnp.float32)
        return {'x': x}
    _L1_attn_all = _L1_attn_setup()
    _L1_attn_in = {k: v for k, v in _L1_attn_all.items() if k in ()}
    del _L1_attn_all

    def _L1_ffn_setup():
        import jax, jax.numpy as jnp
        import numpy as np
        import math
        E, DK, R = (8, 32, 16)
        SCALING = 16.0 / 16.0
        key = jax.random.key(seed)
        ks = jax.random.split(key, 7)
        Bt, S, Din, Dout = (4, 512, 1024, 1024)
        x = jax.random.normal(ks[0], (Bt, S, Din), jnp.float32)
        W = jax.random.normal(ks[1], (Dout, Din), jnp.float32) * 0.02
        b = jnp.zeros((Dout,), jnp.float32)
        Wq = jax.random.normal(ks[2], (E * DK, Din), jnp.float32) * 0.02
        Wk = jax.random.normal(ks[3], (E * DK, Din), jnp.float32) * 0.02
        A = jax.random.normal(ks[4], (E, R, Din), jnp.float32) * 0.02
        Bm = jax.random.normal(ks[5], (E, Dout, R), jnp.float32) * 0.02
        return {'x': x, 'W': W, 'b': b, 'Wq': Wq, 'Wk': Wk, 'A': A, 'Bm': Bm}
    _L1_ffn_all = _L1_ffn_setup()
    _L1_ffn_in = {k: v for k, v in _L1_ffn_all.items() if k in ('W', 'b', 'Wq', 'Wk', 'A', 'Bm')}
    del _L1_ffn_all
    return {'x': x, 'L0_tok_conv_in_w': _L0_tok_in['conv_in_w'], 'L0_tok_dw_w': _L0_tok_in['dw_w'], 'L0_tok_dw_b': _L0_tok_in['dw_b'], 'L0_tok_pw_w': _L0_tok_in['pw_w'], 'L0_tok_gn1_w': _L0_tok_in['gn1_w'], 'L0_tok_gn1_b': _L0_tok_in['gn1_b'], 'L0_tok_gn2_w': _L0_tok_in['gn2_w'], 'L0_tok_gn2_b': _L0_tok_in['gn2_b'], 'L0_attn_Wq': _L0_attn_in['Wq'], 'L0_attn_Wk': _L0_attn_in['Wk'], 'L0_attn_Wv': _L0_attn_in['Wv'], 'L0_attn_Wo': _L0_attn_in['Wo'], 'L0_ffn_route_w': _L0_ffn_in['route_w'], 'L0_ffn_A': _L0_ffn_in['A'], 'L0_ffn_Bw': _L0_ffn_in['Bw'], 'L1_ffn_W': _L1_ffn_in['W'], 'L1_ffn_b': _L1_ffn_in['b'], 'L1_ffn_Wq': _L1_ffn_in['Wq'], 'L1_ffn_Wk': _L1_ffn_in['Wk'], 'L1_ffn_A': _L1_ffn_in['A'], 'L1_ffn_Bm': _L1_ffn_in['Bm']}

def reference(x, L0_tok_conv_in_w, L0_tok_dw_w, L0_tok_dw_b, L0_tok_pw_w, L0_tok_gn1_w, L0_tok_gn1_b, L0_tok_gn2_w, L0_tok_gn2_b, L0_attn_Wq, L0_attn_Wk, L0_attn_Wv, L0_attn_Wo, L0_ffn_route_w, L0_ffn_A, L0_ffn_Bw, L1_ffn_W, L1_ffn_b, L1_ffn_Wq, L1_ffn_Wk, L1_ffn_A, L1_ffn_Bm):
    import jax
    import jax.numpy as jnp

    def _L0_tok_ref(x, conv_in_w, dw_w, dw_b, pw_w, gn1_w, gn1_b, gn2_w, gn2_b):
        import jax, jax.numpy as jnp
        import numpy as np
        EPS = 1e-05

        def conv1d(x, w, stride=1, pad=0, groups=1):
            return jax.lax.conv_general_dilated(x, w, window_strides=(stride,), padding=[(pad, pad)], dimension_numbers=('NCH', 'OIH', 'NCH'), feature_group_count=groups)

        def groupnorm1(x, gamma, beta):
            m = jnp.mean(x, axis=(1, 2), keepdims=True)
            v = jnp.mean((x - m) ** 2, axis=(1, 2), keepdims=True)
            xn = (x - m) * jax.lax.rsqrt(v + EPS)
            return xn * gamma[None, :, None] + beta[None, :, None]
        H = conv_in_w.shape[0]
        h = conv1d(x, conv_in_w, stride=1, pad=3)
        h = jax.nn.gelu(groupnorm1(h, gn1_w, gn1_b), approximate=False)
        h = conv1d(h, dw_w, stride=2, pad=2, groups=H) + dw_b[None, :, None]
        h = conv1d(h, pw_w)
        h = jax.nn.gelu(groupnorm1(h, gn2_w, gn2_b), approximate=False)
        return h

    def _L0_attn_ref(hidden_states, Wq, Wk, Wv, Wo):
        import jax, jax.numpy as jnp
        import numpy as np
        B, S, H = (2, 512, 1024)
        NH, NKV, HD = (32, 8, 128)
        GROUPS = NH // NKV
        ROPE_BASE = 500000.0

        def _rope_tables(seq_len, dim, dtype):
            inv_freq = 1.0 / ROPE_BASE ** (jnp.arange(0, dim, 2, dtype=jnp.float32) / dim)
            t = jnp.arange(seq_len, dtype=jnp.float32)
            freqs = jnp.einsum('i,j->ij', t, inv_freq)
            emb = jnp.concatenate([freqs, freqs], axis=-1)
            return (jnp.cos(emb).astype(dtype), jnp.sin(emb).astype(dtype))

        def _rotate_half(x):
            x1, x2 = jnp.split(x, 2, axis=-1)
            return jnp.concatenate([-x2, x1], axis=-1)
        bsz, q_len, _ = hidden_states.shape
        q = (hidden_states @ Wq.T).reshape(bsz, q_len, NH, HD).transpose(0, 2, 1, 3)
        k = (hidden_states @ Wk.T).reshape(bsz, q_len, NKV, HD).transpose(0, 2, 1, 3)
        v = (hidden_states @ Wv.T).reshape(bsz, q_len, NKV, HD).transpose(0, 2, 1, 3)
        cos, sin = _rope_tables(q_len, HD, hidden_states.dtype)
        q = q * cos + _rotate_half(q) * sin
        k = k * cos + _rotate_half(k) * sin
        qg = q.reshape(bsz, NKV, GROUPS, q_len, HD)
        scores = jnp.einsum('bgrqd,bgkd->bgrqk', qg, k) / jnp.sqrt(jnp.asarray(HD, q.dtype))
        attn = jax.nn.softmax(scores.astype(jnp.float32), axis=-1).astype(q.dtype)
        out = jnp.einsum('bgrqk,bgkd->bgrqd', attn, v)
        out = out.reshape(bsz, NH, q_len, HD).transpose(0, 2, 1, 3).reshape(bsz, q_len, NH * HD)
        return out @ Wo.T

    def _L0_ffn_ref(x, route_w, A, Bw):
        import jax, jax.numpy as jnp
        import numpy as np
        R = 16
        LORA_ALPHA = 16
        SCALING = LORA_ALPHA / R
        logits = jnp.einsum('bsd,ed->bse', x, route_w)
        topk_v, topk_idx = jax.lax.top_k(logits, 1)
        E = logits.shape[-1]
        route_weight = jax.nn.one_hot(topk_idx[..., 0], E, dtype=logits.dtype) * topk_v
        h = jnp.einsum('bsd,erd->bser', x, A)
        wh = route_weight[..., None] * h
        out = jnp.einsum('bser,eor->bso', wh, Bw) * SCALING
        return out

    def _L1_attn_ref(x):
        import jax, jax.numpy as jnp
        import numpy as np
        import math
        FACTOR = 1
        B, C, L = x.shape
        xh = x[:, None]
        f = jnp.fft.rfft(xh, axis=-1)
        corr = jnp.fft.irfft(f * jnp.conj(f), n=L, axis=-1)
        top_k = int(FACTOR * math.log(L))
        weights, delay = jax.lax.top_k(corr, top_k)
        tmp_corr = jax.nn.softmax(weights, axis=-1)
        init_index = jnp.arange(L)
        idx = (init_index[None, None, None, None, :] + delay[..., None]) % L
        pattern = jnp.take_along_axis(xh[:, :, :, None, :], idx, axis=-1)
        delays_agg = jnp.sum(pattern * tmp_corr[..., None], axis=-2)
        return delays_agg[:, 0]

    def _L1_ffn_ref(x, W, b, Wq, Wk, A, Bm):
        import jax, jax.numpy as jnp
        import numpy as np
        import math
        E, DK, R = (8, 32, 16)
        SCALING = 16.0 / 16.0
        Bt, S, Din = x.shape
        result = jnp.einsum('bsi,oi->bso', x, W) + b
        q = jnp.einsum('bsi,ni->bsn', x, Wq).reshape(Bt, S, E, DK)
        k = jnp.einsum('bsi,ni->bsn', x, Wk).reshape(Bt, S, E, DK)
        scores = jnp.einsum('bsed,bsed->bse', q, k) / math.sqrt(DK)
        w = jax.nn.softmax(scores, axis=-1)
        h = jnp.einsum('bsi,eri->bser', x, A)
        combined = jnp.einsum('bse,bser,eor->bso', w, h, Bm) * SCALING
        return result + combined
    h = _L0_tok_ref(x, L0_tok_conv_in_w, L0_tok_dw_w, L0_tok_dw_b, L0_tok_pw_w, L0_tok_gn1_w, L0_tok_gn1_b, L0_tok_gn2_w, L0_tok_gn2_b)
    h = h + _L0_attn_ref(_layernorm(h, axis=-1), L0_attn_Wq, L0_attn_Wk, L0_attn_Wv, L0_attn_Wo)
    h = h + _L0_ffn_ref(_layernorm(h, axis=-1), L0_ffn_route_w, L0_ffn_A, L0_ffn_Bw)
    h = h + _L1_attn_ref(_layernorm(h, axis=-1))
    h = h + _L1_ffn_ref(_layernorm(h, axis=-1), L1_ffn_W, L1_ffn_b, L1_ffn_Wq, L1_ffn_Wk, L1_ffn_A, L1_ffn_Bm)
    return h

_drawn_inputs = setup_inputs


def setup_inputs(seed=0):
    import zlib

    import numpy as np

    out = dict(_drawn_inputs(seed))
    spreads = {'L0_tok_gn1_w': (1.0, 0.2),
     'L0_tok_gn1_b': (0.0, 0.1),
     'L0_tok_gn2_w': (1.0, 0.2),
     'L0_tok_gn2_b': (0.0, 0.1),
     'L1_ffn_b': (0.0, 0.1)}
    factors = {'L1_ffn_Wq': 8.0, 'L1_ffn_Wk': 8.0, 'L1_ffn_A': 5.11, 'L1_ffn_Bm': 5.121}
    for name, (base, spread) in spreads.items():
        noise = np.random.default_rng([zlib.crc32(name.encode()), seed]).standard_normal(out[name].shape)
        drawn = base * np.exp(spread * noise) if base else spread * noise
        out[name] = jnp.asarray(drawn.astype(out[name].dtype))
    for name, factor in factors.items():
        out[name] = (out[name] * factor).astype(out[name].dtype)
    return out
```

```python
from contextlib import ExitStack

import concourse.bass as bass
from concourse import mybir

F32 = mybir.dt.float32
F32R = mybir.dt.float32r
I32 = mybir.dt.int32
ALU = mybir.AluOpType
ACT = mybir.ActivationFunctionType
AX = mybir.AxisListType

P = 128
NB = 16
C_IN = 64
T_IN = 2048
L = 1024
KT = L // P
BANK = 512
EPS = 1e-5
TAPS, PAD = 7, 3
PAIRS = (TAPS + 1) // 2
DW, DW_PAD = 5, 2
RSQRT_SEED = 0x5F3759DF
NEWTON = 3
RSQRT_LINKS = 2 + NEWTON * 4


class Links:

    def __init__(self, engine, sem, base):
        self.engine, self.sem, self.base, self.n = engine, sem, base, 0

    def __call__(self, ins):
        self.n += 1
        ins.then_inc(self.sem, 1)
        self.engine.wait_ge(self.sem, self.base + self.n)


def rsqrt(e, y, v, t, link):
    link(e.tensor_scalar(t.bitcast(I32), v.bitcast(I32), 1, None, ALU.logical_shift_right))
    link(e.tensor_scalar(y.bitcast(I32), t.bitcast(I32), -1.0, float(RSQRT_SEED), ALU.mult, ALU.add))
    for _ in range(NEWTON):
        link(e.tensor_tensor(t, y, y, ALU.mult))
        link(e.tensor_tensor(t, t, v, ALU.mult))
        link(e.scalar_tensor_tensor(out=t, in0=t, scalar=3.0, in1=y, op0=ALU.subtract, op1=ALU.mult))
        link(e.tensor_scalar(y, t, -0.5, None, ALU.mult))


def row(ap3, i):
    return ap3[:, bass.ds(i, 1), :].rearrange("p a n -> p (a n)")


def prime(nc, sems):
    with nc.Block() as block:

        @block.sync
        def _(sp):
            for s in sems:
                sp.sem_inc(s, 1)


def after(engine, sem, count):
    engine.wait_ge(sem, count + 1)


def setup_constants(nc, ctx, ident, ones_mean):
    filled = ctx.enter_context(nc.semaphore("const_filled"))
    with nc.Block() as block:

        @block.gpsimd
        def _(pool):
            pool.memset(ident[:, :], 1.0).then_inc(filled, 1)
            pool.memset(ones_mean[:, :], 1.0 / P)
            pool.wait_ge(filled, 1)
            pool.affine_select(out=ident[:, :], in_=ident[:, :], compare_op=ALU.is_equal, fill=0.0,
                               base=0, pattern=[[-1, P]], channel_multiplier=1).then_inc(filled, 1)
            pool.wait_ge(filled, 2)


def conv_stage(nc, h, ident, ones_mean, x, conv_w, dw_w, chan, pw_wT):
    XW = T_IN + 2 * PAD + 2
    GW = T_IN + 2 * DW_PAD
    NCH = T_IN // BANK
    T2 = T_IN // 2
    LAST = NB + 3
    with ExitStack() as ctx:
        def sb(name, shape, dt=F32):
            return ctx.enter_context(nc.sbuf_tensor(name, shape, dt))

        def sem(name):
            return ctx.enter_context(nc.semaphore(name))

        x_in = [sb(f"cv_x{i}", [P, XW]) for i in range(2)]
        x_hi = [sb(f"cv_xhi{i}", [P, XW], F32R) for i in range(2)]
        x_lo = [sb(f"cv_xlo{i}", [P, XW], F32R) for i in range(2)]
        raw = [sb(f"cv_raw{i}", [P, T_IN]) for i in range(2)]
        g = sb("cv_g", [P, GW])
        y = sb("cv_y", [P, T2])
        y_hi = sb("cv_yhi", [P, T2], F32R)
        y_lo = sb("cv_ylo", [P, T2], F32R)
        cw = sb("cv_w", [P, PAIRS * P])
        cw_hi = sb("cv_whi", [P, PAIRS * P], F32R)
        cw_lo = sb("cv_wlo", [P, PAIRS * P], F32R)
        pw = sb("cv_pw", [P, P])
        pw_hi = sb("cv_pwhi", [P, P], F32R)
        pw_lo = sb("cv_pwlo", [P, P], F32R)
        dww = sb("cv_dww", [P, DW])
        ch = sb("cv_ch", [P, 5])
        dummy = sb("cv_dummy", [P, 1])
        st = [sb(f"cv_st{n}", [P, 4, 6]) for n in range(2)]
        mv = [sb(f"cv_mv{n}", [P, 2]) for n in range(2)]
        mean = [sb(f"cv_mean{n}", [P, 1]) for n in range(2)]
        dev = [sb(f"cv_dev{n}", [P, 1]) for n in range(2)]
        var = [sb(f"cv_var{n}", [P, 1]) for n in range(2)]
        tmp = [sb(f"cv_tmp{n}", [P, 1]) for n in range(2)]
        rstd = [sb(f"cv_rstd{n}", [P, 1]) for n in range(2)]
        scale = [sb(f"cv_scale{n}", [P, 1]) for n in range(2)]
        shift = [sb(f"cv_shift{n}", [P, 1]) for n in range(2)]
        cp = ctx.enter_context(nc.psum_tensor("cv_cp", [P, NCH, BANK], F32))
        pp = ctx.enter_context(nc.psum_tensor("cv_pp", [P, 2, BANK], F32))
        sp = [ctx.enter_context(nc.psum_tensor(f"cv_sp{n}", [P, BANK], F32)) for n in range(2)]

        w_loaded, pads, w_hi_done, w_lo_done = sem("cv_w_loaded"), sem("cv_pads"), sem("cv_whi_d"), sem("cv_wlo_d")
        x_loaded = [sem(f"cv_x_loaded{i}") for i in range(2)]
        xhi_done, xlo_done = sem("cv_xhi_done"), sem("cv_xlo_done")
        conv_done, raw_done = sem("cv_conv_done"), sem("cv_raw_done")
        stat = [sem(f"cv_stat{n}") for n in range(2)]
        mean_mm = [sem(f"cv_mean_mm{n}") for n in range(2)]
        coef = [sem(f"cv_coef{n}") for n in range(2)]
        gelu1, dw_acc, yhi_done, ylo_done = sem("cv_gelu1"), sem("cv_dw_acc"), sem("cv_yhi"), sem("cv_ylo")
        pw_done, gelu2 = sem("cv_pw_done"), sem("cv_gelu2")

        PRE1 = [4 + 1, 2 + 1]
        STAT_LINKS = [c + 1 + 1 + 2 + RSQRT_LINKS + 2 for c in PRE1]
        DW_LINKS = DW

        def steps(e, body):
            def peeled(it):
                body(it, it % 2, lambda k: 0 <= it - k < NB)
            for it in range(4):
                peeled(it)
            with e.Fori(2, NB // 2 - 1) as pair:
                body(pair * 2, 0, lambda k: True)
                body(pair * 2 + 1, 1, lambda k: True)
            for it in range(NB - 2, LAST):
                peeled(it)

        with nc.Block() as block:

            @block.sync
            def _(sp_):
                for dst, src in ((cw, conv_w), (pw, pw_wT), (dww, dw_w), (ch, chan)):
                    sp_.dma_start(dst[:, :], src).then_inc(w_loaded, 16)
                sp_.wait_ge(pads, 1)

                def body(it, par, on):
                    if not on(0):
                        return
                    if not (isinstance(it, int) and it < 2):
                        sp_.wait_ge(xlo_done, it - 1)
                    src = x[bass.ds(it, 1), :, :].rearrange("b c t -> (b c) t")
                    sp_.dma_start(x_in[par][0:C_IN, PAD:PAD + T_IN], src).then_inc(x_loaded[par], 16)
                    sp_.dma_start(x_in[par][C_IN:P, PAD - 1:PAD - 1 + T_IN], src).then_inc(x_loaded[par], 16)
                steps(sp_, body)

            @block.gpsimd
            def _(pool):
                for par in range(2):
                    pool.memset(x_in[par][:, 0:PAD], 0.0)
                    pool.memset(x_in[par][:, XW - PAD - 3:XW], 0.0)
                pool.memset(g[:, 0:DW_PAD], 0.0)
                pool.memset(g[:, GW - DW_PAD:GW], 0.0).then_inc(pads, 1)

                def body(it, par, on):
                    if on(0):
                        pool.wait_ge(xhi_done, it + 1)
                        if not (isinstance(it, int) and it < 2):
                            pool.wait_ge(conv_done, (it - 1) * NCH)
                        pool.tensor_tensor(x_lo[par][:, :], x_in[par][:, :], x_hi[par][:, :].bitcast(F32),
                                           ALU.subtract).then_inc(xlo_done, 1)
                    if on(1):
                        pool.wait_ge(yhi_done, it)
                        if not (isinstance(it, int) and it < 2):
                            pool.wait_ge(pw_done, it - 1)
                        pool.tensor_tensor(y_lo[:, :], y[:, :], y_hi[:, :].bitcast(F32),
                                           ALU.subtract).then_inc(ylo_done, 1)
                steps(pool, body)

            @block.scalar
            def _(act):
                act.wait_ge(w_loaded, 64)
                act.copy(cw_hi[:, :], cw[:, :])
                act.copy(pw_hi[:, :], pw[:, :]).then_inc(w_hi_done, 1)

                def split_in(i, par):
                    act.wait_ge(x_loaded[par], (i // 2 + 1) * 32)
                    if not (isinstance(i, int) and i < 2):
                        act.wait_ge(conv_done, (i - 1) * NCH)
                    act.copy(x_hi[par][:, :], x_in[par][:, :]).then_inc(xhi_done, 1)

                def body(it, par, on):
                    if on(0) and isinstance(it, int) and it == 0:
                        act.wait_ge(pads, 1)
                        split_in(0, 0)
                    if on(-1):
                        split_in(it + 1, 1 - par)
                    if on(1):
                        act.wait_ge(coef[0], it)
                        if not (isinstance(it, int) and it < 2):
                            act.wait_ge(dw_acc, (it - 1) * DW_LINKS)
                        act.activation(g[:, DW_PAD:DW_PAD + T_IN], raw[1 - par][:, :], ACT.Gelu,
                                       bias=shift[0][:, :], scale=scale[0][:, :]).then_inc(gelu1, 1)
                    if on(0):
                        for c in range(NCH):
                            act.wait_ge(conv_done, it * NCH + c + 1)
                            act.copy(raw[par][:, c * BANK:(c + 1) * BANK], cp[:, c, :]).then_inc(raw_done, 1)
                    if on(3):
                        act.wait_ge(coef[1], it - 2)
                        act.activation(row(h, it - 3), pp[:, :, :], ACT.Gelu,
                                       bias=shift[1][:, :], scale=scale[1][:, :]).then_inc(gelu2, 1)
                    if on(1):
                        act.wait_ge(dw_acc, it * DW_LINKS)
                        if not (isinstance(it, int) and it < 2):
                            act.wait_ge(pw_done, it - 1)
                        act.copy(y_hi[:, :], y[:, :]).then_inc(yhi_done, 1)
                steps(act, body)

            @block.vector
            def _(dve):
                dve.wait_ge(w_hi_done, 1)
                dve.tensor_tensor(cw_lo[:, :], cw[:, :], cw_hi[:, :].bitcast(F32), ALU.subtract)
                dve.tensor_tensor(pw_lo[:, :], pw[:, :], pw_hi[:, :].bitcast(F32), ALU.subtract).then_inc(w_lo_done, 1)

                def head(n, i, chunks):
                    link = Links(dve, stat[n], i * STAT_LINKS[n])
                    for c, src in enumerate(chunks):
                        if n == 0:
                            dve.wait_ge(raw_done, i * NCH + c + 1)
                        link(dve.bn_stats(st[n][:, c, :], src))
                    dve.memset(dummy[:, :], 0.0)
                    link(dve.bn_aggr(mv[n][:, :], st[n][:, 0:len(chunks), :]))

                def middle(n, i):
                    link = Links(dve, stat[n], i * STAT_LINKS[n] + PRE1[n])
                    dve.wait_ge(mean_mm[n], 2 * i + 1)
                    link(dve.tensor_copy(mean[n][:, :], sp[n][:, 0:1]))
                    link(dve.tensor_tensor(dev[n][:, :], mv[n][:, 0:1], mean[n][:, :], ALU.subtract))
                    link(dve.scalar_tensor_tensor(out=dev[n][:, :], in0=dev[n][:, :], scalar=dev[n][:, :],
                                                  in1=mv[n][:, 1:2], op0=ALU.mult, op1=ALU.add))

                def tail(n, i):
                    link = Links(dve, stat[n], i * STAT_LINKS[n] + PRE1[n] + 3)
                    dve.wait_ge(mean_mm[n], 2 * i + 2)
                    link(dve.tensor_scalar(var[n][:, :], sp[n][:, 0:1], EPS, None, ALU.add))
                    rsqrt(dve, rstd[n][:, :], var[n][:, :], tmp[n][:, :], link)
                    link(dve.tensor_tensor(scale[n][:, :], ch[:, 1 + 2 * n:2 + 2 * n], rstd[n][:, :], ALU.mult))
                    link(dve.tensor_tensor(tmp[n][:, :], mean[n][:, :], scale[n][:, :], ALU.mult))
                    assert link.n + PRE1[n] + 3 == STAT_LINKS[n]
                    dve.tensor_tensor(shift[n][:, :], ch[:, 2 + 2 * n:3 + 2 * n], tmp[n][:, :],
                                      ALU.subtract).then_inc(coef[n], 1)

                gv = g[:, :].rearrange("p (t s) -> p t s", s=2)

                def body(it, par, on):
                    if on(3):
                        middle(1, it - 3)
                    if on(1):
                        middle(0, it - 1)
                    if on(3):
                        tail(1, it - 3)
                    if on(1):
                        tail(0, it - 1)
                        link = Links(dve, dw_acc, (it - 1) * DW_LINKS)
                        dve.wait_ge(gelu1, it)
                        if not (isinstance(it, int) and it < 2):
                            dve.wait_ge(ylo_done, it - 1)
                        link(dve.tensor_scalar(y[:, :], gv[:, 0:T2, 0], dww[:, 0:1], ch[:, 0:1], ALU.mult, ALU.add))
                        for k in range(1, DW):
                            link(dve.scalar_tensor_tensor(out=y[:, :], in0=gv[:, k // 2:k // 2 + T2, k % 2],
                                                          scalar=dww[:, k:k + 1], in1=y[:, :],
                                                          op0=ALU.mult, op1=ALU.add))
                    if on(2):
                        dve.wait_ge(pw_done, it - 1)
                        head(1, it - 2, [pp[:, c, :] for c in range(2)])
                    if on(0):
                        head(0, it, [raw[par][:, c * BANK:(c + 1) * BANK] for c in range(NCH)])
                steps(dve, body)

            @block.tensor
            def _(pe):
                pe.wait_ge(w_lo_done, 1)

                def conv(i, par, c):
                    if not (isinstance(i, int) and i < 1):
                        pe.wait_ge(raw_done, (i - 1) * NCH + c + 1)
                    if c == 0:
                        pe.wait_ge(xhi_done, i + 1)
                    for q in range(PAIRS):
                        w = slice(q * P, (q + 1) * P)
                        cols = slice(c * BANK + 2 * q, (c + 1) * BANK + 2 * q)
                        pe.matmul(cp[:, c, :], cw_hi[:, w], x_hi[par][:, cols], start=(q == 0), stop=False)
                        pe.matmul(cp[:, c, :], cw_lo[:, w], x_hi[par][:, cols], start=False, stop=False)
                    if c == 0:
                        pe.wait_ge(xlo_done, i + 1)
                    for q in range(PAIRS):
                        w = slice(q * P, (q + 1) * P)
                        cols = slice(c * BANK + 2 * q, (c + 1) * BANK + 2 * q)
                        last = pe.matmul(cp[:, c, :], cw_hi[:, w], x_lo[par][:, cols], start=False, stop=(q == PAIRS - 1))
                    last.then_inc(conv_done, 1)

                def average(n, i, which):
                    done = PRE1[n] if which == 0 else PRE1[n] + 3
                    pe.wait_ge(stat[n], i * STAT_LINKS[n] + done)
                    src = mv[n][:, 0:1] if which == 0 else dev[n][:, :]
                    pe.matmul(sp[n][:, 0:1], ones_mean[:, :], src, start=True, stop=True).then_inc(mean_mm[n], 1)

                def pointwise(i):
                    pe.wait_ge(ylo_done, i + 1)
                    if not (isinstance(i, int) and i < 1):
                        pe.wait_ge(gelu2, i)
                    for c in range(2):
                        cols = slice(c * BANK, (c + 1) * BANK)
                        pe.matmul(pp[:, c, :], pw_hi[:, :], y_hi[:, cols], start=True, stop=False)
                        pe.matmul(pp[:, c, :], pw_hi[:, :], y_lo[:, cols], start=False, stop=False)
                        last = pe.matmul(pp[:, c, :], pw_lo[:, :], y_hi[:, cols], start=False, stop=True)
                    last.then_inc(pw_done, 1)

                def body(it, par, on):
                    if on(0):
                        conv(it, par, 0)
                    if on(3):
                        average(1, it - 3, 0)
                    if on(1):
                        average(0, it - 1, 0)
                    if on(0):
                        conv(it, par, 1)
                    if on(3):
                        average(1, it - 3, 1)
                    if on(1):
                        average(0, it - 1, 1)
                    if on(0):
                        conv(it, par, 2)
                    if on(0):
                        conv(it, par, 3)
                    if on(2):
                        pointwise(it - 2)
                steps(pe, body)


HEADS = 4
KV = 8
D = 128
QUARTERS = 4
QB = NB // QUARTERS
QT = QB * P
TILES = 2 + HEADS
SCALE = float(D) ** -0.5
STAGED_FIRST = 1 + TILES
STAGED_STEP = TILES + HEADS


def attention_stage(nc, h, ident, w_qkv, w_o, rope):
    with ExitStack() as ctx:
        def sb(name, shape, dt=F32):
            return ctx.enter_context(nc.sbuf_tensor(name, shape, dt))

        def sem(name):
            return ctx.enter_context(nc.semaphore(name))

        def psum(name):
            return ctx.enter_context(nc.psum_tensor(name, [P, BANK], F32))

        x_hi = sb("at_xhi", [P, KT, QT], F32R)
        x_lo = sb("at_xlo", [P, KT, QT], F32R)
        stage = [sb(f"at_stage{i}", [P, L]) for i in range(2)]
        w_hi = [sb(f"at_whi{i}", [P, L], F32R) for i in range(2)]
        w_lo = [sb(f"at_wlo{i}", [P, L], F32R) for i in range(2)]
        wo_hi = sb("at_wohi", [P, HEADS, L], F32R)
        wo_lo = sb("at_wolo", [P, HEADS, L], F32R)
        qT = [sb(f"at_q{i}", [P, HEADS, QT]) for i in range(2)]
        kT = [sb(f"at_k{i}", [P, QT]) for i in range(2)]
        vT = sb("at_vT", [P, QT])
        v = [sb(f"at_v{i}", [P, QB, D]) for i in range(2)]
        probs = sb("at_probs", [P, HEADS, P])
        pT = sb("at_pT", [P, HEADS * P])
        o_hi = sb("at_ohi", [P, HEADS * P], F32R)
        o_lo = sb("at_olo", [P, HEADS * P], F32R)
        cs = sb("at_cs", [P, 2, P])
        turned = sb("at_turned", [P, QT])
        kept = sb("at_kept", [P, QT])
        xn = [sb(f"at_xn{i}", [P, L]) for i in range(2)]
        st = sb("at_st", [P, QB, 2, 6])
        mv = sb("at_mv", [P, QB, 2])
        var, rstd, tmp, shift = (sb(f"at_{n}", [P, QB]) for n in ("var", "rstd", "tmp", "shift"))
        dummy = sb("at_dummy", [P, 1])
        top = sb("at_top", [P, HEADS])
        ntop = sb("at_ntop", [P, HEADS])
        total = sb("at_total", [P, HEADS])
        rtotal = sb("at_rtotal", [P, HEADS])
        proj = [psum(f"at_proj{i}") for i in range(2)]
        sc = [psum(f"at_sc{i}") for i in range(2)]
        tp = psum("at_tp")
        ov = psum("at_ov")
        out = ctx.enter_context(nc.psum_tensor("at_out", [P, 2, BANK], F32))

        rope_in = sem("at_rope_in")
        staged = [sem(f"at_staged{i}") for i in range(2)]
        hi_done, lo_done = sem("at_hi_done"), sem("at_lo_done")
        norm = sem("at_norm")
        normed, turned_in = sem("at_normed"), sem("at_turned_in")
        xhi_done, xlo_done = sem("at_xhi_done"), sem("at_xlo_done")
        proj_done, roped, vT_done = sem("at_proj_done"), sem("at_roped"), sem("at_vT_done")
        rope_mul = sem("at_rope_mul")
        v_turned, v_done = sem("at_v_turned"), sem("at_v_done")
        sc_done, top_done, ntop_done = sem("at_sc_done"), sem("at_top_done"), sem("at_ntop_done")
        exp_done, rtotal_done, probs_done = sem("at_exp_done"), sem("at_rtotal_done"), sem("at_probs_done")
        pT_mm, pT_done, ov_mm = sem("at_pT_mm"), sem("at_pT_done"), sem("at_ov_mm")
        ohi_done, olo_done = sem("at_ohi_done"), sem("at_olo_done")
        out_mm, added = sem("at_out_mm"), sem("at_added")

        prime(nc, [hi_done, lo_done, norm, normed, turned_in, xhi_done, xlo_done, proj_done, roped, vT_done,
                   rope_mul, v_turned, v_done, sc_done, top_done, ntop_done, exp_done, rtotal_done,
                   probs_done, pT_mm, pT_done, ov_mm, ohi_done, olo_done, out_mm, added])

        NORM_LINKS = 3 * QB + 1 + RSQRT_LINKS + 1

        STEPS_STAGED = STAGED_FIRST + (KV - 1) * STAGED_STEP - 1 + HEADS

        def steps(e, prologue, step):
            with e.Fori(0, QUARTERS) as qt:
                prologue(qt)
                step(qt, -1, 1, False, 2)
                with e.Fori(0, KV // 2 - 1) as pair:
                    step(qt, pair * 2, 0, True, 2)
                    step(qt, pair * 2 + 1, 1, True, 2)
                step(qt, KV - 2, 0, True, 1)
                step(qt, KV - 1, 1, True, 0)

        def tile_at(qt, g, j):
            return qt * (KV * TILES) + g * TILES + j

        def batch_at(qt, g, b):
            return qt * (KV * QB) + g * QB + b

        def staged_at(qt, g, i):
            if isinstance(g, int) and g == -1:
                return qt * STEPS_STAGED + 1 + i
            last = isinstance(g, int) and g == KV - 1
            return qt * STEPS_STAGED + STAGED_FIRST + g * STAGED_STEP + i - (1 if last else 0)

        def parity_at(g, i):
            return i % 2 if isinstance(g, int) and g == KV - 1 else (1 + i) % 2

        assert STAGED_FIRST % 2 == 1 and STAGED_STEP % 2 == 0 and STEPS_STAGED % 2 == 0

        def step_tiles(att, nxt):
            order = []
            if nxt:
                order.append(("w", 1))
            if att:
                order += [("o", 0), ("o", 1)]
            if nxt:
                order.append(("w", 2))
            if att:
                order += [("o", 2), ("o", 3)]
            if nxt:
                order += [("w", 3), ("w", 4), ("w", 5)]
            if nxt > 1:
                order.append(("k",))
            return order

        assert len(step_tiles(True, 2)) == STAGED_STEP and len(step_tiles(False, 2)) == STAGED_FIRST - 1

        with nc.Block() as block:

            @block.sync
            def _(sp):
                sp.dma_start(cs[:, :, :], rope).then_inc(rope_in, 16)

                def load(n, parity, src):
                    after(sp, lo_done, n - 1)
                    sp.dma_start(stage[parity][:, :], src).then_inc(staged[parity], 16)

                def w_src(g, j):
                    return w_qkv[bass.ds(g, 1), j, :, :].rearrange("a p n -> (a p) n")

                def prologue(qt):
                    after(sp, lo_done, qt * STEPS_STAGED)
                    sp.dma_start(stage[0][:, :], w_src(0, 0)).then_inc(staged[0], 16)

                def step(qt, g, par, att, nxt):
                    for i, what in enumerate(step_tiles(att, nxt)):
                        if what[0] == "w":
                            src = w_src(g + 1, what[1])
                        elif what[0] == "k":
                            src = w_src(g + 2, 0)
                        else:
                            src = w_o[bass.ds(g, 1), what[1], :, :].rearrange("a p n -> (a p) n")
                        load(staged_at(qt, g, i), parity_at(g, i), src)
                steps(sp, prologue, step)

            @block.scalar
            def _(act):

                def split(qt, g, i, what):
                    parity = parity_at(g, i)
                    act.wait_ge(staged[parity], half_count(qt, g, i) * 16)
                    if what[0] == "o":
                        if what[1] == 0:
                            after(act, out_mm, batch_at(qt, g, 0))
                        dst = wo_hi[:, what[1], :]
                    else:
                        j = what[1] if what[0] == "w" else 0
                        ahead = 1 if what[0] == "w" else 2
                        after(act, proj_done, tile_at(qt, g + ahead, j) - 1)
                        dst = w_hi[j % 2][:, :]
                    act.copy(dst, stage[parity][:, :]).then_inc(hi_done, 1)

                def half_count(qt, g, i):
                    if isinstance(g, int) and g == -1:
                        inside = (1 + i) // 2
                    else:
                        inside = g * (STAGED_STEP // 2) + (STAGED_FIRST + i - (1 if isinstance(g, int) and g == KV - 1 else 0)) // 2
                    return qt * (STEPS_STAGED // 2) + inside + 1

                def prologue(qt):
                    for b in range(QB):
                        after(act, norm, (qt + 1) * NORM_LINKS)
                        if b >= 2:
                            after(act, turned_in, qt * QB + b - 1)
                        act.activation(xn[b % 2][:, :], row(h, qt * QB + b), ACT.Identity,
                                       bias=shift[:, b:b + 1], scale=rstd[:, b:b + 1]).then_inc(normed, 1)
                        if b == 0:
                            act.wait_ge(staged[0], qt * (STEPS_STAGED // 2 * 16) + 16)
                            act.copy(w_hi[0][:, :], stage[0][:, :]).then_inc(hi_done, 1)
                        if b >= 1:
                            out_of(qt, b - 1)
                    out_of(qt, QB - 1)

                def out_of(qt, b):
                    after(act, turned_in, qt * QB + b + 1)
                    act.copy(x_hi[:, :, b * P:(b + 1) * P],
                             out[:, :, :].rearrange("p a (k t) -> p (a k) t", t=P)).then_inc(xhi_done, 1)

                def soft(qt, g, b):
                    n = batch_at(qt, g, b)
                    after(act, ntop_done, n + 1)
                    after(act, pT_mm, n)
                    for r in range(HEADS):
                        last = act.activation(probs[:, r, :], sc[b % 2][:, r * P:(r + 1) * P], ACT.Exp,
                                              bias=ntop[:, r:r + 1], scale=SCALE, accum_out=total[:, r:r + 1])
                    last.then_inc(exp_done, 1)

                def pT_out(qt, g, b):
                    n = batch_at(qt, g, b)
                    after(act, pT_mm, n + 1)
                    after(act, ov_mm, n)
                    act.copy(pT[:, :], tp[:, :]).then_inc(pT_done, 1)

                def o_split(qt, g, b):
                    n = batch_at(qt, g, b)
                    after(act, ov_mm, n + 1)
                    after(act, out_mm, n)
                    act.copy(o_hi[:, :], ov[:, :]).then_inc(ohi_done, 1)

                def v_out(qt, g):
                    after(act, proj_done, tile_at(qt, g, 1) + 1)
                    act.copy(vT[:, :], proj[1][:, :]).then_inc(vT_done, 1)

                def v_rows(qt, g, par):
                    after(act, v_turned, qt * KV + g + 1)
                    act.copy(v[par][:, :, :], tp[:, :].rearrange("p (b d) -> p b d", d=D)).then_inc(v_done, 1)

                def step(qt, g, par, att, nxt):
                    order = step_tiles(att, nxt)

                    def splits(*which):
                        for i, what in enumerate(order):
                            if what in which:
                                split(qt, g, i, what)
                    if att:
                        v_rows(qt, g, par)
                        soft(qt, g, 0)
                    splits(("w", 1), ("o", 0), ("o", 1))
                    if att:
                        pT_out(qt, g, 0)
                        soft(qt, g, 1)
                    splits(("w", 2))
                    if nxt:
                        v_out(qt, g + 1)
                    if att:
                        pT_out(qt, g, 1)
                        o_split(qt, g, 0)
                        soft(qt, g, 2)
                    splits(("o", 2), ("o", 3), ("w", 3))
                    if att:
                        pT_out(qt, g, 2)
                        o_split(qt, g, 1)
                        soft(qt, g, 3)
                    splits(("w", 4))
                    if att:
                        pT_out(qt, g, 3)
                        o_split(qt, g, 2)
                    splits(("w", 5))
                    if att:
                        o_split(qt, g, 3)
                    splits(("k",))
                steps(act, prologue, step)

            @block.vector
            def _(dve):
                def norm_rows(qt):
                    link = Links(dve, norm, qt * NORM_LINKS + 1)
                    for b in range(QB):
                        for c in range(2):
                            link(dve.bn_stats(st[:, b, c, :], row(h, qt * QB + b)[:, c * BANK:(c + 1) * BANK]))
                    for b in range(QB):
                        dve.memset(dummy[:, :], 0.0)
                        link(dve.bn_aggr(mv[:, b, :], st[:, b, :, :]))
                    link(dve.tensor_scalar(var[:, :], mv[:, :, 1], EPS, None, ALU.add))
                    rsqrt(dve, rstd[:, :], var[:, :], tmp[:, :], link)
                    link(dve.scalar_tensor_tensor(out=shift[:, :], in0=mv[:, :, 0], scalar=-1.0, in1=rstd[:, :],
                                                  op0=ALU.mult, op1=ALU.mult))
                    assert link.n == NORM_LINKS

                def prologue(qt):
                    after(dve, added, qt * (KV * QB))
                    norm_rows(qt)
                    for b in range(QB):
                        after(dve, xhi_done, qt * QB + b + 1)
                        cols = slice(b * P, (b + 1) * P)
                        dve.tensor_tensor(x_lo[:, :, cols], out[:, :, :].rearrange("p a (k t) -> p (a k) t", t=P),
                                          x_hi[:, :, cols].bitcast(F32), ALU.subtract).then_inc(xlo_done, 1)
                        if b == 0:
                            after(dve, hi_done, qt * STEPS_STAGED + 1)
                            dve.tensor_tensor(w_lo[0][:, :], stage[0][:, :], w_hi[0][:, :].bitcast(F32),
                                              ALU.subtract).then_inc(lo_done, 1)

                def split(qt, g, i, what):
                    n = staged_at(qt, g, i)
                    after(dve, hi_done, n + 1)
                    if what[0] == "o":
                        hi, lo = wo_hi[:, what[1], :], wo_lo[:, what[1], :]
                    else:
                        j = what[1] if what[0] == "w" else 0
                        hi, lo = w_hi[j % 2][:, :], w_lo[j % 2][:, :]
                    dve.tensor_tensor(lo, stage[parity_at(g, i)][:, :], hi.bitcast(F32), ALU.subtract).then_inc(lo_done, 1)

                def rope_out(qt, g, par, j):
                    n = qt * (KV * (TILES - 1)) + g * (TILES - 1) + (j if j == 0 else j - 1)
                    src = proj[j % 2]
                    dst = kT[par][:, :] if j == 0 else qT[par][:, j - 2, :]
                    HD = D // 2

                    def cols(ap):
                        return ap.rearrange("p (b t) -> p b t", t=P)

                    def table(which, rows):
                        return cs[rows, which:which + 1, :].to_broadcast([HD if rows != slice(0, P) else P, QB, P])
                    after(dve, proj_done, tile_at(qt, g, j) + 1)
                    after(dve, roped, n)
                    dve.tensor_tensor(cols(kept[:, :]), cols(src[:, :]), table(0, slice(0, P)), ALU.mult)\
                       .then_inc(rope_mul, 1)
                    low, high = slice(0, HD), slice(HD, P)
                    dve.tensor_tensor(cols(turned[low, :]), cols(src[high, :]), table(1, high), ALU.mult)\
                       .then_inc(rope_mul, 1)
                    dve.tensor_tensor(cols(turned[high, :]), cols(src[low, :]), table(1, low), ALU.mult)\
                       .then_inc(rope_mul, 1)
                    after(dve, rope_mul, n * 3 + 3)
                    dve.tensor_tensor(dst, kept[:, :], turned[:, :], ALU.add).then_inc(roped, 1)

                def top_of(qt, g, b):
                    n = batch_at(qt, g, b)
                    after(dve, sc_done, n + 1)
                    dve.tensor_reduce(top[:, :], sc[b % 2][:, :].rearrange("p (r k) -> p r k", k=P),
                                      AX.X, ALU.max).then_inc(top_done, 1)
                    after(dve, top_done, n + 1)
                    dve.tensor_scalar(ntop[:, :], top[:, :], -SCALE, None, ALU.mult).then_inc(ntop_done, 1)

                def normalize(qt, g, b):
                    n = batch_at(qt, g, b)
                    after(dve, exp_done, n + 1)
                    dve.reciprocal(rtotal[:, :], total[:, :]).then_inc(rtotal_done, 1)
                    after(dve, rtotal_done, n + 1)
                    dve.tensor_tensor(probs[:, :, :], probs[:, :, :],
                                      rtotal[:, :].rearrange("p (r a) -> p r a", a=1).to_broadcast([P, HEADS, P]),
                                      ALU.mult).then_inc(probs_done, 1)

                def o_split(qt, g, b):
                    n = batch_at(qt, g, b)
                    after(dve, ohi_done, n + 1)
                    dve.tensor_tensor(o_lo[:, :], ov[:, :], o_hi[:, :].bitcast(F32), ALU.subtract).then_inc(olo_done, 1)

                def add(qt, g, b):
                    n = batch_at(qt, g, b)
                    after(dve, out_mm, n + 1)
                    hb = row(h, qt * QB + b)
                    dve.tensor_tensor(hb, hb, out[:, :, :].rearrange("p a n -> p (a n)"), ALU.add).then_inc(added, 1)

                def step(qt, g, par, att, nxt):
                    order = step_tiles(att, nxt)

                    def splits(*which):
                        for i, what in enumerate(order):
                            if what in which:
                                split(qt, g, i, what)
                    if att:
                        top_of(qt, g, 0)
                    splits(("w", 1))
                    if att:
                        normalize(qt, g, 0)
                    splits(("o", 0), ("o", 1))
                    if nxt:
                        rope_out(qt, g + 1, 1 - par, 0)
                    if att:
                        top_of(qt, g, 1)
                        normalize(qt, g, 1)
                    splits(("w", 2))
                    if att:
                        top_of(qt, g, 2)
                        o_split(qt, g, 0)
                        normalize(qt, g, 2)
                    splits(("o", 2), ("o", 3), ("w", 3))
                    if nxt:
                        rope_out(qt, g + 1, 1 - par, 2)
                    if att:
                        top_of(qt, g, 3)
                        o_split(qt, g, 1)
                        add(qt, g, 0)
                        normalize(qt, g, 3)
                    splits(("w", 4))
                    if nxt:
                        rope_out(qt, g + 1, 1 - par, 3)
                    if att:
                        o_split(qt, g, 2)
                        add(qt, g, 1)
                    splits(("w", 5))
                    if nxt:
                        rope_out(qt, g + 1, 1 - par, 4)
                    if att:
                        o_split(qt, g, 3)
                        add(qt, g, 2)
                    splits(("k",))
                    if nxt:
                        rope_out(qt, g + 1, 1 - par, 5)
                    if att:
                        add(qt, g, 3)
                dve.wait_ge(rope_in, 16)
                steps(dve, prologue, step)

            @block.tensor
            def _(pe):
                def prologue(qt):
                    for b in range(QB):
                        after(pe, normed, qt * QB + b + 1)
                        after(pe, xlo_done, qt * QB + b)
                        for k in range(KT):
                            last = pe.transpose(out[:, k // 4, (k % 4) * P:(k % 4 + 1) * P],
                                                xn[b % 2][:, k * P:(k + 1) * P], ident[:, :])
                        last.then_inc(turned_in, 1)

                def project(qt, g, j):
                    n = tile_at(qt, g, j)
                    hi, lo = w_hi[j % 2], w_lo[j % 2]
                    after(pe, lo_done, project_staged(qt, g, j) + 1)
                    if j == 0:
                        after(pe, xlo_done, (qt + 1) * QB)
                    if j == 3:
                        after(pe, vT_done, qt * KV + g + 1)
                    else:
                        out_before = {0: -2, 1: -1, 2: 1, 4: 2, 5: 3}[j]
                        after(pe, roped, qt * (KV * (TILES - 1)) + g * (TILES - 1) + out_before + (0 if j > 1 else 1))
                    for k in range(KT):
                        w = slice(k * P, (k + 1) * P)
                        pe.matmul(proj[j % 2][:, :], hi[:, w], x_hi[:, k, :], start=(k == 0), stop=False)
                        pe.matmul(proj[j % 2][:, :], hi[:, w], x_lo[:, k, :], start=False, stop=False)
                        last = pe.matmul(proj[j % 2][:, :], lo[:, w], x_hi[:, k, :], start=False, stop=(k == KT - 1))
                    last.then_inc(proj_done, 1)

                def project_staged(qt, g, j):
                    if isinstance(g, int) and g == 0:
                        return qt * STEPS_STAGED if j == 0 else \
                            staged_at(qt, -1, step_tiles(False, 2).index(("w", j)))
                    if j == 0:
                        if isinstance(g, int) and g == 1:
                            return staged_at(qt, -1, step_tiles(False, 2).index(("k",)))
                        return staged_at(qt, g - 2, step_tiles(True, 2).index(("k",)))
                    return staged_at(qt, g - 1, step_tiles(True, 2).index(("w", j)))

                def scores(qt, g, par, b):
                    n = batch_at(qt, g, b)
                    if b == 0:
                        after(pe, roped, qt * (KV * (TILES - 1)) + (g + 1) * (TILES - 1))
                    cols = slice(b * P, (b + 1) * P)
                    for r in range(HEADS):
                        last = pe.matmul(sc[b % 2][:, r * P:(r + 1) * P], qT[par][:, r, cols], kT[par][:, cols],
                                         start=True, stop=True)
                    last.then_inc(sc_done, 1)

                def turn_probs(qt, g, b):
                    n = batch_at(qt, g, b)
                    after(pe, probs_done, n + 1)
                    if b == 0:
                        after(pe, v_done, qt * KV + g + 1)
                    else:
                        after(pe, pT_done, n)
                    for r in range(HEADS):
                        last = pe.transpose(tp[:, r * P:(r + 1) * P], probs[:, r, :], ident[:, :])
                    last.then_inc(pT_mm, 1)

                def values(qt, g, par, b):
                    n = batch_at(qt, g, b)
                    after(pe, pT_done, n + 1)
                    after(pe, olo_done, n)
                    pe.matmul(ov[:, :], v[par][:, b, :], pT[:, :], start=True, stop=True).then_inc(ov_mm, 1)

                def outputs(qt, g, b):
                    n = batch_at(qt, g, b)
                    after(pe, olo_done, n + 1)
                    after(pe, added, n)
                    if b == 0:
                        after(pe, lo_done, staged_at(qt, g, wo_last(g)) + 1)
                    for r in range(HEADS):
                        rows = slice(r * P, (r + 1) * P)
                        for a, w, first, end in ((o_hi, wo_hi, r == 0, False), (o_hi, wo_lo, False, False),
                                                 (o_lo, wo_hi, False, r == HEADS - 1)):
                            for c in range(2):
                                last = pe.matmul(out[:, c, :], a[:, rows], w[:, r, c * BANK:(c + 1) * BANK],
                                                 start=first, stop=end)
                    last.then_inc(out_mm, 1)

                def wo_last(g):
                    nxt = 0 if isinstance(g, int) and g == KV - 1 else 2
                    return step_tiles(True, nxt).index(("o", 3))

                def turn_v(qt, g):
                    after(pe, vT_done, qt * KV + g + 1)
                    after(pe, pT_done, batch_at(qt, g, 0))
                    for b in range(QB):
                        last = pe.transpose(tp[:, b * D:(b + 1) * D], vT[:, b * P:(b + 1) * P], ident[:, :])
                    last.then_inc(v_turned, 1)

                def step(qt, g, par, att, nxt):
                    for j in range(TILES):
                        if att:
                            if 3 <= j:
                                outputs(qt, g, j - 3)
                            if 2 <= j:
                                values(qt, g, par, j - 2)
                            if j < QB:
                                scores(qt, g, par, j)
                            if 1 <= j <= QB:
                                turn_probs(qt, g, j - 1)
                        if nxt:
                            project(qt, g + 1, j)
                    if att:
                        outputs(qt, g, QB - 1)
                    if nxt:
                        turn_v(qt, g + 1)
                steps(pe, prologue, step)


class Rows:

    LINKS = 2 + 1 + 1 + 11 + 1

    def __init__(self, nc, ctx, name, h, ident):
        def sb(n, shape, dt=F32):
            return ctx.enter_context(nc.sbuf_tensor(f"{name}_{n}", shape, dt))

        def sem(n):
            return ctx.enter_context(nc.semaphore(f"{name}_{n}"))

        self.h, self.ident = h, ident
        self.xn = sb("xn", [P, L])
        self.x_hi = [sb(f"xhi{i}", [P, KT, P], F32R) for i in range(2)]
        self.x_lo = [sb(f"xlo{i}", [P, KT, P], F32R) for i in range(2)]
        self.st = sb("st", [P, 2, 6])
        self.mv = sb("mv", [P, 2])
        self.var, self.tmp, self.dummy = sb("var", [P, 1]), sb("tmp", [P, 1]), sb("dummy", [P, 1])
        self.rstd = [sb(f"rstd{i}", [P, 1]) for i in range(2)]
        self.shift = [sb(f"shift{i}", [P, 1]) for i in range(2)]
        self.tp = ctx.enter_context(nc.psum_tensor(f"{name}_tp", [P, 2, BANK], F32))
        self.norm = sem("norm")
        self.normed = sem("normed")
        self.turned = sem("turned")
        self.hi_done = sem("xhi_done")
        self.lo_done = sem("xlo_done")
        prime(nc, [self.norm, self.normed, self.turned, self.hi_done, self.lo_done])

    def stats(self, dve, t, par):
        after(dve, self.normed, t - 1)
        link = Links(dve, self.norm, t * self.LINKS + 1)
        hb = row(self.h, t)
        for c in range(2):
            link(dve.bn_stats(self.st[:, c, :], hb[:, c * BANK:(c + 1) * BANK]))
        dve.memset(self.dummy[:, :], 0.0)
        link(dve.bn_aggr(self.mv[:, :], self.st[:, :, :]))
        link(dve.tensor_scalar(self.var[:, :], self.mv[:, 1:2], EPS, None, ALU.add))
        rstd, tmp, var = self.rstd[par][:, :], self.tmp[:, :], self.var[:, :]
        link(dve.tensor_scalar(tmp.bitcast(I32), var.bitcast(I32), 1, None, ALU.logical_shift_right))
        link(dve.tensor_scalar(rstd.bitcast(I32), tmp.bitcast(I32), -1.0, float(RSQRT_SEED), ALU.mult, ALU.add))
        for _ in range(NEWTON):
            link(dve.scalar_tensor_tensor(out=tmp, in0=rstd, scalar=var, in1=rstd, op0=ALU.mult, op1=ALU.mult))
            link(dve.tensor_scalar(tmp, tmp, -0.5, 1.5, ALU.mult, ALU.add))
            link(dve.tensor_tensor(rstd, rstd, tmp, ALU.mult))
        link(dve.scalar_tensor_tensor(out=self.shift[par][:, :], in0=self.mv[:, 0:1], scalar=-1.0, in1=rstd,
                                      op0=ALU.mult, op1=ALU.mult))
        assert link.n == self.LINKS

    def normalize(self, act, t, par):
        after(act, self.norm, (t + 1) * self.LINKS)
        after(act, self.turned, t)
        act.activation(self.xn[:, :], row(self.h, t), ACT.Identity,
                       bias=self.shift[par][:, :], scale=self.rstd[par][:, :]).then_inc(self.normed, 1)

    def turn(self, pe, t, par):
        after(pe, self.normed, t + 1)
        after(pe, self.lo_done, t)
        for k in range(KT):
            last = pe.transpose(self.tp[:, k // 4, (k % 4) * P:(k % 4 + 1) * P],
                                self.xn[:, k * P:(k + 1) * P], self.ident[:, :])
        last.then_inc(self.turned, 1)

    def high(self, act, t, par, used, count):
        after(act, self.turned, t + 1)
        after(act, used, count)
        act.copy(self.x_hi[par][:, :, :], self.tp[:, :, :].rearrange("p a (k t) -> p (a k) t", t=P))\
           .then_inc(self.hi_done, 1)

    def low(self, dve, t, par):
        after(dve, self.hi_done, t + 1)
        dve.tensor_tensor(self.x_lo[par][:, :, :], self.tp[:, :, :].rearrange("p a (k t) -> p (a k) t", t=P),
                          self.x_hi[par][:, :, :].bitcast(F32), ALU.subtract).then_inc(self.lo_done, 1)


def load_split(nc, ctx, name, parts, chunk):
    halves = [(ctx.enter_context(nc.sbuf_tensor(f"{name}_{n}_hi", [P, src.shape[1]], F32R)),
               ctx.enter_context(nc.sbuf_tensor(f"{name}_{n}_lo", [P, src.shape[1]], F32R))) for n, src in parts]
    steps = [(p, at, min(chunk, src.shape[1] - at)) for p, (_, src) in enumerate(parts)
             for at in range(0, src.shape[1], chunk)]
    with ExitStack() as inner:
        stage = [inner.enter_context(nc.sbuf_tensor(f"{name}_stage{i}", [P, chunk], F32)) for i in range(2)]
        landed = [inner.enter_context(nc.semaphore(f"{name}_landed{i}")) for i in range(2)]
        hi_done = inner.enter_context(nc.semaphore(f"{name}_hi_done"))
        lo_done = inner.enter_context(nc.semaphore(f"{name}_lo_done"))
        with nc.Block() as block:

            @block.sync
            def _(sp):
                for n, (p, at, size) in enumerate(steps):
                    if n >= 2:
                        sp.wait_ge(lo_done, n - 1)
                    sp.dma_start(stage[n % 2][:, 0:size], parts[p][1][:, at:at + size]).then_inc(landed[n % 2], 16)

            @block.scalar
            def _(act):
                for n, (p, at, size) in enumerate(steps):
                    act.wait_ge(landed[n % 2], 16 * (n // 2 + 1))
                    act.copy(halves[p][0][:, at:at + size], stage[n % 2][:, 0:size]).then_inc(hi_done, 1)

            @block.vector
            def _(dve):
                for n, (p, at, size) in enumerate(steps):
                    dve.wait_ge(hi_done, n + 1)
                    dve.tensor_tensor(halves[p][1][:, at:at + size], stage[n % 2][:, 0:size],
                                      halves[p][0][:, at:at + size].bitcast(F32), ALU.subtract).then_inc(lo_done, 1)
    return halves


def tile_steps(e, before, body, finish):
    before()
    body(0, 0, False)
    with e.Fori(0, NB // 2 - 1) as pair:
        body(pair * 2 + 1, 1, False)
        body(pair * 2 + 2, 0, False)
    body(NB - 1, 1, True)
    finish()


EXPERTS = 8
RANK = 16
ER = EXPERTS * RANK


def mixture_stage(nc, h, ident, a_route, bw, experts):
    NP_ = ER + EXPERTS
    with ExitStack() as ctx:
        def sb(name, shape, dt=F32):
            return ctx.enter_context(nc.sbuf_tensor(name, shape, dt))

        def sem(name):
            return ctx.enter_context(nc.semaphore(name))

        (ar_hi, ar_lo), (bw_hi, bw_lo) = load_split(nc, ctx, "mx_w", [("ar", a_route), ("bw", bw)], 1088)
        rows = Rows(nc, ctx, "mx", h, ident)
        logits = sb("mx_logits", [P, EXPERTS])
        best = sb("mx_best", [P, 8])
        at = sb("mx_at", [P, 8], mybir.dt.uint32)
        atf = sb("mx_atf", [P, 1])
        weight = sb("mx_weight", [P, EXPERTS])
        numbers = sb("mx_numbers", [P, EXPERTS])
        wh = sb("mx_wh", [P, ER])
        wt_hi = sb("mx_wthi", [P, P], F32R)
        wt_lo = sb("mx_wtlo", [P, P], F32R)
        pj = ctx.enter_context(nc.psum_tensor("mx_pj", [P, BANK], F32))
        wt = ctx.enter_context(nc.psum_tensor("mx_wt", [P, BANK], F32))
        out = ctx.enter_context(nc.psum_tensor("mx_out", [P, 2, BANK], F32))
        numbers_in, pj_done, route = sem("mx_numbers_in"), sem("mx_pj_done"), sem("mx_route")
        wh_done, wt_mm, wthi_done, wtlo_done = sem("mx_wh_done"), sem("mx_wt_mm"), sem("mx_wthi"), sem("mx_wtlo")
        out_mm, added = sem("mx_out_mm"), sem("mx_added")
        prime(nc, [pj_done, route, wh_done, wt_mm, wthi_done, wtlo_done, out_mm, added])
        ROUTE_LINKS = 5

        with nc.Block() as block:

            @block.sync
            def _(sp):
                sp.dma_start(numbers[:, :], experts).then_inc(numbers_in, 16)

            @block.scalar
            def _(act):
                def before():
                    rows.normalize(act, 0, 0)
                    rows.high(act, 0, 0, pj_done, 0)

                def split(t):
                    after(act, wt_mm, t + 1)
                    after(act, out_mm, t)
                    act.copy(wt_hi[:, :], wt[:, 0:P]).then_inc(wthi_done, 1)

                def body(t, par, last):
                    if not last:
                        rows.normalize(act, t + 1, 1 - par)
                        rows.high(act, t + 1, 1 - par, pj_done, t)
                    split(t)
                tile_steps(act, before, body, lambda: None)

            @block.vector
            def _(dve):
                def before():
                    rows.stats(dve, 0, 0)
                    rows.low(dve, 0, 0)

                def route_of(t):
                    after(dve, pj_done, t + 1)
                    link = Links(dve, route, t * ROUTE_LINKS + 1)
                    link(dve.tensor_copy(logits[:, :], pj[:, ER:NP_]))
                    dve.memset(rows.dummy[:, :], 0.0)
                    link(dve.max(best[:, :], logits[:, :]))
                    dve.memset(rows.dummy[:, :], 0.0)
                    link(dve.max_index(at[:, :], best[:, :], logits[:, :]))
                    link(dve.tensor_copy(atf[:, :], at[:, 0:1]))
                    link(dve.tensor_scalar(weight[:, :], numbers[:, :], atf[:, :], best[:, 0:1],
                                           ALU.is_equal, ALU.mult))
                    assert link.n == ROUTE_LINKS
                    after(dve, wt_mm, t)
                    dve.tensor_tensor(wh[:, :].rearrange("p (e r) -> p e r", r=RANK),
                                      pj[:, 0:ER].rearrange("p (e r) -> p e r", r=RANK),
                                      weight[:, :].rearrange("p (e a) -> p e a", a=1).to_broadcast([P, EXPERTS, RANK]),
                                      ALU.mult).then_inc(wh_done, 1)

                def body(t, par, last):
                    if not last:
                        rows.stats(dve, t + 1, 1 - par)
                    route_of(t)
                    if not last:
                        rows.low(dve, t + 1, 1 - par)
                    after(dve, wthi_done, t + 1)
                    dve.tensor_tensor(wt_lo[:, :], wt[:, 0:P], wt_hi[:, :].bitcast(F32), ALU.subtract)\
                       .then_inc(wtlo_done, 1)
                    after(dve, out_mm, t + 1)
                    hb = row(h, t)
                    dve.tensor_tensor(hb, hb, out[:, :, :].rearrange("p a n -> p (a n)"), ALU.add).then_inc(added, 1)
                dve.wait_ge(numbers_in, 16)
                tile_steps(dve, before, body, lambda: None)

            @block.tensor
            def _(pe):
                def before():
                    rows.turn(pe, 0, 0)

                def body(t, par, last):
                    after(pe, rows.lo_done, t + 1)
                    after(pe, wh_done, t)
                    xh, xl = rows.x_hi[par], rows.x_lo[par]
                    for k in range(KT):
                        w = slice(k * NP_, (k + 1) * NP_)
                        pe.matmul(pj[:, 0:NP_], xh[:, k, :], ar_hi[:, w], start=(k == 0), stop=False)
                        pe.matmul(pj[:, 0:NP_], xh[:, k, :], ar_lo[:, w], start=False, stop=False)
                        mm = pe.matmul(pj[:, 0:NP_], xl[:, k, :], ar_hi[:, w], start=False, stop=(k == KT - 1))
                    mm.then_inc(pj_done, 1)
                    if not last:
                        rows.turn(pe, t + 1, 1 - par)
                    after(pe, wh_done, t + 1)
                    after(pe, wtlo_done, t)
                    pe.transpose(wt[:, 0:P], wh[:, :], ident[:, :]).then_inc(wt_mm, 1)
                    after(pe, wtlo_done, t + 1)
                    after(pe, added, t)
                    for c in range(2):
                        w = slice(c * BANK, (c + 1) * BANK)
                        pe.matmul(out[:, c, :], wt_hi[:, :], bw_hi[:, w], start=True, stop=False)
                        pe.matmul(out[:, c, :], wt_hi[:, :], bw_lo[:, w], start=False, stop=False)
                        mm = pe.matmul(out[:, c, :], wt_lo[:, :], bw_hi[:, w], start=False, stop=True)
                    mm.then_inc(out_mm, 1)
                tile_steps(pe, before, body, lambda: None)


TOP_K = 6
HALF = L // 2
NO_WEIGHT = 150.0


def screen(nc, h, ident, f_dram, c_dram, rstd, shift, flag):
    with ExitStack() as ctx:
        def sb(name, shape, dt=F32):
            return ctx.enter_context(nc.sbuf_tensor(name, shape, dt))

        def sem(name):
            return ctx.enter_context(nc.semaphore(name))

        f_hi = sb("sc_fhi", [P, KT, L], F32R)
        c_hi = sb("sc_chi", [P, KT // 2, HALF], F32R)
        with ExitStack() as inner:
            stage = [inner.enter_context(nc.sbuf_tensor(f"sc_stage{i}", [P, L], F32)) for i in range(2)]
            landed = [inner.enter_context(nc.semaphore(f"sc_landed{i}")) for i in range(2)]
            used = inner.enter_context(nc.semaphore("sc_used"))
            srcs = [(f_hi[:, k, :], f_dram[:, k * L:(k + 1) * L]) for k in range(KT)]
            srcs += [(c_hi[:, k:k + 2, :].rearrange("p k n -> p (k n)"), c_dram[:, k * HALF:(k + 2) * HALF])
                     for k in range(0, KT // 2, 2)]
            with nc.Block() as block:

                @block.sync
                def _(sp):
                    for n, (_, src) in enumerate(srcs):
                        if n >= 2:
                            sp.wait_ge(used, n - 1)
                        sp.dma_start(stage[n % 2][:, :], src).then_inc(landed[n % 2], 16)

                @block.scalar
                def _(act):
                    for n, (dst, _) in enumerate(srcs):
                        act.wait_ge(landed[n % 2], 16 * (n // 2 + 1))
                        act.copy(dst, stage[n % 2][:, :]).then_inc(used, 1)

        xn = [sb(f"sc_xn{i}", [P, L]) for i in range(2)]
        x_hi = [sb(f"sc_xhi{i}", [P, KT, QT], F32R) for i in range(2)]
        squares = [sb(f"sc_sq{i}", [P, 2, BANK]) for i in range(2)]
        power = [sb(f"sc_pw{i}", [P, KT // 2, QT], F32R) for i in range(2)]
        st = sb("sc_st", [P, QB, 2, 6])
        mv = sb("sc_mv", [P, NB, 2])
        var, tmp = sb("sc_var", [P, QB]), sb("sc_tmp", [P, QB])
        top = sb("sc_top", [P, NB])
        lead = sb("sc_lead", [P, NB])
        least = sb("sc_least", [P, 1])
        least_row = sb("sc_least_row", [1, 1])
        tp = ctx.enter_context(nc.psum_tensor("sc_tp", [P, 2, BANK], F32))
        ri = ctx.enter_context(nc.psum_tensor("sc_ri", [P, 2, 2, BANK], F32))
        co = ctx.enter_context(nc.psum_tensor("sc_co", [P, 2, BANK], F32))
        norm, normed, turned, hi_done = sem("sc_norm"), sem("sc_normed"), sem("sc_turned"), sem("sc_hi_done")
        spectrum, squared, powered = sem("sc_spectrum"), sem("sc_squared"), sem("sc_powered")
        corr_mm, topped, leads, least_t = sem("sc_corr_mm"), sem("sc_topped"), sem("sc_leads"), sem("sc_least_t")
        NORM_LINKS = 3 * QB + 1 + RSQRT_LINKS + 1
        FT = KT // 2

        with nc.Block() as block:

            @block.vector
            def _(dve):
                def stats(qt):
                    link = Links(dve, norm, qt * NORM_LINKS)
                    these = slice(qt * QB, (qt + 1) * QB)
                    for b in range(QB):
                        for c in range(2):
                            link(dve.bn_stats(st[:, b, c, :], h[:, qt * QB + b, c * BANK:(c + 1) * BANK]))
                    for b in range(QB):
                        link(dve.bn_aggr(mv[:, qt * QB + b, :], st[:, b, :, :]))
                    link(dve.tensor_scalar(var[:, :], mv[:, these, 1], EPS, None, ALU.add))
                    rsqrt(dve, rstd[:, these], var[:, :], tmp[:, :], link)
                    link(dve.scalar_tensor_tensor(out=shift[:, these], in0=mv[:, these, 0], scalar=-1.0,
                                                  in1=rstd[:, these], op0=ALU.mult, op1=ALU.mult))

                def add_power(qt, i):
                    n = qt * FT + i
                    dve.wait_ge(squared, n + 1)
                    if qt >= 2 and i == 0:
                        dve.wait_ge(corr_mm, (qt - 1) * QB)
                    sq = squares[n % 2]
                    dve.tensor_tensor(power[qt % 2][:, i, :], sq[:, 0, :], sq[:, 1, :], ALU.add).then_inc(powered, 1)

                def tops(qt):
                    for b in range(QB):
                        t = qt * QB + b
                        dve.wait_ge(corr_mm, t + 1)
                        dve.tensor_reduce(top[:, t:t + 1], co[:, t % 2, :], AX.X, ALU.max).then_inc(topped, 1)

                stats(0)
                for qt in range(QUARTERS):
                    if qt + 1 < QUARTERS:
                        stats(qt + 1)
                    add_power(qt, 0)
                    if qt:
                        tops(qt - 1)
                    for i in range(1, FT):
                        add_power(qt, i)
                tops(QUARTERS - 1)
                link = Links(dve, leads, 0)
                dve.wait_ge(topped, NB)
                link(dve.tensor_tensor(lead[:, :], mv[:, :, 1], rstd[:, :], ALU.mult))
                link(dve.tensor_tensor(lead[:, :], lead[:, :], rstd[:, :], ALU.mult))
                link(dve.scalar_tensor_tensor(out=lead[:, :], in0=lead[:, :], scalar=float(L), in1=top[:, :],
                                              op0=ALU.mult, op1=ALU.subtract))
                link(dve.tensor_reduce(least[:, :], lead[:, :], AX.X, ALU.min))
                dve.wait_ge(least_t, 1)
                link(dve.tensor_reduce(least_row[:, :], tp[0:1, 0, 0:P], AX.X, ALU.min))
                link(dve.tensor_scalar(flag[:, :], least_row[:, :], NO_WEIGHT, None, ALU.is_ge))

            @block.scalar
            def _(act):
                def rows(qt, b):
                    t = qt * QB + b
                    act.wait_ge(norm, (qt + 1) * NORM_LINKS)
                    if t >= 2:
                        act.wait_ge(turned, t - 1)
                    act.activation(xn[t % 2][:, :], h[:, t, :], ACT.Identity,
                                   bias=shift[:, t:t + 1], scale=rstd[:, t:t + 1]).then_inc(normed, 1)

                def high(qt, b):
                    t = qt * QB + b
                    act.wait_ge(turned, t + 1)
                    if qt >= 2 and b == 0:
                        act.wait_ge(spectrum, (qt - 1) * FT)
                    act.copy(x_hi[qt % 2][:, :, b * P:(b + 1) * P],
                             tp[:, :, :].rearrange("p a (k t) -> p (a k) t", t=P)).then_inc(hi_done, 1)

                def square(qt, i):
                    n = qt * FT + i
                    act.wait_ge(spectrum, n + 1)
                    if n >= 2:
                        act.wait_ge(powered, n - 1)
                    act.activation(squares[n % 2][:, :, :], ri[:, n % 2, :, :], ACT.Square).then_inc(squared, 1)

                for b in range(QB):
                    rows(0, b)
                    high(0, b)
                for qt in range(QUARTERS):
                    for i in range(FT):
                        if qt + 1 < QUARTERS:
                            rows(qt + 1, i)
                        square(qt, i)
                        if qt + 1 < QUARTERS:
                            high(qt + 1, i)

            @block.tensor
            def _(pe):
                def turn(qt, b):
                    t = qt * QB + b
                    pe.wait_ge(normed, t + 1)
                    if t:
                        pe.wait_ge(hi_done, t)
                    for k in range(KT):
                        last = pe.transpose(tp[:, k // 4, (k % 4) * P:(k % 4 + 1) * P],
                                            xn[t % 2][:, k * P:(k + 1) * P], ident[:, :])
                    last.then_inc(turned, 1)

                def dft(qt, i):
                    n = qt * FT + i
                    if i == 0:
                        pe.wait_ge(hi_done, (qt + 1) * QB)
                    if n >= 2:
                        pe.wait_ge(squared, n - 1)
                    for part in range(2):
                        at = part * HALF + i * P
                        for k in range(KT):
                            last = pe.matmul(ri[:, n % 2, part, :], f_hi[:, k, at:at + P], x_hi[qt % 2][:, k, :],
                                             start=(k == 0), stop=(k == KT - 1))
                    last.then_inc(spectrum, 1)

                def correlate(qt):
                    pe.wait_ge(powered, (qt + 1) * FT)
                    for b in range(QB):
                        t = qt * QB + b
                        if t >= 2:
                            pe.wait_ge(topped, t - 1)
                        for k in range(FT):
                            last = pe.matmul(co[:, t % 2, :], power[qt % 2][:, k, b * P:(b + 1) * P], c_hi[:, k, :],
                                             start=(k == 0), stop=(k == FT - 1))
                        last.then_inc(corr_mm, 1)

                for b in range(QB):
                    turn(0, b)
                for qt in range(QUARTERS):
                    for i in range(FT):
                        dft(qt, i)
                        if qt + 1 < QUARTERS:
                            turn(qt + 1, i)
                        if i == 0 and qt:
                            correlate(qt - 1)
                correlate(QUARTERS - 1)
                pe.wait_ge(leads, 4)
                pe.transpose(tp[0:1, 0, 0:P], least[:, :], ident[:, :]).then_inc(least_t, 1)


TURNS = (["xn", "x_turned", "xT", "x_dft", "x_spectrum", "re2", "im2", "power", "power_0", "power_512",
          "power_turned", "powerT", "corr_mm", "corr", "best", "at", "at_f", "minus", "exp", "rtotal", "weights",
          "spread_0"] + [f"{what}_{j}" for j in range(1, TOP_K) for what in ("one", "spread")] +
         ["w_turned", "wT", "w_dft", "w_spectrum", "rr", "ii", "re", "ir", "ri", "im", "re_0", "re_512",
          "a_turned", "aT", "agg", "added"])


def delay_average(nc, ctx, h, ident, f_dram, g_dram, lags, rstd, shift):
    def sb(name, shape, dt=F32):
        return ctx.enter_context(nc.sbuf_tensor(name, shape, dt))

    fwd, inv = sb("da_fwd", [P, KT, L]), sb("da_inv", [P, KT, L])
    lag_row = sb("da_lags", [P, L])
    xn, corr, spread, one = (sb(f"da_{n}", [P, L]) for n in ("xn", "corr", "spread", "one"))
    xT = sb("da_xT", [P, KT, P])
    xs, ws, sq, am = (sb(f"da_{n}", [P, 2, HALF]) for n in ("xs", "ws", "sq", "am"))
    power = sb("da_power", [P, KT // 2 + 1, P])
    best, at_f, weights = (sb(f"da_{n}", [P, 8]) for n in ("best", "at_f", "weights"))
    at = sb("da_at", [P, 8], mybir.dt.uint32)
    minus, total, rtotal, dummy = (sb(f"da_{n}", [P, 1]) for n in ("minus", "total", "rtotal", "dummy"))
    tp = ctx.enter_context(nc.psum_tensor("da_tp", [P, KT, P], F32))
    mm = ctx.enter_context(nc.psum_tensor("da_mm", [P, 2, BANK], F32))
    tables = ctx.enter_context(nc.semaphore("da_tables"))
    cleared = ctx.enter_context(nc.semaphore("da_cleared"))
    done = ctx.enter_context(nc.semaphore("da_done"))
    prime(nc, [done])
    S = len(TURNS)
    flat = power[:, :, :].rearrange("p k n -> p (k n)")


    def turn(e, t, name, ins):
        after(e, done, t * S + TURNS.index(name))
        ins().then_inc(done, 1)

    def sync(sp):
        sp.dma_start(fwd[:, :, :].rearrange("p k n -> p (k n)"), f_dram).then_inc(tables, 16)
        sp.dma_start(inv[:, :, :].rearrange("p k n -> p (k n)"), g_dram).then_inc(tables, 16)
        sp.dma_start(lag_row[:, :], lags).then_inc(tables, 16)

    def scalar(act):
        act.wait_ge(cleared, 1)
        with act.Fori(0, NB) as t:
            turn(act, t, "xn", lambda: act.activation(
                xn[:, :], row(h, t), ACT.Identity,
                bias=shift[:, bass.ds(t, 1)], scale=rstd[:, bass.ds(t, 1)]))
            turn(act, t, "xT", lambda: act.copy(xT[:, :, :], tp[:, :, :]))
            turn(act, t, "x_spectrum", lambda: act.copy(xs[:, :, :], mm[:, :, :]))
            turn(act, t, "powerT", lambda: act.copy(xT[:, 0:5, :], tp[:, 0:5, :]))
            turn(act, t, "corr", lambda: act.copy(corr[:, :], mm[:, :, :].rearrange("p a n -> p (a n)")))
            turn(act, t, "exp", lambda: act.activation(
                weights[:, 0:TOP_K], best[:, 0:TOP_K], ACT.Exp, bias=minus[:, :], accum_out=total[:, :]))
            turn(act, t, "wT", lambda: act.copy(xT[:, :, :], tp[:, :, :]))
            turn(act, t, "w_spectrum", lambda: act.copy(ws[:, :, :], mm[:, :, :]))
            turn(act, t, "aT", lambda: act.copy(xT[:, :, :], tp[:, :, :]))

    def vector(dve):
        dve.wait_ge(tables, 48)
        dve.memset(power[:, KT // 2, :], 0.0).then_inc(cleared, 1)
        re, im = slice(0, 1), slice(1, 2)

        def product(out, a, b):
            return lambda: dve.tensor_tensor(out, a, b, ALU.mult)
        with dve.Fori(0, NB) as t:
            turn(dve, t, "re2", product(sq[:, 0, :], xs[:, 0, :], xs[:, 0, :]))
            turn(dve, t, "im2", product(sq[:, 1, :], xs[:, 1, :], xs[:, 1, :]))
            turn(dve, t, "power", lambda: dve.tensor_tensor(flat[:, 0:HALF], sq[:, 0, :], sq[:, 1, :], ALU.add))
            turn(dve, t, "power_0", lambda: dve.tensor_copy(flat[:, 0:1], sq[:, 0, 0:1]))
            turn(dve, t, "power_512", lambda: dve.tensor_copy(flat[:, HALF:HALF + 1], sq[:, 1, 0:1]))
            after(dve, done, t * S + TURNS.index("best"))
            dve.memset(dummy[:, :], 0.0)
            dve.max(best[:, :], corr[:, :]).then_inc(done, 1)
            after(dve, done, t * S + TURNS.index("at"))
            dve.memset(dummy[:, :], 0.0)
            dve.max_index(at[:, :], best[:, :], corr[:, :]).then_inc(done, 1)
            turn(dve, t, "at_f", lambda: dve.tensor_copy(at_f[:, :], at[:, :]))
            turn(dve, t, "minus", lambda: dve.tensor_scalar(minus[:, :], best[:, 0:1], -1.0, None, ALU.mult))
            turn(dve, t, "rtotal", lambda: dve.reciprocal(rtotal[:, :], total[:, :]))
            turn(dve, t, "weights", lambda: dve.tensor_scalar(
                weights[:, 0:TOP_K], weights[:, 0:TOP_K], rtotal[:, :], None, ALU.mult))
            for j in range(TOP_K):
                dst = spread if j == 0 else one
                turn(dve, t, "spread_0" if j == 0 else f"one_{j}", lambda: dve.tensor_scalar(
                    dst[:, :], lag_row[:, :], at_f[:, j:j + 1], weights[:, j:j + 1], ALU.is_equal, ALU.mult))
                if j:
                    turn(dve, t, f"spread_{j}", lambda: dve.tensor_tensor(
                        spread[:, :], spread[:, :], one[:, :], ALU.add))
            turn(dve, t, "rr", product(sq[:, 0, :], xs[:, 0, :], ws[:, 0, :]))
            turn(dve, t, "ii", product(sq[:, 1, :], xs[:, 1, :], ws[:, 1, :]))
            turn(dve, t, "re", lambda: dve.tensor_tensor(am[:, 0, :], sq[:, 0, :], sq[:, 1, :], ALU.add))
            turn(dve, t, "ir", product(sq[:, 0, :], xs[:, 1, :], ws[:, 0, :]))
            turn(dve, t, "ri", product(sq[:, 1, :], xs[:, 0, :], ws[:, 1, :]))
            turn(dve, t, "im", lambda: dve.tensor_tensor(am[:, 1, :], sq[:, 0, :], sq[:, 1, :], ALU.subtract))
            turn(dve, t, "re_0", product(am[:, 0, 0:1], xs[:, 0, 0:1], ws[:, 0, 0:1]))
            turn(dve, t, "re_512", product(am[:, 1, 0:1], xs[:, 1, 0:1], ws[:, 1, 0:1]))
            turn(dve, t, "added", lambda: dve.tensor_tensor(
                row(h, t), row(h, t), mm[:, :, :].rearrange("p a n -> p (a n)"), ALU.add))

    def tensor(pe):
        pe.wait_ge(tables, 48)

        def turned(t, name, src, tiles):
            after(pe, done, t * S + TURNS.index(name))
            for k in range(tiles):
                last = pe.transpose(tp[:, k, :], src[:, k * P:(k + 1) * P], ident[:, :])
            last.then_inc(done, 1)

        def transform(t, name, table, tiles):
            after(pe, done, t * S + TURNS.index(name))
            for c in range(2):
                for k in range(tiles):
                    last = pe.matmul(mm[:, c, :], xT[:, k, :], table[:, k, c * BANK:(c + 1) * BANK],
                                     start=(k == 0), stop=(k == tiles - 1))
            last.then_inc(done, 1)

        with pe.Fori(0, NB) as t:
            turned(t, "x_turned", xn, KT)
            transform(t, "x_dft", fwd, KT)
            turned(t, "power_turned", flat, KT // 2 + 1)
            transform(t, "corr_mm", inv, KT // 2 + 1)
            turned(t, "w_turned", spread, KT)
            transform(t, "w_dft", fwd, KT)
            turned(t, "a_turned", am[:, :, :].rearrange("p a n -> p (a n)"), KT)
            transform(t, "agg", inv, KT)

    return sync, scalar, vector, tensor


def delay_stage(nc, h, ident, f_dram, g_dram, c_dram, lags):
    with ExitStack() as ctx:
        def sb(name, shape, dt=F32):
            return ctx.enter_context(nc.sbuf_tensor(name, shape, dt))

        rstd, shift, gain = sb("dl_rstd", [P, NB]), sb("dl_shift", [P, NB]), sb("dl_gain", [P, NB])
        flag = sb("dl_flag", [1, 1], I32)
        gained = ctx.enter_context(nc.semaphore("dl_gained"))
        screen(nc, h, ident, f_dram, c_dram, rstd, shift, flag)
        sync, scalar, vector, tensor = delay_average(nc, ctx, h, ident, f_dram, g_dram, lags, rstd, shift)
        ACT_TILES = 6

        with nc.Block() as block:

            def only_zero(e):
                return e.value_load(flag[0:1, 0:1], min_val=0, max_val=1)

            @block.sync
            def _(sp):
                with sp.If(only_zero(sp) < 1):
                    sync(sp)

            @block.tensor
            def _(pe):
                with pe.If(only_zero(pe) < 1):
                    tensor(pe)

            @block.vector
            def _(dve):
                with dve.If(only_zero(dve) < 1):
                    vector(dve)
                with dve.Else():
                    dve.tensor_scalar(gain[:, :], rstd[:, :], 1.0, None, ALU.add).then_inc(gained, 1)
                    dve.wait_ge(gained, 1)
                    for t in range(ACT_TILES, NB):
                        dve.tensor_scalar(h[:, t, :], h[:, t, :], gain[:, t:t + 1], shift[:, t:t + 1],
                                          ALU.mult, ALU.add)

            @block.scalar
            def _(act):
                with act.If(only_zero(act) < 1):
                    scalar(act)
                with act.Else():
                    act.wait_ge(gained, 1)
                    for t in range(ACT_TILES):
                        act.activation(h[:, t, :], h[:, t, :], ACT.Identity,
                                       bias=shift[:, t:t + 1], scale=gain[:, t:t + 1])


DK = 32
QK = EXPERTS * DK
QKA = 2 * QK + ER


def final_stage(nc, h, ident, w_t, qka_t, bm_t, bias, out_dram):
    SC = float(DK) ** -0.5
    with ExitStack() as ctx:
        def sb(name, shape, dt=F32):
            return ctx.enter_context(nc.sbuf_tensor(name, shape, dt))

        def sem(name):
            return ctx.enter_context(nc.semaphore(name))

        (w_hi, w_lo), (p_hi, p_lo), (b_hi, b_lo) = load_split(
            nc, ctx, "fn_w", [("w", w_t), ("qka", qka_t), ("bm", bm_t)], 1024)
        rows = Rows(nc, ctx, "fn", h, ident)
        bias_row = sb("fn_bias", [P, L])
        q = sb("fn_q", [P, QK])
        qk = sb("fn_qk", [P, QK])
        s8, w8 = sb("fn_s8", [P, EXPERTS]), sb("fn_w8", [P, EXPERTS])
        col = {n: sb(f"fn_{n}", [P, 1]) for n in ("top", "ntop", "total", "rtotal")}
        wh = sb("fn_wh", [P, ER])
        wt_hi, wt_lo = sb("fn_wthi", [P, P], F32R), sb("fn_wtlo", [P, P], F32R)
        ka = ctx.enter_context(nc.psum_tensor("fn_ka", [P, BANK], F32))
        qp = ctx.enter_context(nc.psum_tensor("fn_qp", [P, BANK], F32))
        out = ctx.enter_context(nc.psum_tensor("fn_out", [P, 2, 2, BANK], F32))
        bias_in, ka_done, q_done, gate = sem("fn_bias_in"), sem("fn_ka_done"), sem("fn_q_done"), sem("fn_gate")
        exp_done, biased = sem("fn_exp_done"), sem("fn_biased")
        wh_done, wt_mm, wthi_done, wtlo_done = sem("fn_wh_done"), sem("fn_wt_mm"), sem("fn_wthi"), sem("fn_wtlo")
        out_mm, added = sem("fn_out_mm"), sem("fn_added")
        stored = sem("fn_stored")
        prime(nc, [ka_done, q_done, gate, exp_done, biased, wh_done, wt_mm, wthi_done, wtlo_done, out_mm, added])
        GATE_LINKS = 6

        with nc.Block() as block:

            @block.sync
            def _(sp):
                sp.dma_start(bias_row[:, :], bias).then_inc(bias_in, 16)
                with sp.Fori(0, NB) as t:
                    after(sp, added, t + 1)
                    sp.dma_start(out_dram[bass.ds(t, 1), :, :].rearrange("b p l -> (b p) l"), row(h, t))\
                      .then_inc(stored, 16)
                sp.wait_ge(stored, 16 * NB)

            @block.gpsimd
            def _(pool):
                pool.wait_ge(bias_in, 16)
                with pool.Fori(0, NB) as t:
                    after(pool, rows.normed, t + 1)
                    pool.tensor_tensor(row(h, t), row(h, t), bias_row[:, :], ALU.add).then_inc(biased, 1)

            @block.scalar
            def _(act):
                def before():
                    rows.normalize(act, 0, 0)
                    rows.high(act, 0, 0, out_mm, 0)

                def body(t, par, last):
                    after(act, q_done, t + 1)
                    after(act, gate, t * GATE_LINKS)
                    act.copy(q[:, :], qp[:, 0:QK]).then_inc(exp_done, 1)
                    if not last:
                        rows.normalize(act, t + 1, 1 - par)
                        rows.high(act, t + 1, 1 - par, out_mm, t)
                    after(act, gate, t * GATE_LINKS + 4)
                    act.activation(s8[:, :], s8[:, :], ACT.Exp, bias=col["ntop"][:, :], scale=SC,
                                   accum_out=col["total"][:, :]).then_inc(exp_done, 1)
                    after(act, wt_mm, t + 1)
                    act.copy(wt_hi[:, :], qp[:, 0:P]).then_inc(wthi_done, 1)
                tile_steps(act, before, body, lambda: None)

            @block.vector
            def _(dve):
                def before():
                    rows.stats(dve, 0, 0)
                    rows.low(dve, 0, 0)

                def gate_of(t):
                    link = Links(dve, gate, t * GATE_LINKS + 1)
                    after(dve, ka_done, t + 1)
                    after(dve, exp_done, 2 * t + 1)
                    link(dve.tensor_tensor(qk[:, :], ka[:, 0:QK], q[:, :], ALU.mult))
                    link(dve.tensor_reduce(s8[:, :], qk[:, :].rearrange("p (e d) -> p e d", d=DK), AX.X, ALU.add))
                    link(dve.tensor_reduce(col["top"][:, :], s8[:, :], AX.X, ALU.max))
                    link(dve.tensor_scalar(col["ntop"][:, :], col["top"][:, :], -SC, None, ALU.mult))
                    after(dve, exp_done, 2 * t + 2)
                    link(dve.reciprocal(col["rtotal"][:, :], col["total"][:, :]))
                    link(dve.tensor_scalar(w8[:, :], s8[:, :], col["rtotal"][:, :], None, ALU.mult))
                    assert link.n == GATE_LINKS
                    after(dve, wt_mm, t)
                    dve.tensor_tensor(wh[:, :].rearrange("p (e r) -> p e r", r=RANK),
                                      ka[:, QK:QK + ER].rearrange("p (e r) -> p e r", r=RANK),
                                      w8[:, :].rearrange("p (e a) -> p e a", a=1).to_broadcast([P, EXPERTS, RANK]),
                                      ALU.mult).then_inc(wh_done, 1)

                def add(t, par):
                    after(dve, out_mm, t + 1)
                    after(dve, biased, t + 1)
                    hb = row(h, t)
                    dve.tensor_tensor(hb, hb, out[:, par, :, :].rearrange("p a n -> p (a n)"), ALU.add)\
                       .then_inc(added, 1)

                def body(t, par, last):
                    if not last:
                        rows.stats(dve, t + 1, 1 - par)
                    gate_of(t)
                    if not last:
                        rows.low(dve, t + 1, 1 - par)
                    after(dve, wthi_done, t + 1)
                    dve.tensor_tensor(wt_lo[:, :], qp[:, 0:P], wt_hi[:, :].bitcast(F32), ALU.subtract)\
                       .then_inc(wtlo_done, 1)
                    add(t, par)
                tile_steps(dve, before, body, lambda: None)

            @block.tensor
            def _(pe):
                def before():
                    rows.turn(pe, 0, 0)

                def group(t, par, dst, w_halves, width, lo, hi, final=True):
                    xh, xl = rows.x_hi[par], rows.x_lo[par]
                    wh_, wl_ = w_halves
                    for k in range(KT):
                        w = slice(k * width + lo, k * width + hi)
                        pe.matmul(dst, xh[:, k, :], wh_[:, w], start=(k == 0), stop=False)
                        pe.matmul(dst, xh[:, k, :], wl_[:, w], start=False, stop=False)
                        mm = pe.matmul(dst, xl[:, k, :], wh_[:, w], start=False, stop=(final and k == KT - 1))
                    return mm

                def body(t, par, last):
                    after(pe, rows.lo_done, t + 1)
                    after(pe, wtlo_done, t)
                    group(t, par, qp[:, 0:QK], (p_hi, p_lo), QKA, 0, QK).then_inc(q_done, 1)
                    after(pe, wh_done, t)
                    group(t, par, ka[:, 0:QK + ER], (p_hi, p_lo), QKA, QK, QKA).then_inc(ka_done, 1)
                    if not last:
                        rows.turn(pe, t + 1, 1 - par)
                    after(pe, added, t - 1)
                    for c in range(2):
                        group(t, par, out[:, par, c, :], (w_hi, w_lo), L, c * BANK, (c + 1) * BANK, final=False)
                    after(pe, wh_done, t + 1)
                    pe.transpose(qp[:, 0:P], wh[:, :], ident[:, :]).then_inc(wt_mm, 1)
                    after(pe, wtlo_done, t + 1)
                    for c in range(2):
                        w = slice(c * BANK, (c + 1) * BANK)
                        dst = out[:, par, c, :]
                        pe.matmul(dst, wt_hi[:, :], b_hi[:, w], start=False, stop=False)
                        pe.matmul(dst, wt_hi[:, :], b_lo[:, w], start=False, stop=False)
                        mm = pe.matmul(dst, wt_lo[:, :], b_hi[:, w], start=False, stop=True)
                    mm.then_inc(out_mm, 1)
                tile_steps(pe, before, body, lambda: None)


def audio_tower(nc, x, conv_w, dw_w, chan, pw_t, w_qkv, w_o, rope, a_route, bw, experts, dft_fwd, dft_inv,
                lag_cos, lags, w_t, qka_t, bm_t, bias, out):
    with ExitStack() as ctx:
        h = ctx.enter_context(nc.sbuf_tensor("h", [P, NB, L], F32))
        ident = ctx.enter_context(nc.sbuf_tensor("ident", [P, P], F32))
        ones_mean = ctx.enter_context(nc.sbuf_tensor("ones_mean", [P, P], F32))
        setup_constants(nc, ctx, ident, ones_mean)
        conv_stage(nc, h, ident, ones_mean, x, conv_w, dw_w, chan, pw_t)
        attention_stage(nc, h, ident, w_qkv, w_o, rope)
        mixture_stage(nc, h, ident, a_route, bw, experts)
        delay_stage(nc, h, ident, dft_fwd, dft_inv, lag_cos, lags)
        final_stage(nc, h, ident, w_t, qka_t, bm_t, bias, out)


def _layout(a):
    import numpy as np

    def flat(m):
        return np.ascontiguousarray(m)

    def moving(w):
        return flat(w.reshape(w.shape[0], KT, P).transpose(2, 1, 0).reshape(P, KT * w.shape[0]))

    def head_tiles(w):
        n = w.shape[0] // P
        return w.reshape(n, P, KT, P).transpose(0, 3, 2, 1).reshape(n, P, L)

    def packed(m):
        return flat(m.reshape(-1, P, m.shape[1]).transpose(1, 0, 2).reshape(P, -1).astype(np.float32))

    taps = np.zeros((P, C_IN, 2 * PAIRS), np.float32)
    taps[:, :, :TAPS] = a["L0_tok_conv_in_w"]
    q = head_tiles(a["L0_attn_Wq"]).reshape(KV, HEADS, P, L)
    k, v = (head_tiles(a[f"L0_attn_{n}"])[:, None] for n in ("Wk", "Wv"))
    inv_freq = (1.0 / np.power(np.float32(500000.0), np.arange(0, D, 2, dtype=np.float32) / np.float32(D)))
    angle = np.arange(P, dtype=np.float32)[:, None] * inv_freq.astype(np.float32)[None]
    angle = np.concatenate([angle, angle], 1).astype(np.float64).T
    turn = np.sin(angle)
    turn[D // 2:] *= -1.0
    n = np.arange(L)
    w = 2 * np.pi * (n[:, None] * n[None, :] % L) / L
    cos, sin = np.cos(w), np.sin(w)
    fwd = np.concatenate([cos[:, :HALF], cos[:, HALF:HALF + 1], -sin[:, 1:HALF]], 1)
    twice = np.where(n[:HALF, None] == 0, 1.0, 2.0)
    inv = np.concatenate([cos[:HALF] * twice, cos[HALF:HALF + 1], -2 * sin[1:HALF]], 0) / L

    def all_rows(r):
        return flat(np.broadcast_to(r, (P, r.shape[0])))

    return {
        "x": flat(a["x"]),
        "conv_w": flat(taps.reshape(P, C_IN, PAIRS, 2).transpose(3, 1, 2, 0).reshape(P, PAIRS * P)),
        "dw_w": flat(a["L0_tok_dw_w"].reshape(P, DW)),
        "chan": flat(np.stack([a[f"L0_tok_{m}"] for m in ("dw_b", "gn1_w", "gn1_b", "gn2_w", "gn2_b")], 1)),
        "pw_t": flat(a["L0_tok_pw_w"][:, :, 0].T),
        "w_qkv": flat(np.concatenate([k, v, q], 1)),
        "w_o": flat(a["L0_attn_Wo"].T.reshape(KV, HEADS, D, L)),
        "rope": flat(np.stack([np.cos(angle), turn], 1).astype(np.float32)),
        "a_route": moving(np.concatenate([a["L0_ffn_A"].reshape(ER, L), a["L0_ffn_route_w"]], 0)),
        "bw": flat(a["L0_ffn_Bw"].transpose(0, 2, 1).reshape(ER, L)),
        "experts": all_rows(np.arange(EXPERTS, dtype=np.float32)),
        "dft_fwd": packed(fwd),
        "dft_inv": packed(inv),
        "lag_cos": packed(inv[:HALF, 1:HALF + 1]),
        "lags": all_rows(np.arange(L, dtype=np.float32)),
        "w_t": moving(a["L1_ffn_W"]),
        "qka_t": moving(np.concatenate([a["L1_ffn_Wq"], a["L1_ffn_Wk"], a["L1_ffn_A"].reshape(ER, L)], 0)),
        "bm_t": flat(a["L1_ffn_Bm"].transpose(0, 2, 1).reshape(ER, L)),
        "bias": all_rows(a["L1_ffn_b"]),
    }


def kernel(**inputs):
    import numpy as _np
    import concourse.bacc as _bacc
    from concourse import mybir as _mybir
    from concourse.bass_utils import run_bass_kernel_spmd as _run

    nc = _bacc.Bacc("TRN2", target_bir_lowering=False, num_devices=1)
    arrays, args = {}, []
    for name, a in _layout({k: _np.asarray(v) for k, v in inputs.items()}).items():
        arrays[f"in_{name}_dram"] = a
        args.append(nc.dram_tensor(f"in_{name}_dram", a.shape, _mybir.dt.from_np(a.dtype), kind="ExternalInput").ap())
    out = nc.dram_tensor("out_dram", (NB, P, L), _mybir.dt.float32, kind="ExternalOutput").ap()
    audio_tower(nc, *args, out)
    r = _run(nc, [arrays], core_ids=[0])
    return r.results[0]["out_dram"]
```

```python
from contextlib import ExitStack

import concourse.bass as bass
from concourse import mybir

F32 = mybir.dt.float32
F32R = mybir.dt.float32r
I32 = mybir.dt.int32
ALU = mybir.AluOpType
ACT = mybir.ActivationFunctionType
AX = mybir.AxisListType

P = 128
NB = 16
C_IN = 64
T_IN = 2048
L = 1024
KT = L // P
BANK = 512
EPS = 1e-5
TAPS, PAD = 7, 3
PAIRS = (TAPS + 1) // 2
DW, DW_PAD = 5, 2
RSQRT_SEED = 0x5F3759DF
NEWTON = 3
RSQRT_LINKS = 3 + NEWTON * 3


class Links:

    def __init__(self, engine, sem, base):
        self.engine, self.sem, self.base, self.n = engine, sem, base, 0

    def __call__(self, ins):
        self.n += 1
        ins.then_inc(self.sem, 1)
        self.engine.wait_ge(self.sem, self.base + self.n)


def rsqrt(e, y, v, t, link):
    link(e.tensor_scalar(t.bitcast(I32), v.bitcast(I32), 1, None, ALU.logical_shift_right))
    link(e.tensor_scalar(y.bitcast(I32), t.bitcast(I32), -1.0, float(RSQRT_SEED), ALU.mult, ALU.add))
    link(e.tensor_scalar(v, v, -0.5, None, ALU.mult))
    for _ in range(NEWTON):
        link(e.tensor_tensor(t, y, y, ALU.mult))
        link(e.tensor_tensor(t, t, v, ALU.mult))
        link(e.scalar_tensor_tensor(out=y, in0=t, scalar=1.5, in1=y, op0=ALU.add, op1=ALU.mult))


def row(ap3, i):
    return ap3[:, bass.ds(i, 1), :].rearrange("p a n -> p (a n)")


def early(i, n):
    return isinstance(i, int) and i < n


def prime(nc, sems):
    with nc.Block() as block:

        @block.sync
        def _(sp):
            for s in sems:
                sp.sem_inc(s, 1)


def after(engine, sem, count):
    if not early(count, 1):
        engine.wait_ge(sem, count + 1)


def setup_constants(nc, ctx, ident, ones_mean):
    filled = ctx.enter_context(nc.semaphore("const_filled"))
    with nc.Block() as block:

        @block.gpsimd
        def _(pool):
            pool.memset(ident[:, :], 1.0).then_inc(filled, 1)
            pool.memset(ones_mean[:, :], 1.0 / P)
            pool.wait_ge(filled, 1)
            pool.affine_select(out=ident[:, :], in_=ident[:, :], compare_op=ALU.is_equal, fill=0.0,
                               base=0, pattern=[[-1, P]], channel_multiplier=1).then_inc(filled, 1)
            pool.wait_ge(filled, 2)


def conv_stage(nc, h, ident, ones_mean, x, conv_w, dw_w, chan, pw_wT):
    XW = T_IN + 2 * PAD + 2
    GW = T_IN + 2 * DW_PAD
    NCH = T_IN // BANK
    T2 = T_IN // 2
    LAST = NB + 3
    with ExitStack() as ctx:
        def sb(name, shape, dt=F32):
            return ctx.enter_context(nc.sbuf_tensor(name, shape, dt))

        def sem(name):
            return ctx.enter_context(nc.semaphore(name))

        x_in = [sb(f"cv_x{i}", [P, XW]) for i in range(2)]
        x_hi = [sb(f"cv_xhi{i}", [P, XW], F32R) for i in range(2)]
        x_lo = [sb(f"cv_xlo{i}", [P, XW], F32R) for i in range(2)]
        raw = [sb(f"cv_raw{i}", [P, T_IN]) for i in range(2)]
        g = sb("cv_g", [P, GW])
        tap_0 = sb("cv_tap0", [P, T2])
        y = sb("cv_y", [P, T2])
        y_hi = sb("cv_yhi", [P, T2], F32R)
        y_lo = sb("cv_ylo", [P, T2], F32R)
        cw = sb("cv_w", [P, PAIRS * P])
        cw_hi = sb("cv_whi", [P, PAIRS * P], F32R)
        cw_lo = sb("cv_wlo", [P, PAIRS * P], F32R)
        pw = sb("cv_pw", [P, P])
        pw_hi = sb("cv_pwhi", [P, P], F32R)
        pw_lo = sb("cv_pwlo", [P, P], F32R)
        dww = sb("cv_dww", [P, DW])
        ch = sb("cv_ch", [P, 5])
        dummy = sb("cv_dummy", [P, 1])
        carrier = sb("cv_carrier", [P, 1])
        st = [sb(f"cv_st{n}", [P, 4, 6]) for n in range(2)]
        mv = sb("cv_mv", [P, 2, 2])
        mean, dev, var, tmp, rstd, scale, shift = (
            sb(f"cv_{n}", [P, 2]) for n in ("mean", "dev", "var", "tmp", "rstd", "scale", "shift"))
        cp = ctx.enter_context(nc.psum_tensor("cv_cp", [P, NCH, BANK], F32))
        pp = ctx.enter_context(nc.psum_tensor("cv_pp", [P, 2, BANK], F32))
        sp = ctx.enter_context(nc.psum_tensor("cv_sp", [P, BANK], F32))

        w_loaded, pads, w_hi_done, w_lo_done = sem("cv_w_loaded"), sem("cv_pads"), sem("cv_whi_d"), sem("cv_wlo_d")
        x_loaded = [sem(f"cv_x_loaded{i}") for i in range(2)]
        xhi_done, xlo_done = sem("cv_xhi_done"), sem("cv_xlo_done")
        conv_done, raw_done = sem("cv_conv_done"), sem("cv_raw_done")
        head_done = [sem(f"cv_head_done{n}") for n in range(2)]
        chain = sem("cv_chain")
        mean_mm = sem("cv_mean_mm")
        coef = sem("cv_coef")
        gelu1, tap_done, dw_acc, yhi_done, ylo_done = sem("cv_gelu1"), sem("cv_tap_done"), sem("cv_dw_acc"), sem("cv_yhi"), sem("cv_ylo")
        pw_done, gelu2 = sem("cv_pw_done"), sem("cv_gelu2")

        HEAD_LINKS = 2
        MIDDLE_LINKS = 3
        CHAIN_LINKS = MIDDLE_LINKS + 1 + RSQRT_LINKS + 2
        DW_LINKS = DW - 1

        def steps(e, body):
            def peeled(it):
                body(it, it % 2, lambda k: 0 <= it - k < NB)
            for it in range(4):
                peeled(it)
            with e.Fori(2, NB // 2 - 1) as pair:
                body(pair * 2, 0, lambda k: True)
                body(pair * 2 + 1, 1, lambda k: True)
            for it in range(NB - 2, LAST):
                peeled(it)

        gv = g[:, :].rearrange("p (t s) -> p t s", s=2)

        with nc.Block() as block:

            @block.sync
            def _(sp_):
                for dst, src in ((cw, conv_w), (pw, pw_wT), (dww, dw_w), (ch, chan)):
                    sp_.dma_start(dst[:, :], src).then_inc(w_loaded, 16)
                sp_.wait_ge(pads, 1)

                def body(it, par, on):
                    if not on(0):
                        return
                    if not early(it, 2):
                        sp_.wait_ge(xlo_done, it - 1)
                    src = x[bass.ds(it, 1), :, :].rearrange("b c t -> (b c) t")
                    sp_.dma_start(x_in[par][0:C_IN, PAD:PAD + T_IN], src).then_inc(x_loaded[par], 16)
                    sp_.dma_start(x_in[par][C_IN:P, PAD - 1:PAD - 1 + T_IN], src).then_inc(x_loaded[par], 16)
                steps(sp_, body)

            @block.gpsimd
            def _(pool):
                for par in range(2):
                    pool.memset(x_in[par][:, 0:PAD], 0.0)
                    pool.memset(x_in[par][:, XW - PAD - 3:XW], 0.0)
                pool.memset(g[:, 0:DW_PAD], 0.0)
                pool.memset(g[:, GW - DW_PAD:GW], 0.0).then_inc(pads, 1)

                def split_in(i, par):
                    pool.wait_ge(xhi_done, i + 1)
                    if not early(i, 2):
                        pool.wait_ge(conv_done, (i - 1) * NCH)
                    pool.tensor_tensor(x_lo[par][:, :], x_in[par][:, :], x_hi[par][:, :].bitcast(F32),
                                       ALU.subtract).then_inc(xlo_done, 1)

                def body(it, par, on):
                    if early(it, 1):
                        split_in(0, 0)
                    if on(-1):
                        split_in(it + 1, 1 - par)
                    if on(2):
                        pool.wait_ge(yhi_done, it - 1)
                        if not early(it, 3):
                            pool.wait_ge(pw_done, it - 2)
                        pool.tensor_tensor(y_lo[:, :], y[:, :], y_hi[:, :].bitcast(F32),
                                           ALU.subtract).then_inc(ylo_done, 1)
                    if on(1):
                        pool.wait_ge(gelu1, it)
                        if not early(it, 2):
                            pool.wait_ge(dw_acc, (it - 1) * DW_LINKS)
                        pool.tensor_tensor(carrier[:, :], ch[:, 0:1], ch[:, 0:1], ALU.add)
                        pool.tensor_scalar(tap_0[:, :], gv[:, 0:T2, 0], dww[:, 0:1], ch[:, 0:1],
                                           ALU.mult, ALU.add).then_inc(tap_done, 1)
                steps(pool, body)

            @block.scalar
            def _(act):
                act.wait_ge(w_loaded, 64)
                act.copy(cw_hi[:, :], cw[:, :])
                act.copy(pw_hi[:, :], pw[:, :]).then_inc(w_hi_done, 1)

                def split_in(i, par):
                    act.wait_ge(x_loaded[par], (i // 2 + 1) * 32)
                    if not early(i, 2):
                        act.wait_ge(conv_done, (i - 1) * NCH)
                    act.copy(x_hi[par][:, :], x_in[par][:, :]).then_inc(xhi_done, 1)

                def body(it, par, on):
                    if early(it, 1):
                        act.wait_ge(pads, 1)
                        split_in(0, 0)

                    def evacuate(c):
                        act.wait_ge(conv_done, it * NCH + c + 1)
                        if c == 0 and not early(it, 2):
                            act.wait_ge(gelu1, it - 1)
                        act.copy(raw[par][:, c * BANK:(c + 1) * BANK], cp[:, c, :]).then_inc(raw_done, 1)

                    if on(0):
                        evacuate(0)
                    if on(-1):
                        split_in(it + 1, 1 - par)
                    if on(0):
                        for c in range(1, NCH - 1):
                            evacuate(c)
                    if on(2):
                        act.wait_ge(dw_acc, (it - 1) * DW_LINKS)
                        if not early(it, 3):
                            act.wait_ge(pw_done, it - 2)
                        act.copy(y_hi[:, :], y[:, :]).then_inc(yhi_done, 1)
                    if on(0):
                        evacuate(NCH - 1)
                    if on(1) or on(3):
                        act.wait_ge(coef, it)
                    if on(3):
                        act.activation(row(h, it - 3), pp[:, :, :], ACT.Gelu,
                                       bias=shift[:, 1:2], scale=scale[:, 1:2]).then_inc(gelu2, 1)
                    if on(1):
                        act.activation(g[:, DW_PAD:DW_PAD + T_IN], raw[1 - par][:, :], ACT.Gelu,
                                       bias=shift[:, 0:1], scale=scale[:, 0:1]).then_inc(gelu1, 1)
                steps(act, body)

            @block.vector
            def _(dve):
                dve.wait_ge(w_hi_done, 1)
                dve.tensor_tensor(cw_lo[:, :], cw[:, :], cw_hi[:, :].bitcast(F32), ALU.subtract)
                dve.tensor_tensor(pw_lo[:, :], pw[:, :], pw_hi[:, :].bitcast(F32), ALU.subtract).then_inc(w_lo_done, 1)

                dve.memset(mv[:, :, :], 0.0)

                def head(n, i, chunks):
                    link = Links(dve, head_done[n], i * HEAD_LINKS)
                    for c, src in enumerate(chunks):
                        if n == 0:
                            dve.wait_ge(raw_done, i * NCH + c + 1)
                        last = dve.bn_stats(st[n][:, c, :], src)
                    link(last)
                    dve.memset(dummy[:, :], 0.0)
                    link(dve.bn_aggr(mv[:, n, :], st[n][:, 0:len(chunks), :]))
                    assert link.n == HEAD_LINKS

                def middle(it):
                    link = Links(dve, chain, (it - 1) * CHAIN_LINKS)
                    dve.wait_ge(mean_mm, 2 * it - 1)
                    dve.tensor_copy(mean[:, :], sp[:, 0:2])
                    link(dve.tensor_tensor(dev[:, :], mv[:, :, 0], sp[:, 0:2], ALU.subtract))
                    link(dve.tensor_tensor(dev[:, :], dev[:, :], dev[:, :], ALU.mult))
                    link(dve.tensor_tensor(dev[:, :], dev[:, :], mv[:, :, 1], ALU.add))
                    assert link.n == MIDDLE_LINKS

                def tail(it):
                    link = Links(dve, chain, (it - 1) * CHAIN_LINKS + MIDDLE_LINKS)
                    gamma_beta = ch[:, 1:5].rearrange("p (n c) -> p n c", c=2)
                    dve.wait_ge(mean_mm, 2 * it)
                    link(dve.tensor_scalar(var[:, :], sp[:, 0:2], EPS, None, ALU.add))
                    rsqrt(dve, rstd[:, :], var[:, :], tmp[:, :], link)
                    link(dve.tensor_tensor(scale[:, :], gamma_beta[:, :, 0], rstd[:, :], ALU.mult))
                    link(dve.tensor_tensor(tmp[:, :], mean[:, :], scale[:, :], ALU.mult))
                    assert link.n == CHAIN_LINKS - MIDDLE_LINKS
                    dve.tensor_tensor(shift[:, :], gamma_beta[:, :, 1], tmp[:, :], ALU.subtract).then_inc(coef, 1)

                def taps(i, which):
                    link = Links(dve, dw_acc, i * DW_LINKS + which[0] - 1)
                    if which[0] == 1:
                        dve.wait_ge(tap_done, i + 1)
                        if not early(i, 1):
                            dve.wait_ge(ylo_done, i)
                    for k in which:
                        link(dve.scalar_tensor_tensor(out=y[:, :], in0=gv[:, k // 2:k // 2 + T2, k % 2],
                                                      scalar=dww[:, k:k + 1], in1=(tap_0 if k == 1 else y)[:, :],
                                                      op0=ALU.mult, op1=ALU.add))

                def body(it, par, on):
                    if on(1):
                        head(0, it - 1, [raw[1 - par][:, c * BANK:(c + 1) * BANK] for c in range(NCH)])
                    if on(3):
                        dve.wait_ge(pw_done, it - 2)
                        head(1, it - 3, [pp[:, c, :] for c in range(2)])
                    if on(2):
                        taps(it - 2, (1, 2))
                    if not early(it, 1):
                        middle(it)
                    if on(2):
                        taps(it - 2, (3, 4))
                    if not early(it, 1):
                        tail(it)
                steps(dve, body)

            @block.tensor
            def _(pe):
                pe.wait_ge(w_lo_done, 1)

                def conv(i, par, c):
                    if not early(i, 1):
                        pe.wait_ge(raw_done, (i - 1) * NCH + c + 1)
                    if c == 0:
                        pe.wait_ge(xhi_done, i + 1)
                    for q in range(PAIRS):
                        w = slice(q * P, (q + 1) * P)
                        cols = slice(c * BANK + 2 * q, (c + 1) * BANK + 2 * q)
                        pe.matmul(cp[:, c, :], cw_hi[:, w], x_hi[par][:, cols], start=(q == 0), stop=False)
                        pe.matmul(cp[:, c, :], cw_lo[:, w], x_hi[par][:, cols], start=False, stop=False)
                    if c == 0:
                        pe.wait_ge(xlo_done, i + 1)
                    for q in range(PAIRS):
                        w = slice(q * P, (q + 1) * P)
                        cols = slice(c * BANK + 2 * q, (c + 1) * BANK + 2 * q)
                        last = pe.matmul(cp[:, c, :], cw_hi[:, w], x_lo[par][:, cols], start=False, stop=(q == PAIRS - 1))
                    last.then_inc(conv_done, 1)

                def average(it, on, which):
                    if early(it, 1):
                        return
                    if which == 0:
                        if on(1):
                            pe.wait_ge(head_done[0], it * HEAD_LINKS)
                        if on(3):
                            pe.wait_ge(head_done[1], (it - 2) * HEAD_LINKS)
                        if not early(it, 2):
                            pe.wait_ge(chain, (it - 1) * CHAIN_LINKS)
                    else:
                        pe.wait_ge(chain, (it - 1) * CHAIN_LINKS + MIDDLE_LINKS)
                    src = mv[:, :, 0] if which == 0 else dev[:, :]
                    pe.matmul(sp[:, 0:2], ones_mean[:, :], src, start=True, stop=True).then_inc(mean_mm, 1)

                def pointwise(i):
                    pe.wait_ge(ylo_done, i + 1)
                    if not early(i, 1):
                        pe.wait_ge(gelu2, i)
                    for c in range(2):
                        cols = slice(c * BANK, (c + 1) * BANK)
                        pe.matmul(pp[:, c, :], pw_hi[:, :], y_hi[:, cols], start=True, stop=False)
                        pe.matmul(pp[:, c, :], pw_hi[:, :], y_lo[:, cols], start=False, stop=False)
                        last = pe.matmul(pp[:, c, :], pw_lo[:, :], y_hi[:, cols], start=False, stop=True)
                    last.then_inc(pw_done, 1)

                def body(it, par, on):
                    if on(0):
                        conv(it, par, 0)
                    if on(3):
                        pointwise(it - 3)
                    if on(0):
                        conv(it, par, 1)
                    average(it, on, 0)
                    if on(0):
                        conv(it, par, 2)
                    average(it, on, 1)
                    if on(0):
                        conv(it, par, 3)
                steps(pe, body)


HEADS = 4
KV = 8
D = 128
QUARTERS = 4
QB = NB // QUARTERS
QT = QB * P
TILES = 2 + HEADS
SCALE = float(D) ** -0.5


def attention_stage(nc, h, ident, w_qkv, w_o, rope):
    STEPS = QUARTERS * KV
    ROPED = TILES - 1
    UNITS = 2 * QB
    with ExitStack() as ctx:
        def sb(name, shape, dt=F32):
            return ctx.enter_context(nc.sbuf_tensor(name, shape, dt))

        def sem(name):
            return ctx.enter_context(nc.semaphore(name))

        def psum(name):
            return ctx.enter_context(nc.psum_tensor(name, [P, BANK], F32))

        x_hi = sb("at_xhi", [P, KT, QT], F32R)
        x_lo = sb("at_xlo", [P, KT, QT], F32R)
        w_stage = [sb(f"at_wstage{i}", [P, L]) for i in range(2)]
        o_stage = [sb(f"at_ostage{i}", [P, L]) for i in range(2)]
        w_hi = [sb(f"at_whi{i}", [P, L], F32R) for i in range(2)]
        w_lo = [sb(f"at_wlo{i}", [P, L], F32R) for i in range(2)]
        wo_hi = sb("at_wohi", [P, HEADS, L], F32R)
        wo_lo = sb("at_wolo", [P, HEADS, L], F32R)
        qT = [sb(f"at_q{i}", [P, HEADS, QT]) for i in range(2)]
        kT = [sb(f"at_k{i}", [P, QT]) for i in range(2)]
        vT = sb("at_vT", [P, QT])
        v = [sb(f"at_v{i}", [P, QB, D]) for i in range(2)]
        probs = sb("at_probs", [P, HEADS, P])
        pT = sb("at_pT", [P, HEADS * P])
        o_hi = sb("at_ohi", [P, HEADS * P], F32R)
        o_lo = sb("at_olo", [P, HEADS * P], F32R)
        cs = sb("at_cs", [P, 2, P])
        turned = sb("at_turned", [P, QT])
        xn = [sb(f"at_xn{i}", [P, L]) for i in range(2)]
        st = sb("at_st", [P, QB, 2, 6])
        mv = sb("at_mv", [P, QB, 2])
        var, rstd, tmp, shift = (sb(f"at_{n}", [P, QB]) for n in ("var", "rstd", "tmp", "shift"))
        dummy = sb("at_dummy", [P, 1])
        top = sb("at_top", [P, HEADS])
        ntop = sb("at_ntop", [P, HEADS])
        total = sb("at_total", [P, HEADS])
        rtotal = sb("at_rtotal", [P, HEADS])
        proj = [psum(f"at_proj{i}") for i in range(2)]
        sc = [psum(f"at_sc{i}") for i in range(2)]
        tp = psum("at_tp")
        ov = psum("at_ov")
        out = ctx.enter_context(nc.psum_tensor("at_out", [P, 2, BANK], F32))

        rope_in = sem("at_rope_in")
        w_staged = [sem(f"at_w_staged{i}") for i in range(2)]
        o_staged = [sem(f"at_o_staged{i}") for i in range(2)]
        whi_done, wlo_done = sem("at_whi_done"), sem("at_wlo_done")
        wohi_done, wolo_done = sem("at_wohi_done"), sem("at_wolo_done")
        norm = sem("at_norm")
        normed, turned_in = sem("at_normed"), sem("at_turned_in")
        xhi_done, xlo_done = sem("at_xhi_done"), sem("at_xlo_done")
        proj_done, roped, vT_done = sem("at_proj_done"), sem("at_roped"), sem("at_vT_done")
        rope_mul = sem("at_rope_mul")
        v_turned, v_done = sem("at_v_turned"), sem("at_v_done")
        sc_done, top_done, ntop_done = sem("at_sc_done"), sem("at_top_done"), sem("at_ntop_done")
        exp_done, rtotal_done, probs_done = sem("at_exp_done"), sem("at_rtotal_done"), sem("at_probs_done")
        pT_mm, pT_done, ov_mm = sem("at_pT_mm"), sem("at_pT_done"), sem("at_ov_mm")
        ohi_done, olo_done = sem("at_ohi_done"), sem("at_olo_done")
        out_mm, added = sem("at_out_mm"), sem("at_added")

        prime(nc, [whi_done, wlo_done, wohi_done, wolo_done, norm, normed, turned_in, xhi_done, xlo_done,
                   proj_done, roped, vT_done, rope_mul, v_turned, v_done, sc_done, top_done, ntop_done, exp_done,
                   rtotal_done, probs_done, pT_mm, pT_done, ov_mm, ohi_done, olo_done, out_mm, added])

        NORM_LINKS = 3 * QB + 1 + RSQRT_LINKS + 1

        def steps(e, first, step):
            first()
            step(0, -1, 1, False, 2, False)

            def quarter(qt, more):
                with e.Fori(0, KV // 2 - 1) as pair:
                    step(qt, pair * 2, 0, True, 2, False)
                    step(qt, pair * 2 + 1, 1, True, 2, False)
                step(qt, KV - 2, 0, True, 2 if more else 1, False)
                step(qt, KV - 1, 1, True, 2 if more else 0, more)
            with e.Fori(0, QUARTERS - 1) as qt:
                quarter(qt, True)
            quarter(QUARTERS - 1, False)

        def head_at(qt, g):
            return qt * KV + g

        def tile_at(s, j):
            return s * TILES + j

        def wrapped(g):
            return g % KV if isinstance(g, int) else g

        def splits(att, nxt):
            order = []
            if nxt:
                order.append(("w", 1, 1))
            if att:
                order += [("o", 0), ("o", 1)]
            if nxt:
                order.append(("w", 1, 2))
            if att:
                order += [("o", 2), ("o", 3)]
            if nxt:
                order += [("w", 1, 3), ("w", 1, 4), ("w", 1, 5)]
            if nxt > 1:
                order.append(("w", 2, 0))
            return order

        def before_turn(g, nxt):
            return isinstance(g, int) and g == KV - 2 and nxt == 2

        assert TILES % 2 == 0 and HEADS % 2 == 0

        with nc.Block() as block:

            @block.sync
            def _(sp):
                def load_w(s, g, j):
                    src = w_qkv[bass.ds(wrapped(g), 1), j, :, :].rearrange("a p n -> (a p) n")
                    sp.dma_start(w_stage[j % 2][:, :], src).then_inc(w_staged[j % 2], 16)

                def load_o(s, g, r):
                    src = w_o[bass.ds(wrapped(g), 1), r, :, :].rearrange("a p n -> (a p) n")
                    sp.dma_start(o_stage[r % 2][:, :], src).then_inc(o_staged[r % 2], 16)

                def first():
                    sp.dma_start(cs[:, :, :], rope).then_inc(rope_in, 16)
                    load_w(0, 0, 0)
                    load_w(0, 0, 1)
                    load_o(0, 0, 0)
                    load_o(0, 0, 1)
                    after(sp, wlo_done, 1)
                    load_w(0, 0, 2)

                def step(qt, g, par, att, nxt, turn):
                    s = head_at(qt, g)
                    for what in splits(att, nxt):
                        if what[0] == "w":
                            ahead, j = what[1] + (what[2] + 2) // TILES, (what[2] + 2) % TILES
                            if ahead <= nxt:
                                after(sp, wlo_done, tile_at(s + what[1], what[2]) + 1)
                                load_w(s + ahead, g + ahead, j)
                        else:
                            r, ahead = (what[1] + 2) % HEADS, (what[1] + 2) // HEADS
                            if ahead == 0 or nxt:
                                after(sp, wolo_done, s * HEADS + what[1] + 1)
                                load_o(s + ahead, g + ahead, r)
                steps(sp, first, step)

            @block.gpsimd
            def _(pool):
                def low(hi, lo, stage, done):
                    pool.tensor_tensor(lo, stage[:, :], hi.bitcast(F32), ALU.subtract).then_inc(done, 1)

                def split_w(n, j):
                    after(pool, whi_done, n + 1)
                    low(w_hi[j % 2][:, :], w_lo[j % 2][:, :], w_stage[j % 2], wlo_done)

                def first():
                    split_w(0, 0)

                def step(qt, g, par, att, nxt, turn):
                    s = head_at(qt, g)
                    for what in splits(att, nxt):
                        if what[0] == "w":
                            split_w(tile_at(s + what[1], what[2]), what[2])
                        else:
                            r = what[1]
                            after(pool, wohi_done, s * HEADS + r + 1)
                            low(wo_hi[:, r, :], wo_lo[:, r, :], o_stage[r % 2], wolo_done)
                steps(pool, first, step)

            @block.scalar
            def _(act):

                def split_w(s, j):
                    act.wait_ge(w_staged[j % 2], (s * (TILES // 2) + j // 2 + 1) * 16)
                    if not (isinstance(s, int) and s == 0 and j < 2):
                        after(act, proj_done, tile_at(s, j) - 1)
                    act.copy(w_hi[j % 2][:, :], w_stage[j % 2][:, :]).then_inc(whi_done, 1)

                def split_o(s, r):
                    act.wait_ge(o_staged[r % 2], (s * (HEADS // 2) + r // 2 + 1) * 16)
                    if r == 0:
                        after(act, out_mm, s * QB)
                    act.copy(wo_hi[:, r, :], o_stage[r % 2][:, :]).then_inc(wohi_done, 1)

                def normalize(qt, b):
                    after(act, norm, (qt + 1) * NORM_LINKS)
                    if b >= 2:
                        after(act, turned_in, qt * UNITS + 2 * b - 2)
                    act.activation(xn[b % 2][:, :], row(h, qt * QB + b), ACT.Identity,
                                   bias=shift[:, b:b + 1], scale=rstd[:, b:b + 1]).then_inc(normed, 1)

                def x_out(qt, b):
                    for c in range(2):
                        after(act, turned_in, qt * UNITS + 2 * b + c + 1)
                        act.copy(x_hi[:, c * KT // 2:(c + 1) * KT // 2, b * P:(b + 1) * P],
                                 proj[c][:, :].rearrange("p (k t) -> p k t", t=P)).then_inc(xhi_done, 1)

                def first():
                    normalize(0, 0)
                    normalize(0, 1)
                    split_w(0, 0)
                    x_out(0, 0)
                    normalize(0, 2)
                    x_out(0, 1)
                    normalize(0, 3)
                    x_out(0, 2)
                    x_out(0, 3)

                def soft(n, b):
                    after(act, ntop_done, n + 1)
                    after(act, pT_mm, n)
                    for r in range(HEADS):
                        last = act.activation(probs[:, r, :], sc[b % 2][:, r * P:(r + 1) * P], ACT.Exp,
                                              bias=ntop[:, r:r + 1], scale=SCALE, accum_out=total[:, r:r + 1])
                    last.then_inc(exp_done, 1)

                def pT_out(n):
                    after(act, pT_mm, n + 1)
                    after(act, ov_mm, n)
                    act.copy(pT[:, :], tp[:, :]).then_inc(pT_done, 1)

                def o_split(n):
                    after(act, ov_mm, n + 1)
                    after(act, out_mm, n)
                    act.copy(o_hi[:, :], ov[:, :]).then_inc(ohi_done, 1)

                def v_out(s):
                    after(act, proj_done, tile_at(s, 1) + 1)
                    act.copy(vT[:, :], proj[1][:, :]).then_inc(vT_done, 1)

                def v_rows(s, par):
                    after(act, v_turned, s + 1)
                    act.copy(v[par][:, :, :], tp[:, :].rearrange("p (b d) -> p b d", d=D)).then_inc(v_done, 1)

                def step(qt, g, par, att, nxt, turn):
                    s = head_at(qt, g)
                    n = s * QB
                    order = splits(att, nxt)

                    def split(*which):
                        for what in which:
                            if what in order:
                                if what[0] == "w":
                                    split_w(s + what[1], what[2])
                                else:
                                    split_o(s, what[1])
                    if att:
                        v_rows(s, par)
                    if turn:
                        x_out(qt + 1, 0)
                        soft(n, 0)
                        normalize(qt + 1, 2)
                        x_out(qt + 1, 1)
                        normalize(qt + 1, 3)
                        x_out(qt + 1, 2)
                        x_out(qt + 1, 3)
                    elif att:
                        soft(n, 0)
                    split(("w", 1, 1), ("o", 0), ("o", 1))
                    if att:
                        pT_out(n)
                        soft(n + 1, 1)
                    split(("w", 1, 2), ("o", 2))
                    if nxt:
                        v_out(s + 1)
                    if att:
                        pT_out(n + 1)
                        o_split(n)
                    split(("o", 3),)
                    if att:
                        soft(n + 2, 2)
                    split(("w", 1, 3),)
                    if att:
                        pT_out(n + 2)
                        o_split(n + 1)
                        soft(n + 3, 3)
                    split(("w", 1, 4),)
                    if att:
                        pT_out(n + 3)
                        o_split(n + 2)
                    split(("w", 1, 5))
                    if att:
                        o_split(n + 3)
                    split(("w", 2, 0))
                    if before_turn(g, nxt):
                        normalize(qt + 1, 0)
                        normalize(qt + 1, 1)
                steps(act, first, step)

            @block.vector
            def _(dve):
                def norm_stats(qt, link, b):
                    for c in range(2):
                        link(dve.bn_stats(st[:, b, c, :], row(h, qt * QB + b)[:, c * BANK:(c + 1) * BANK]))

                def norm_coefficients(link):
                    for b in range(QB):
                        dve.memset(dummy[:, :], 0.0)
                        link(dve.bn_aggr(mv[:, b, :], st[:, b, :, :]))
                    link(dve.tensor_scalar(var[:, :], mv[:, :, 1], EPS, None, ALU.add))
                    rsqrt(dve, rstd[:, :], var[:, :], tmp[:, :], link)
                    link(dve.scalar_tensor_tensor(out=shift[:, :], in0=mv[:, :, 0], scalar=-1.0, in1=rstd[:, :],
                                                  op0=ALU.mult, op1=ALU.mult))
                    assert link.n == NORM_LINKS

                def x_low(qt, b):
                    for c in range(2):
                        after(dve, xhi_done, qt * UNITS + 2 * b + c + 1)
                        tiles, cols = slice(c * KT // 2, (c + 1) * KT // 2), slice(b * P, (b + 1) * P)
                        dve.tensor_tensor(x_lo[:, tiles, cols], proj[c][:, :].rearrange("p (k t) -> p k t", t=P),
                                          x_hi[:, tiles, cols].bitcast(F32), ALU.subtract).then_inc(xlo_done, 1)

                def first():
                    link = Links(dve, norm, 1)
                    for b in range(QB):
                        norm_stats(0, link, b)
                    norm_coefficients(link)
                    for b in range(QB):
                        x_low(0, b)

                def rope_out(s, par, j):
                    n = s * ROPED + (j if j == 0 else j - 1)
                    src = proj[j % 2]
                    dst = kT[par][:, :] if j == 0 else qT[par][:, j - 2, :]
                    HD = D // 2

                    def cols(ap):
                        return ap.rearrange("p (b t) -> p b t", t=P)

                    def table(which, rows):
                        return cs[rows, which:which + 1, :].to_broadcast([HD if rows != slice(0, P) else P, QB, P])
                    after(dve, proj_done, tile_at(s, j) + 1)
                    after(dve, roped, n)
                    dve.tensor_tensor(cols(dst), cols(src[:, :]), table(0, slice(0, P)), ALU.mult)\
                       .then_inc(rope_mul, 1)
                    low, high = slice(0, HD), slice(HD, P)
                    dve.tensor_tensor(cols(turned[low, :]), cols(src[high, :]), table(1, high), ALU.mult)\
                       .then_inc(rope_mul, 1)
                    dve.tensor_tensor(cols(turned[high, :]), cols(src[low, :]), table(1, low), ALU.mult)\
                       .then_inc(rope_mul, 1)
                    after(dve, rope_mul, n * 3 + 3)
                    dve.tensor_tensor(dst, dst, turned[:, :], ALU.add).then_inc(roped, 1)

                def top_of(n, b):
                    after(dve, sc_done, n + 1)
                    dve.tensor_reduce(top[:, :], sc[b % 2][:, :].rearrange("p (r k) -> p r k", k=P),
                                      AX.X, ALU.max).then_inc(top_done, 1)
                    after(dve, top_done, n + 1)
                    dve.tensor_scalar(ntop[:, :], top[:, :], -SCALE, None, ALU.mult).then_inc(ntop_done, 1)

                def normalize(n):
                    after(dve, exp_done, n + 1)
                    dve.reciprocal(rtotal[:, :], total[:, :]).then_inc(rtotal_done, 1)
                    after(dve, rtotal_done, n + 1)
                    dve.tensor_tensor(probs[:, :, :], probs[:, :, :],
                                      rtotal[:, :].rearrange("p (r a) -> p r a", a=1).to_broadcast([P, HEADS, P]),
                                      ALU.mult).then_inc(probs_done, 1)

                def o_split(n):
                    after(dve, ohi_done, n + 1)
                    dve.tensor_tensor(o_lo[:, :], ov[:, :], o_hi[:, :].bitcast(F32), ALU.subtract).then_inc(olo_done, 1)

                def add(qt, n, b):
                    after(dve, out_mm, n + 1)
                    hb = row(h, qt * QB + b)
                    dve.tensor_tensor(hb, hb, out[:, :, :].rearrange("p a n -> p (a n)"), ALU.add).then_inc(added, 1)

                def step(qt, g, par, att, nxt, turn):
                    s = head_at(qt, g)
                    n = s * QB
                    stats = before_turn(g, nxt)
                    if stats:
                        link = Links(dve, norm, (qt + 1) * NORM_LINKS + 1)
                    if att:
                        top_of(n, 0)
                    if turn:
                        x_low(qt + 1, 0)
                    if att:
                        normalize(n)
                    if turn:
                        for b in range(1, QB):
                            x_low(qt + 1, b)
                    if nxt:
                        rope_out(s + 1, 1 - par, 0)
                    if att:
                        top_of(n + 1, 1)
                        normalize(n + 1)
                        top_of(n + 2, 2)
                        o_split(n)
                        normalize(n + 2)
                    if nxt:
                        rope_out(s + 1, 1 - par, 2)
                    if att:
                        top_of(n + 3, 3)
                        o_split(n + 1)
                        add(qt, n, 0)
                        normalize(n + 3)
                    if stats:
                        norm_stats(qt + 1, link, 0)
                    if nxt:
                        rope_out(s + 1, 1 - par, 3)
                    if stats:
                        norm_stats(qt + 1, link, 1)
                    if att:
                        o_split(n + 2)
                        add(qt, n + 1, 1)
                    if stats:
                        norm_stats(qt + 1, link, 2)
                    if nxt:
                        rope_out(s + 1, 1 - par, 4)
                    if stats:
                        norm_stats(qt + 1, link, 3)
                    if att:
                        o_split(n + 3)
                        add(qt, n + 2, 2)
                    if nxt:
                        rope_out(s + 1, 1 - par, 5)
                    if stats:
                        after(dve, normed, (qt + 1) * QB)
                        norm_coefficients(link)
                    if att:
                        add(qt, n + 3, 3)
                dve.wait_ge(rope_in, 16)
                steps(dve, first, step)

            @block.tensor
            def _(pe):
                def turn_rows(qt):
                    for b in range(QB):
                        after(pe, normed, qt * QB + b + 1)
                        for c in range(2):
                            if b > 0:
                                after(pe, xlo_done, qt * UNITS + 2 * b + c - 1)
                            for k in range(KT // 2):
                                at = (c * KT // 2 + k) * P
                                last = pe.transpose(proj[c][:, k * P:(k + 1) * P], xn[b % 2][:, at:at + P],
                                                    ident[:, :])
                            last.then_inc(turned_in, 1)

                def project(qt, s, g, j):
                    after(pe, wlo_done, tile_at(s, j) + 1)
                    if j == 0:
                        after(pe, xlo_done, (qt + 1) * UNITS)
                    if j == 3:
                        after(pe, vT_done, s + 1)
                    else:
                        after(pe, roped, s * ROPED + {0: -1, 1: 0, 2: 1, 4: 2, 5: 3}[j])
                    hi, lo = w_hi[j % 2], w_lo[j % 2]
                    for k in range(KT):
                        w = slice(k * P, (k + 1) * P)
                        pe.matmul(proj[j % 2][:, :], hi[:, w], x_hi[:, k, :], start=(k == 0), stop=False)
                        pe.matmul(proj[j % 2][:, :], hi[:, w], x_lo[:, k, :], start=False, stop=False)
                        last = pe.matmul(proj[j % 2][:, :], lo[:, w], x_hi[:, k, :], start=False, stop=(k == KT - 1))
                    last.then_inc(proj_done, 1)

                def scores(s, n, par, b):
                    if b == 0:
                        after(pe, roped, (s + 1) * ROPED)
                    cols = slice(b * P, (b + 1) * P)
                    for r in range(HEADS):
                        last = pe.matmul(sc[b % 2][:, r * P:(r + 1) * P], qT[par][:, r, cols], kT[par][:, cols],
                                         start=True, stop=True)
                    last.then_inc(sc_done, 1)

                def turn_probs(s, n, b):
                    after(pe, probs_done, n + 1)
                    if b == 0:
                        after(pe, v_done, s + 1)
                    else:
                        after(pe, pT_done, n)
                    for r in range(HEADS):
                        last = pe.transpose(tp[:, r * P:(r + 1) * P], probs[:, r, :], ident[:, :])
                    last.then_inc(pT_mm, 1)

                def values(n, par, b):
                    after(pe, pT_done, n + 1)
                    after(pe, olo_done, n)
                    pe.matmul(ov[:, :], v[par][:, b, :], pT[:, :], start=True, stop=True).then_inc(ov_mm, 1)

                def outputs(s, n, b):
                    after(pe, olo_done, n + 1)
                    after(pe, added, n)
                    if b == 0:
                        after(pe, wolo_done, (s + 1) * HEADS)
                    for r in range(HEADS):
                        rows = slice(r * P, (r + 1) * P)
                        for a, w, first, end in ((o_hi, wo_hi, r == 0, False), (o_hi, wo_lo, False, False),
                                                 (o_lo, wo_hi, False, r == HEADS - 1)):
                            for c in range(2):
                                last = pe.matmul(out[:, c, :], a[:, rows], w[:, r, c * BANK:(c + 1) * BANK],
                                                 start=first, stop=end)
                    last.then_inc(out_mm, 1)

                def turn_v(s):
                    after(pe, vT_done, s + 1)
                    after(pe, pT_done, s * QB)
                    for b in range(QB):
                        last = pe.transpose(tp[:, b * D:(b + 1) * D], vT[:, b * P:(b + 1) * P], ident[:, :])
                    last.then_inc(v_turned, 1)

                def step(qt, g, par, att, nxt, turn):
                    s = head_at(qt, g)
                    n = s * QB
                    for j in range(TILES):
                        if att:
                            if 3 <= j:
                                outputs(s, n + j - 3, j - 3)
                            if 2 <= j:
                                values(n + j - 2, par, j - 2)
                            if j < QB:
                                scores(s, n + j, par, j)
                            if 1 <= j <= QB:
                                turn_probs(s, n + j - 1, j - 1)
                        if turn and j == 0:
                            turn_rows(qt + 1)
                        if nxt:
                            project(qt + 1 if turn else qt, s + 1, g + 1, j)
                    if att:
                        outputs(s, n + QB - 1, QB - 1)
                    if nxt:
                        turn_v(s + 1)
                steps(pe, lambda: turn_rows(0), step)


GROUP = 4


class Rows:

    LINKS = 3 + RSQRT_LINKS + 1

    def __init__(self, nc, ctx, name, h, ident):
        def sb(n, shape, dt=F32):
            return ctx.enter_context(nc.sbuf_tensor(f"{name}_{n}", shape, dt))

        def sem(n):
            return ctx.enter_context(nc.semaphore(f"{name}_{n}"))

        self.h, self.ident = h, ident
        self.xn = sb("xn", [P, L])
        self.x_hi = [sb(f"xhi{i}", [P, KT, P], F32R) for i in range(2)]
        self.x_lo = [sb(f"xlo{i}", [P, KT, P], F32R) for i in range(2)]
        self.st = sb("st", [P, GROUP, 2, 6])
        self.mv = sb("mv", [P, GROUP, 2])
        self.var, self.tmp, self.root = (sb(n, [P, GROUP]) for n in ("var", "tmp", "root"))
        self.rstd, self.shift = sb("rstd", [P, GROUP]), sb("shift", [P, GROUP])
        self.dummy = sb("dummy", [P, 1])
        self.tp = ctx.enter_context(nc.psum_tensor(f"{name}_tp", [P, 2, BANK], F32))
        self.norm = sem("norm")
        self.normed = sem("normed")
        self.turned = sem("turned")
        self.hi_done = sem("xhi_done")
        self.lo_done = sem("xlo_done")
        self.sems = [self.norm, self.normed, self.turned, self.hi_done, self.lo_done]

    def stats(self, dve, group, tiles):
        for i in tiles:
            hb = row(self.h, group * GROUP + i)
            for c in range(2):
                last = dve.bn_stats(self.st[:, i, c, :], hb[:, c * BANK:(c + 1) * BANK])
        if GROUP - 1 in tiles:
            self.coefficients(dve, group, last)

    def coefficients(self, dve, group, last):
        link = Links(dve, self.norm, group * self.LINKS + 1)
        link(last)
        dve.memset(self.dummy[:, :], 0.0)
        for i in range(GROUP):
            last = dve.bn_aggr(self.mv[:, i, :], self.st[:, i, :, :])
        link(last)
        link(dve.tensor_scalar(self.var[:, :], self.mv[:, :, 1], EPS, None, ALU.add))
        rsqrt(dve, self.root[:, :], self.var[:, :], self.tmp[:, :], link)
        after(dve, self.normed, group * GROUP)
        dve.tensor_copy(self.rstd[:, :], self.root[:, :])
        link(dve.scalar_tensor_tensor(out=self.shift[:, :], in0=self.mv[:, :, 0], scalar=-1.0,
                                      in1=self.root[:, :], op0=ALU.mult, op1=ALU.mult))
        assert link.n == self.LINKS

    def normalize(self, act, group, i):
        t = group * GROUP + i
        after(act, self.norm, (group + 1) * self.LINKS)
        after(act, self.turned, t)
        act.activation(self.xn[:, :], row(self.h, t), ACT.Identity,
                       bias=self.shift[:, i:i + 1], scale=self.rstd[:, i:i + 1]).then_inc(self.normed, 1)

    def turn(self, pe, t):
        after(pe, self.normed, t + 1)
        after(pe, self.lo_done, t)
        for k in range(KT):
            last = pe.transpose(self.tp[:, k // 4, (k % 4) * P:(k % 4 + 1) * P],
                                self.xn[:, k * P:(k + 1) * P], self.ident[:, :])
        last.then_inc(self.turned, 1)

    def high(self, act, t, par, used, count):
        after(act, self.turned, t + 1)
        after(act, used, count)
        act.copy(self.x_hi[par][:, :, :], self.tp[:, :, :].rearrange("p a (k t) -> p (a k) t", t=P))\
           .then_inc(self.hi_done, 1)

    def low(self, dve, t, par):
        after(dve, self.hi_done, t + 1)
        dve.tensor_tensor(self.x_lo[par][:, :, :], self.tp[:, :, :].rearrange("p a (k t) -> p (a k) t", t=P),
                          self.x_hi[par][:, :, :].bitcast(F32), ALU.subtract).then_inc(self.lo_done, 1)


def tile_steps(e, before, body, finish):
    GROUPS = NB // GROUP

    def group(g, first, last):
        for i in range(GROUP):
            body(g, i, g * GROUP + i, lambda k: not (first and i + k < 0 or last and i + k >= GROUP))
    before()
    group(0, True, False)
    with e.Fori(1, GROUPS - 1) as g:
        group(g, False, False)
    group(GROUPS - 1, False, True)
    finish()


def landing(nc, ctx, name, shape):
    with nc.sbuf_tensor(f"{name}_raw", shape, F32) as raw:
        pass
    return raw, ctx.enter_context(nc.sbuf_tensor(name, shape, F32R))


class Weight:

    CHUNK = 1024

    def __init__(self, nc, ctx, name, src):
        self.name, self.src, self.n = name, src, src.shape[1]
        self.chunks = -(-self.n // self.CHUNK)
        self.raw, self.lo = landing(nc, ctx, f"{name}_lo", [P, self.n])
        self.landed = [ctx.enter_context(nc.semaphore(f"{name}_landed{c}")) for c in range(self.chunks)]

    def add_high(self, nc, ctx):
        self.hi = ctx.enter_context(nc.sbuf_tensor(f"{self.name}_hi", [P, self.n], F32R))
        self.hi_done = ctx.enter_context(nc.semaphore(f"{self.name}_hi_done"))
        self.lo_done = ctx.enter_context(nc.semaphore(f"{self.name}_lo_done"))
        return self

    def cols(self, c):
        return slice(c * self.CHUNK, min(self.n, (c + 1) * self.CHUNK))

    def load(self, sp):
        for c in range(self.chunks):
            sp.dma_start(self.raw[:, self.cols(c)], self.src[:, self.cols(c)]).then_inc(self.landed[c], 16)

    def high(self, act):
        for c in range(self.chunks):
            act.wait_ge(self.landed[c], 16)
            act.copy(self.hi[:, self.cols(c)], self.raw[:, self.cols(c)]).then_inc(self.hi_done, 1)

    def low(self, e, chunks=None):
        for c in range(self.chunks) if chunks is None else chunks:
            e.wait_ge(self.hi_done, c + 1)
            cols = self.cols(c)
            e.tensor_tensor(self.lo[:, cols], self.raw[:, cols], self.hi[:, cols].bitcast(F32), ALU.subtract)\
             .then_inc(self.lo_done, 1)

    def ready(self, pe):
        pe.wait_ge(self.lo_done, self.chunks)


EXPERTS = 8
RANK = 16
ER = EXPERTS * RANK
ROUTED = ER + EXPERTS


class ScreenTables:

    def __init__(self, nc, ctx, f_dram, c_dram):
        f_raw, self.f_hi = landing(nc, ctx, "sc_fhi", [P, KT, L])
        c_raw, self.c_hi = landing(nc, ctx, "sc_chi", [P, KT // 2, HALF])
        self.landed = ctx.enter_context(nc.semaphore("sc_tables_landed"))
        self.rounded = ctx.enter_context(nc.semaphore("sc_tables_rounded"))

        def pair(ap, k):
            return ap[:, k:k + 2, :].rearrange("p k n -> p (k n)")
        self.chunks = [(self.f_hi[:, k, :], f_raw[:, k, :], f_dram[:, k * L:(k + 1) * L]) for k in range(KT)]
        self.chunks += [(pair(self.c_hi, k), pair(c_raw, k), c_dram[:, k * HALF:(k + 2) * HALF])
                        for k in range(0, KT // 2, 2)]

    def load(self, sp):
        for _, raw, src in self.chunks:
            sp.dma_start(raw, src).then_inc(self.landed, 16)

    def round(self, pool):
        pool.wait_ge(self.landed, 16 * len(self.chunks))
        for hi, raw, _ in self.chunks:
            pool.tensor_copy(hi, raw).then_inc(self.rounded, 1)


def mixture_stage(nc, h, ident, a_route, bw, experts, tables):
    with ExitStack() as ctx:
        def sb(name, shape, dt=F32):
            return ctx.enter_context(nc.sbuf_tensor(name, shape, dt))

        def sem(name):
            return ctx.enter_context(nc.semaphore(name))

        ar = Weight(nc, ctx, "mx_ar", a_route).add_high(nc, ctx)
        b = Weight(nc, ctx, "mx_b", bw).add_high(nc, ctx)
        rows = Rows(nc, ctx, "mx", h, ident)
        logits = sb("mx_logits", [P, EXPERTS])
        best = sb("mx_best", [P, 8])
        at = sb("mx_at", [P, 8], mybir.dt.uint32)
        atf = sb("mx_atf", [P, 1])
        weight = sb("mx_weight", [P, EXPERTS])
        numbers = sb("mx_numbers", [P, EXPERTS])
        wh = sb("mx_wh", [P, ER])
        wt_hi = sb("mx_wthi", [P, P], F32R)
        wt_lo = sb("mx_wtlo", [P, P], F32R)
        pj = ctx.enter_context(nc.psum_tensor("mx_pj", [P, BANK], F32))
        wt = ctx.enter_context(nc.psum_tensor("mx_wt", [P, BANK], F32))
        out = ctx.enter_context(nc.psum_tensor("mx_out", [P, 2, BANK], F32))
        numbers_in, pj_done, route = sem("mx_numbers_in"), sem("mx_pj_done"), sem("mx_route")
        wh_done, wt_mm, wthi_done, wtlo_done = sem("mx_wh_done"), sem("mx_wt_mm"), sem("mx_wthi"), sem("mx_wtlo")
        out_mm, added = sem("mx_out_mm"), sem("mx_added")
        prime(nc, rows.sems + [pj_done, route, wh_done, wt_mm, wthi_done, wtlo_done, out_mm, added])
        ROUTE_LINKS = 5

        with nc.Block() as block:

            @block.sync
            def _(sp):
                ar.load(sp)
                sp.dma_start(numbers[:, :], experts).then_inc(numbers_in, 16)
                b.load(sp)
                tables.load(sp)

            @block.gpsimd
            def _(pool):
                tables.round(pool)

            @block.scalar
            def _(act):
                def before():
                    ar.high(act)
                    rows.normalize(act, 0, 0)
                    rows.high(act, 0, 0, pj_done, 0)
                    rows.normalize(act, 0, 1)
                    b.high(act)

                def body(g, i, t, on):
                    if on(1):
                        rows.high(act, t + 1, (i + 1) % 2, pj_done, t)
                    after(act, wt_mm, t + 1)
                    after(act, out_mm, t)
                    act.copy(wt_hi[:, :], wt[:, 0:P]).then_inc(wthi_done, 1)
                    if on(2):
                        rows.normalize(act, g + (i + 2) // GROUP, (i + 2) % GROUP)
                tile_steps(act, before, body, lambda: None)

            @block.vector
            def _(dve):
                def before():
                    rows.stats(dve, 0, range(GROUP))
                    ar.low(dve)
                    rows.low(dve, 0, 0)
                    b.low(dve)
                    dve.wait_ge(numbers_in, 16)

                def route_of(t):
                    after(dve, pj_done, t + 1)
                    link = Links(dve, route, t * ROUTE_LINKS + 1)
                    link(dve.tensor_copy(logits[:, :], pj[:, ER:ROUTED]))
                    dve.memset(rows.dummy[:, :], 0.0)
                    link(dve.max(best[:, :], logits[:, :]))
                    dve.memset(rows.dummy[:, :], 0.0)
                    link(dve.max_index(at[:, :], best[:, :], logits[:, :]))
                    link(dve.tensor_copy(atf[:, :], at[:, 0:1]))
                    link(dve.tensor_scalar(weight[:, :], numbers[:, :], atf[:, :], best[:, 0:1],
                                           ALU.is_equal, ALU.mult))
                    assert link.n == ROUTE_LINKS
                    after(dve, wt_mm, t)
                    dve.tensor_tensor(wh[:, :].rearrange("p (e r) -> p e r", r=RANK),
                                      pj[:, 0:ER].rearrange("p (e r) -> p e r", r=RANK),
                                      weight[:, :].rearrange("p (e a) -> p e a", a=1).to_broadcast([P, EXPERTS, RANK]),
                                      ALU.mult).then_inc(wh_done, 1)

                def add(t):
                    after(dve, out_mm, t + 1)
                    hb = row(h, t)
                    dve.tensor_tensor(hb, hb, out[:, :, :].rearrange("p a n -> p (a n)"), ALU.add).then_inc(added, 1)

                def body(g, i, t, on):
                    route_of(t)
                    if on(1):
                        rows.low(dve, t + 1, (i + 1) % 2)
                    if on(-1):
                        add(t - 1)
                    after(dve, wthi_done, t + 1)
                    dve.tensor_tensor(wt_lo[:, :], wt[:, 0:P], wt_hi[:, :].bitcast(F32), ALU.subtract)\
                       .then_inc(wtlo_done, 1)
                    if i < 2 and on(GROUP):
                        rows.stats(dve, g + 1, (2 * i, 2 * i + 1))
                tile_steps(dve, before, body, lambda: add(NB - 1))

            @block.tensor
            def _(pe):
                def before():
                    rows.turn(pe, 0)
                    ar.ready(pe)
                    b.ready(pe)

                def outputs(t):
                    after(pe, wtlo_done, t + 1)
                    after(pe, added, t)
                    for c in range(2):
                        w = slice(c * BANK, (c + 1) * BANK)
                        pe.matmul(out[:, c, :], wt_hi[:, :], b.hi[:, w], start=True, stop=False)
                        pe.matmul(out[:, c, :], wt_hi[:, :], b.lo[:, w], start=False, stop=False)
                        mm = pe.matmul(out[:, c, :], wt_lo[:, :], b.hi[:, w], start=False, stop=True)
                    mm.then_inc(out_mm, 1)

                def body(g, i, t, on):
                    after(pe, rows.lo_done, t + 1)
                    after(pe, wh_done, t)
                    xh, xl = rows.x_hi[i % 2], rows.x_lo[i % 2]
                    for k in range(KT):
                        w = slice(k * ROUTED, (k + 1) * ROUTED)
                        pe.matmul(pj[:, 0:ROUTED], xh[:, k, :], ar.hi[:, w], start=(k == 0), stop=False)
                        pe.matmul(pj[:, 0:ROUTED], xh[:, k, :], ar.lo[:, w], start=False, stop=False)
                        mm = pe.matmul(pj[:, 0:ROUTED], xl[:, k, :], ar.hi[:, w], start=False, stop=(k == KT - 1))
                    mm.then_inc(pj_done, 1)
                    if on(1):
                        rows.turn(pe, t + 1)
                    if on(-1):
                        outputs(t - 1)
                    after(pe, wh_done, t + 1)
                    after(pe, wtlo_done, t)
                    pe.transpose(wt[:, 0:P], wh[:, :], ident[:, :]).then_inc(wt_mm, 1)
                tile_steps(pe, before, body, lambda: outputs(NB - 1))


TOP_K = 6
HALF = L // 2
NO_WEIGHT = 150.0


def screen(nc, h, ident, tables, rstd, shift, flag, weights):
    with ExitStack() as ctx:
        def sb(name, shape, dt=F32):
            return ctx.enter_context(nc.sbuf_tensor(name, shape, dt))

        def sem(name):
            return ctx.enter_context(nc.semaphore(name))

        f_hi, c_hi = tables.f_hi, tables.c_hi
        xn = [sb(f"sc_xn{i}", [P, L]) for i in range(2)]
        x_hi = [sb(f"sc_xhi{i}", [P, KT, QT], F32R) for i in range(2)]
        squares = [sb(f"sc_sq{i}", [P, 2, BANK]) for i in range(2)]
        power = [sb(f"sc_pw{i}", [P, KT // 2, QT], F32R) for i in range(2)]
        st = sb("sc_st", [P, QB, 2, 6])
        mv = sb("sc_mv", [P, NB, 2])
        var, tmp = sb("sc_var", [P, QB]), sb("sc_tmp", [P, QB])
        top = sb("sc_top", [P, NB])
        lead = sb("sc_lead", [P, NB])
        least = sb("sc_least", [P, 1])
        least_row = sb("sc_least_row", [1, 1])
        tp = ctx.enter_context(nc.psum_tensor("sc_tp", [P, 2, BANK], F32))
        ri = ctx.enter_context(nc.psum_tensor("sc_ri", [P, 2, 2, BANK], F32))
        co = ctx.enter_context(nc.psum_tensor("sc_co", [P, 2, BANK], F32))
        norm, normed, turned, hi_done = sem("sc_norm"), sem("sc_normed"), sem("sc_turned"), sem("sc_hi_done")
        spectrum, squared, powered = sem("sc_spectrum"), sem("sc_squared"), sem("sc_powered")
        corr_mm, topped, leads, least_t = sem("sc_corr_mm"), sem("sc_topped"), sem("sc_leads"), sem("sc_least_t")
        NORM_LINKS = 3 * QB + 1 + RSQRT_LINKS + 1
        FT = KT // 2

        with nc.Block() as block:

            @block.sync
            def _(sp):
                for weight in weights:
                    weight.load(sp)

            @block.vector
            def _(dve):
                def stats(qt):
                    link = Links(dve, norm, qt * NORM_LINKS)
                    these = slice(qt * QB, (qt + 1) * QB)
                    for b in range(QB):
                        for c in range(2):
                            link(dve.bn_stats(st[:, b, c, :], h[:, qt * QB + b, c * BANK:(c + 1) * BANK]))
                    for b in range(QB):
                        link(dve.bn_aggr(mv[:, qt * QB + b, :], st[:, b, :, :]))
                    link(dve.tensor_scalar(var[:, :], mv[:, these, 1], EPS, None, ALU.add))
                    rsqrt(dve, rstd[:, these], var[:, :], tmp[:, :], link)
                    link(dve.scalar_tensor_tensor(out=shift[:, these], in0=mv[:, these, 0], scalar=-1.0,
                                                  in1=rstd[:, these], op0=ALU.mult, op1=ALU.mult))

                def add_power(qt, i):
                    n = qt * FT + i
                    dve.wait_ge(squared, n + 1)
                    if qt >= 2 and i == 0:
                        dve.wait_ge(corr_mm, (qt - 1) * QB)
                    sq = squares[n % 2]
                    dve.tensor_tensor(power[qt % 2][:, i, :], sq[:, 0, :], sq[:, 1, :], ALU.add).then_inc(powered, 1)

                def tops(qt):
                    for b in range(QB):
                        t = qt * QB + b
                        dve.wait_ge(corr_mm, t + 1)
                        dve.tensor_reduce(top[:, t:t + 1], co[:, t % 2, :], AX.X, ALU.max).then_inc(topped, 1)

                stats(0)
                stats(1)
                for qt in range(QUARTERS):
                    add_power(qt, 0)
                    if qt:
                        tops(qt - 1)
                    add_power(qt, 1)
                    if qt + 2 < QUARTERS:
                        stats(qt + 2)
                    for i in range(2, FT):
                        add_power(qt, i)
                tops(QUARTERS - 1)
                link = Links(dve, leads, 0)
                dve.wait_ge(topped, NB)
                link(dve.tensor_tensor(lead[:, :], mv[:, :, 1], rstd[:, :], ALU.mult))
                link(dve.tensor_tensor(lead[:, :], lead[:, :], rstd[:, :], ALU.mult))
                link(dve.scalar_tensor_tensor(out=lead[:, :], in0=lead[:, :], scalar=float(L), in1=top[:, :],
                                              op0=ALU.mult, op1=ALU.subtract))
                link(dve.tensor_reduce(least[:, :], lead[:, :], AX.X, ALU.min))
                dve.wait_ge(least_t, 1)
                link(dve.tensor_reduce(least_row[:, :], tp[0:1, 0, 0:P], AX.X, ALU.min))
                link(dve.tensor_scalar(flag[:, :], least_row[:, :], NO_WEIGHT, None, ALU.is_ge))

            @block.scalar
            def _(act):
                def rows(qt, b):
                    t = qt * QB + b
                    act.wait_ge(norm, (qt + 1) * NORM_LINKS)
                    if t >= 2:
                        act.wait_ge(turned, t - 1)
                    act.activation(xn[t % 2][:, :], h[:, t, :], ACT.Identity,
                                   bias=shift[:, t:t + 1], scale=rstd[:, t:t + 1]).then_inc(normed, 1)

                def high(qt, b):
                    t = qt * QB + b
                    act.wait_ge(turned, t + 1)
                    if qt >= 2 and b == 0:
                        act.wait_ge(spectrum, (qt - 1) * FT)
                    act.copy(x_hi[qt % 2][:, :, b * P:(b + 1) * P],
                             tp[:, :, :].rearrange("p a (k t) -> p (a k) t", t=P)).then_inc(hi_done, 1)

                def square(qt, i):
                    n = qt * FT + i
                    act.wait_ge(spectrum, n + 1)
                    if n >= 2:
                        act.wait_ge(powered, n - 1)
                    act.activation(squares[n % 2][:, :, :], ri[:, n % 2, :, :], ACT.Square).then_inc(squared, 1)

                for b in range(QB):
                    rows(0, b)
                    high(0, b)
                for qt in range(QUARTERS):
                    for i in range(FT):
                        if qt + 1 < QUARTERS:
                            rows(qt + 1, i)
                        square(qt, i)
                        if qt + 1 < QUARTERS:
                            high(qt + 1, i)

            @block.tensor
            def _(pe):
                def turn(qt, b):
                    t = qt * QB + b
                    pe.wait_ge(normed, t + 1)
                    if t:
                        pe.wait_ge(hi_done, t)
                    for k in range(KT):
                        last = pe.transpose(tp[:, k // 4, (k % 4) * P:(k % 4 + 1) * P],
                                            xn[t % 2][:, k * P:(k + 1) * P], ident[:, :])
                    last.then_inc(turned, 1)

                def dft(qt, i):
                    n = qt * FT + i
                    if i == 0:
                        pe.wait_ge(hi_done, (qt + 1) * QB)
                    if n >= 2:
                        pe.wait_ge(squared, n - 1)
                    for part in range(2):
                        at = part * HALF + i * P
                        for k in range(KT):
                            last = pe.matmul(ri[:, n % 2, part, :], f_hi[:, k, at:at + P], x_hi[qt % 2][:, k, :],
                                             start=(k == 0), stop=(k == KT - 1))
                    last.then_inc(spectrum, 1)

                def correlate(qt):
                    pe.wait_ge(powered, (qt + 1) * FT)
                    for b in range(QB):
                        t = qt * QB + b
                        if t >= 2:
                            pe.wait_ge(topped, t - 1)
                        for k in range(FT):
                            last = pe.matmul(co[:, t % 2, :], power[qt % 2][:, k, b * P:(b + 1) * P], c_hi[:, k, :],
                                             start=(k == 0), stop=(k == FT - 1))
                        last.then_inc(corr_mm, 1)

                for b in range(QB):
                    turn(0, b)
                pe.wait_ge(tables.rounded, len(tables.chunks))
                for qt in range(QUARTERS):
                    for i in range(FT):
                        dft(qt, i)
                        if qt + 1 < QUARTERS:
                            turn(qt + 1, i)
                        if i == 0 and qt:
                            correlate(qt - 1)
                correlate(QUARTERS - 1)
                pe.wait_ge(leads, 4)
                pe.transpose(tp[0:1, 0, 0:P], least[:, :], ident[:, :]).then_inc(least_t, 1)


TURNS = (["xn", "x_turned", "xT", "x_dft", "x_spectrum", "re2", "im2", "power", "power_0", "power_512",
          "power_turned", "powerT", "corr_mm", "corr", "best", "at", "at_f", "minus", "exp", "rtotal", "weights",
          "spread_0"] + [f"{what}_{j}" for j in range(1, TOP_K) for what in ("one", "spread")] +
         ["w_turned", "wT", "w_dft", "w_spectrum", "rr", "ii", "re", "ir", "ri", "im", "re_0", "re_512",
          "a_turned", "aT", "agg", "added"])


def delay_average(nc, ctx, h, ident, f_dram, g_dram, lags, rstd, shift):
    def sb(name, shape, dt=F32):
        return ctx.enter_context(nc.sbuf_tensor(name, shape, dt))

    fwd, inv = sb("da_fwd", [P, KT, L]), sb("da_inv", [P, KT, L])
    lag_row = sb("da_lags", [P, L])
    xn, corr, spread, one = (sb(f"da_{n}", [P, L]) for n in ("xn", "corr", "spread", "one"))
    xT = sb("da_xT", [P, KT, P])
    xs, ws, sq, am = (sb(f"da_{n}", [P, 2, HALF]) for n in ("xs", "ws", "sq", "am"))
    power = sb("da_power", [P, KT // 2 + 1, P])
    best, at_f, weights = (sb(f"da_{n}", [P, 8]) for n in ("best", "at_f", "weights"))
    at = sb("da_at", [P, 8], mybir.dt.uint32)
    minus, total, rtotal, dummy = (sb(f"da_{n}", [P, 1]) for n in ("minus", "total", "rtotal", "dummy"))
    tp = ctx.enter_context(nc.psum_tensor("da_tp", [P, KT, P], F32))
    mm = ctx.enter_context(nc.psum_tensor("da_mm", [P, 2, BANK], F32))
    tables = ctx.enter_context(nc.semaphore("da_tables"))
    cleared = ctx.enter_context(nc.semaphore("da_cleared"))
    done = ctx.enter_context(nc.semaphore("da_done"))
    prime(nc, [done])
    S = len(TURNS)
    flat = power[:, :, :].rearrange("p k n -> p (k n)")


    def turn(e, t, name, ins):
        after(e, done, t * S + TURNS.index(name))
        ins().then_inc(done, 1)

    def sync(sp):
        sp.dma_start(fwd[:, :, :].rearrange("p k n -> p (k n)"), f_dram).then_inc(tables, 16)
        sp.dma_start(inv[:, :, :].rearrange("p k n -> p (k n)"), g_dram).then_inc(tables, 16)
        sp.dma_start(lag_row[:, :], lags).then_inc(tables, 16)

    def scalar(act):
        act.wait_ge(cleared, 1)
        with act.Fori(0, NB) as t:
            turn(act, t, "xn", lambda: act.activation(
                xn[:, :], row(h, t), ACT.Identity,
                bias=shift[:, bass.ds(t, 1)], scale=rstd[:, bass.ds(t, 1)]))
            turn(act, t, "xT", lambda: act.copy(xT[:, :, :], tp[:, :, :]))
            turn(act, t, "x_spectrum", lambda: act.copy(xs[:, :, :], mm[:, :, :]))
            turn(act, t, "powerT", lambda: act.copy(xT[:, 0:5, :], tp[:, 0:5, :]))
            turn(act, t, "corr", lambda: act.copy(corr[:, :], mm[:, :, :].rearrange("p a n -> p (a n)")))
            turn(act, t, "exp", lambda: act.activation(
                weights[:, 0:TOP_K], best[:, 0:TOP_K], ACT.Exp, bias=minus[:, :], accum_out=total[:, :]))
            turn(act, t, "wT", lambda: act.copy(xT[:, :, :], tp[:, :, :]))
            turn(act, t, "w_spectrum", lambda: act.copy(ws[:, :, :], mm[:, :, :]))
            turn(act, t, "aT", lambda: act.copy(xT[:, :, :], tp[:, :, :]))

    def vector(dve):
        dve.wait_ge(tables, 48)
        dve.memset(power[:, KT // 2, :], 0.0).then_inc(cleared, 1)
        re, im = slice(0, 1), slice(1, 2)

        def product(out, a, b):
            return lambda: dve.tensor_tensor(out, a, b, ALU.mult)
        with dve.Fori(0, NB) as t:
            turn(dve, t, "re2", product(sq[:, 0, :], xs[:, 0, :], xs[:, 0, :]))
            turn(dve, t, "im2", product(sq[:, 1, :], xs[:, 1, :], xs[:, 1, :]))
            turn(dve, t, "power", lambda: dve.tensor_tensor(flat[:, 0:HALF], sq[:, 0, :], sq[:, 1, :], ALU.add))
            turn(dve, t, "power_0", lambda: dve.tensor_copy(flat[:, 0:1], sq[:, 0, 0:1]))
            turn(dve, t, "power_512", lambda: dve.tensor_copy(flat[:, HALF:HALF + 1], sq[:, 1, 0:1]))
            after(dve, done, t * S + TURNS.index("best"))
            dve.memset(dummy[:, :], 0.0)
            dve.max(best[:, :], corr[:, :]).then_inc(done, 1)
            after(dve, done, t * S + TURNS.index("at"))
            dve.memset(dummy[:, :], 0.0)
            dve.max_index(at[:, :], best[:, :], corr[:, :]).then_inc(done, 1)
            turn(dve, t, "at_f", lambda: dve.tensor_copy(at_f[:, :], at[:, :]))
            turn(dve, t, "minus", lambda: dve.tensor_scalar(minus[:, :], best[:, 0:1], -1.0, None, ALU.mult))
            turn(dve, t, "rtotal", lambda: dve.reciprocal(rtotal[:, :], total[:, :]))
            turn(dve, t, "weights", lambda: dve.tensor_scalar(
                weights[:, 0:TOP_K], weights[:, 0:TOP_K], rtotal[:, :], None, ALU.mult))
            for j in range(TOP_K):
                dst = spread if j == 0 else one
                turn(dve, t, "spread_0" if j == 0 else f"one_{j}", lambda: dve.tensor_scalar(
                    dst[:, :], lag_row[:, :], at_f[:, j:j + 1], weights[:, j:j + 1], ALU.is_equal, ALU.mult))
                if j:
                    turn(dve, t, f"spread_{j}", lambda: dve.tensor_tensor(
                        spread[:, :], spread[:, :], one[:, :], ALU.add))
            turn(dve, t, "rr", product(sq[:, 0, :], xs[:, 0, :], ws[:, 0, :]))
            turn(dve, t, "ii", product(sq[:, 1, :], xs[:, 1, :], ws[:, 1, :]))
            turn(dve, t, "re", lambda: dve.tensor_tensor(am[:, 0, :], sq[:, 0, :], sq[:, 1, :], ALU.add))
            turn(dve, t, "ir", product(sq[:, 0, :], xs[:, 1, :], ws[:, 0, :]))
            turn(dve, t, "ri", product(sq[:, 1, :], xs[:, 0, :], ws[:, 1, :]))
            turn(dve, t, "im", lambda: dve.tensor_tensor(am[:, 1, :], sq[:, 0, :], sq[:, 1, :], ALU.subtract))
            turn(dve, t, "re_0", product(am[:, 0, 0:1], xs[:, 0, 0:1], ws[:, 0, 0:1]))
            turn(dve, t, "re_512", product(am[:, 1, 0:1], xs[:, 1, 0:1], ws[:, 1, 0:1]))
            turn(dve, t, "added", lambda: dve.tensor_tensor(
                row(h, t), row(h, t), mm[:, :, :].rearrange("p a n -> p (a n)"), ALU.add))

    def tensor(pe):
        pe.wait_ge(tables, 48)

        def turned(t, name, src, tiles):
            after(pe, done, t * S + TURNS.index(name))
            for k in range(tiles):
                last = pe.transpose(tp[:, k, :], src[:, k * P:(k + 1) * P], ident[:, :])
            last.then_inc(done, 1)

        def transform(t, name, table, tiles):
            after(pe, done, t * S + TURNS.index(name))
            for c in range(2):
                for k in range(tiles):
                    last = pe.matmul(mm[:, c, :], xT[:, k, :], table[:, k, c * BANK:(c + 1) * BANK],
                                     start=(k == 0), stop=(k == tiles - 1))
            last.then_inc(done, 1)

        with pe.Fori(0, NB) as t:
            turned(t, "x_turned", xn, KT)
            transform(t, "x_dft", fwd, KT)
            turned(t, "power_turned", flat, KT // 2 + 1)
            transform(t, "corr_mm", inv, KT // 2 + 1)
            turned(t, "w_turned", spread, KT)
            transform(t, "w_dft", fwd, KT)
            turned(t, "a_turned", am[:, :, :].rearrange("p a n -> p (a n)"), KT)
            transform(t, "agg", inv, KT)

    return sync, scalar, vector, tensor


def delay_stage(nc, h, ident, f_dram, g_dram, lags, rstd, shift, flag):
    with ExitStack() as ctx:
        def sb(name, shape, dt=F32):
            return ctx.enter_context(nc.sbuf_tensor(name, shape, dt))

        gain = sb("dl_gain", [P, NB])
        gained = ctx.enter_context(nc.semaphore("dl_gained"))
        sync, scalar, vector, tensor = delay_average(nc, ctx, h, ident, f_dram, g_dram, lags, rstd, shift)
        ACT_TILES = 6

        with nc.Block() as block:

            def only_zero(e):
                return e.value_load(flag[0:1, 0:1], min_val=0, max_val=1)

            @block.sync
            def _(sp):
                with sp.If(only_zero(sp) < 1):
                    sync(sp)

            @block.tensor
            def _(pe):
                with pe.If(only_zero(pe) < 1):
                    tensor(pe)

            @block.vector
            def _(dve):
                with dve.If(only_zero(dve) < 1):
                    vector(dve)
                with dve.Else():
                    dve.tensor_scalar(gain[:, :], rstd[:, :], 1.0, None, ALU.add).then_inc(gained, 1)
                    dve.wait_ge(gained, 1)
                    for t in range(ACT_TILES, NB):
                        dve.tensor_scalar(h[:, t, :], h[:, t, :], gain[:, t:t + 1], shift[:, t:t + 1],
                                          ALU.mult, ALU.add)

            @block.scalar
            def _(act):
                with act.If(only_zero(act) < 1):
                    scalar(act)
                with act.Else():
                    act.wait_ge(gained, 1)
                    for t in range(ACT_TILES):
                        act.activation(h[:, t, :], h[:, t, :], ACT.Identity,
                                       bias=shift[:, t:t + 1], scale=gain[:, t:t + 1])


DK = 32
QK = EXPERTS * DK
QKA = 2 * QK + ER


def final_stage(nc, h, ident, w_t, qka, bm, bias, out_dram):
    SC = float(DK) ** -0.5
    with ExitStack() as ctx:
        def sb(name, shape, dt=F32):
            return ctx.enter_context(nc.sbuf_tensor(name, shape, dt))

        def sem(name):
            return ctx.enter_context(nc.semaphore(name))

        w = Weight(nc, ctx, "fn_w", w_t).add_high(nc, ctx)
        qka.add_high(nc, ctx)
        bm.add_high(nc, ctx)
        rows = Rows(nc, ctx, "fn", h, ident)
        bias_row = sb("fn_bias", [P, L])
        q = sb("fn_q", [P, QK])
        qk = sb("fn_qk", [P, QK])
        s8, w8 = sb("fn_s8", [P, EXPERTS]), sb("fn_w8", [P, EXPERTS])
        col = {n: sb(f"fn_{n}", [P, 1]) for n in ("top", "ntop", "total", "rtotal")}
        wh = sb("fn_wh", [P, ER])
        wt_hi, wt_lo = sb("fn_wthi", [P, P], F32R), sb("fn_wtlo", [P, P], F32R)
        ka = ctx.enter_context(nc.psum_tensor("fn_ka", [P, BANK], F32))
        qp = ctx.enter_context(nc.psum_tensor("fn_qp", [P, BANK], F32))
        out = ctx.enter_context(nc.psum_tensor("fn_out", [P, 2, 2, BANK], F32))
        bias_in, ka_done, q_done, gate = sem("fn_bias_in"), sem("fn_ka_done"), sem("fn_q_done"), sem("fn_gate")
        exp_done, biased = sem("fn_exp_done"), sem("fn_biased")
        wh_done, wt_mm, wthi_done, wtlo_done = sem("fn_wh_done"), sem("fn_wt_mm"), sem("fn_wthi"), sem("fn_wtlo")
        out_mm, added = sem("fn_out_mm"), sem("fn_added")
        stored = sem("fn_stored")
        prime(nc, rows.sems + [ka_done, q_done, gate, exp_done, biased, wh_done, wt_mm, wthi_done, wtlo_done, out_mm, added])
        GATE_LINKS = 6

        with nc.Block() as block:

            @block.sync
            def _(sp):
                w.load(sp)
                sp.dma_start(bias_row[:, :], bias).then_inc(bias_in, 16)
                with sp.Fori(0, NB) as t:
                    after(sp, added, t + 1)
                    sp.dma_start(out_dram[bass.ds(t, 1), :, :].rearrange("b p l -> (b p) l"), row(h, t))\
                      .then_inc(stored, 16)
                sp.wait_ge(stored, 16 * NB)

            @block.gpsimd
            def _(pool):
                qka.low(pool)
                w.low(pool, range(KT // 2))
                pool.wait_ge(bias_in, 16)
                with pool.Fori(0, NB) as t:
                    after(pool, rows.normed, t + 1)
                    pool.tensor_tensor(row(h, t), row(h, t), bias_row[:, :], ALU.add).then_inc(biased, 1)

            @block.scalar
            def _(act):
                def before():
                    qka.high(act)
                    rows.normalize(act, 0, 0)
                    rows.high(act, 0, 0, out_mm, 0)
                    rows.normalize(act, 0, 1)
                    w.high(act)
                    bm.high(act)

                def body(g, i, t, on):
                    after(act, q_done, t + 1)
                    after(act, gate, t * GATE_LINKS)
                    act.copy(q[:, :], qp[:, 0:QK]).then_inc(exp_done, 1)
                    if on(1):
                        rows.high(act, t + 1, (i + 1) % 2, out_mm, t)
                    after(act, gate, t * GATE_LINKS + 4)
                    act.activation(s8[:, :], s8[:, :], ACT.Exp, bias=col["ntop"][:, :], scale=SC,
                                   accum_out=col["total"][:, :]).then_inc(exp_done, 1)
                    if on(2):
                        rows.normalize(act, g + (i + 2) // GROUP, (i + 2) % GROUP)
                    after(act, wt_mm, t + 1)
                    act.copy(wt_hi[:, :], qp[:, 0:P]).then_inc(wthi_done, 1)
                tile_steps(act, before, body, lambda: None)

            @block.vector
            def _(dve):
                def before():
                    rows.stats(dve, 0, range(GROUP))
                    rows.low(dve, 0, 0)
                    w.low(dve, range(KT // 2, KT))
                    bm.low(dve)

                def gate_of(t):
                    link = Links(dve, gate, t * GATE_LINKS + 1)
                    after(dve, ka_done, t + 1)
                    after(dve, exp_done, 2 * t + 1)
                    link(dve.tensor_tensor(qk[:, :], ka[:, 0:QK], q[:, :], ALU.mult))
                    link(dve.tensor_reduce(s8[:, :], qk[:, :].rearrange("p (e d) -> p e d", d=DK), AX.X, ALU.add))
                    link(dve.tensor_reduce(col["top"][:, :], s8[:, :], AX.X, ALU.max))
                    link(dve.tensor_scalar(col["ntop"][:, :], col["top"][:, :], -SC, None, ALU.mult))
                    after(dve, exp_done, 2 * t + 2)
                    link(dve.reciprocal(col["rtotal"][:, :], col["total"][:, :]))
                    link(dve.tensor_scalar(w8[:, :], s8[:, :], col["rtotal"][:, :], None, ALU.mult))
                    assert link.n == GATE_LINKS
                    after(dve, wt_mm, t)
                    dve.tensor_tensor(wh[:, :].rearrange("p (e r) -> p e r", r=RANK),
                                      ka[:, QK:QK + ER].rearrange("p (e r) -> p e r", r=RANK),
                                      w8[:, :].rearrange("p (e a) -> p e a", a=1).to_broadcast([P, EXPERTS, RANK]),
                                      ALU.mult).then_inc(wh_done, 1)

                def add(t, par):
                    after(dve, out_mm, t + 1)
                    after(dve, biased, t + 1)
                    hb = row(h, t)
                    dve.tensor_tensor(hb, hb, out[:, par, :, :].rearrange("p a n -> p (a n)"), ALU.add)\
                       .then_inc(added, 1)

                def body(g, i, t, on):
                    gate_of(t)
                    if on(1):
                        rows.low(dve, t + 1, (i + 1) % 2)
                    if i < 2 and on(GROUP):
                        rows.stats(dve, g + 1, (2 * i, 2 * i + 1))
                    after(dve, wthi_done, t + 1)
                    dve.tensor_tensor(wt_lo[:, :], qp[:, 0:P], wt_hi[:, :].bitcast(F32), ALU.subtract)\
                       .then_inc(wtlo_done, 1)
                    add(t, i % 2)
                tile_steps(dve, before, body, lambda: None)

            @block.tensor
            def _(pe):
                def group(par, dst, weight, width, lo, hi, final=True):
                    xh, xl = rows.x_hi[par], rows.x_lo[par]
                    for k in range(KT):
                        cols = slice(k * width + lo, k * width + hi)
                        pe.matmul(dst, xh[:, k, :], weight.hi[:, cols], start=(k == 0), stop=False)
                        pe.matmul(dst, xh[:, k, :], weight.lo[:, cols], start=False, stop=False)
                        mm = pe.matmul(dst, xl[:, k, :], weight.hi[:, cols], start=False,
                                       stop=(final and k == KT - 1))
                    return mm

                def body(g, i, t, on):
                    par = i % 2
                    after(pe, rows.lo_done, t + 1)
                    if early(t, 1):
                        qka.ready(pe)
                    after(pe, wtlo_done, t)
                    group(par, qp[:, 0:QK], qka, QKA, 0, QK).then_inc(q_done, 1)
                    after(pe, wh_done, t)
                    group(par, ka[:, 0:QK + ER], qka, QKA, QK, QKA).then_inc(ka_done, 1)
                    if on(1):
                        rows.turn(pe, t + 1)
                    if early(t, 1):
                        w.ready(pe)
                        bm.ready(pe)
                    else:
                        after(pe, added, t - 1)
                    group(par, out[:, par, 0, :], w, L, 0, BANK, final=False)
                    after(pe, wh_done, t + 1)
                    pe.transpose(qp[:, 0:P], wh[:, :], ident[:, :]).then_inc(wt_mm, 1)
                    group(par, out[:, par, 1, :], w, L, BANK, L, final=False)
                    after(pe, wtlo_done, t + 1)
                    for c in range(2):
                        cols = slice(c * BANK, (c + 1) * BANK)
                        dst = out[:, par, c, :]
                        pe.matmul(dst, wt_hi[:, :], bm.hi[:, cols], start=False, stop=False)
                        pe.matmul(dst, wt_hi[:, :], bm.lo[:, cols], start=False, stop=False)
                        mm = pe.matmul(dst, wt_lo[:, :], bm.hi[:, cols], start=False, stop=True)
                    mm.then_inc(out_mm, 1)
                tile_steps(pe, lambda: rows.turn(pe, 0), body, lambda: None)


def audio_tower(nc, x, conv_w, dw_w, chan, pw_t, w_qkv, w_o, rope, a_route, bw, experts, dft_fwd, dft_inv,
                lag_cos, lags, w_t, qka_t, bm_t, bias, out):
    with ExitStack() as ctx:
        h = ctx.enter_context(nc.sbuf_tensor("h", [P, NB, L], F32))
        ident = ctx.enter_context(nc.sbuf_tensor("ident", [P, P], F32))
        ones_mean = ctx.enter_context(nc.sbuf_tensor("ones_mean", [P, P], F32))
        setup_constants(nc, ctx, ident, ones_mean)
        conv_stage(nc, h, ident, ones_mean, x, conv_w, dw_w, chan, pw_t)
        attention_stage(nc, h, ident, w_qkv, w_o, rope)
        middle_stages(nc, h, ident, (a_route, bw, experts), (dft_fwd, dft_inv, lag_cos, lags),
                      (w_t, qka_t, bm_t, bias), out)


def middle_stages(nc, h, ident, mixture, delay, final, out):
    dft_fwd, dft_inv, lag_cos, lags = delay
    w_t, qka_t, bm_t, bias = final
    with ExitStack() as ctx:
        rstd, shift = (ctx.enter_context(nc.sbuf_tensor(f"dl_{n}", [P, NB], F32)) for n in ("rstd", "shift"))
        flag = ctx.enter_context(nc.sbuf_tensor("dl_flag", [1, 1], I32))
        qka, bm = Weight(nc, ctx, "fn_qka", qka_t), Weight(nc, ctx, "fn_bm", bm_t)
        with ExitStack() as inner:
            tables = ScreenTables(nc, inner, dft_fwd, lag_cos)
            mixture_stage(nc, h, ident, *mixture, tables)
            screen(nc, h, ident, tables, rstd, shift, flag, (qka, bm))
        delay_stage(nc, h, ident, dft_fwd, dft_inv, lags, rstd, shift, flag)
        final_stage(nc, h, ident, w_t, qka, bm, bias, out)


def _layout(a):
    import numpy as np

    def flat(m):
        return np.ascontiguousarray(m)

    def moving(w):
        return flat(w.reshape(w.shape[0], KT, P).transpose(2, 1, 0).reshape(P, KT * w.shape[0]))

    def head_tiles(w):
        n = w.shape[0] // P
        return w.reshape(n, P, KT, P).transpose(0, 3, 2, 1).reshape(n, P, L)

    def packed(m):
        return flat(m.reshape(-1, P, m.shape[1]).transpose(1, 0, 2).reshape(P, -1).astype(np.float32))

    taps = np.zeros((P, C_IN, 2 * PAIRS), np.float32)
    taps[:, :, :TAPS] = a["L0_tok_conv_in_w"]
    q = head_tiles(a["L0_attn_Wq"]).reshape(KV, HEADS, P, L)
    k, v = (head_tiles(a[f"L0_attn_{n}"])[:, None] for n in ("Wk", "Wv"))
    inv_freq = (1.0 / np.power(np.float32(500000.0), np.arange(0, D, 2, dtype=np.float32) / np.float32(D)))
    angle = np.arange(P, dtype=np.float32)[:, None] * inv_freq.astype(np.float32)[None]
    angle = np.concatenate([angle, angle], 1).astype(np.float64).T
    turn = np.sin(angle)
    turn[D // 2:] *= -1.0
    n = np.arange(L)
    w = 2 * np.pi * (n[:, None] * n[None, :] % L) / L
    cos, sin = np.cos(w), np.sin(w)
    fwd = np.concatenate([cos[:, :HALF], cos[:, HALF:HALF + 1], -sin[:, 1:HALF]], 1)
    twice = np.where(n[:HALF, None] == 0, 1.0, 2.0)
    inv = np.concatenate([cos[:HALF] * twice, cos[HALF:HALF + 1], -2 * sin[1:HALF]], 0) / L

    def all_rows(r):
        return flat(np.broadcast_to(r, (P, r.shape[0])))

    return {
        "x": flat(a["x"]),
        "conv_w": flat(taps.reshape(P, C_IN, PAIRS, 2).transpose(3, 1, 2, 0).reshape(P, PAIRS * P)),
        "dw_w": flat(a["L0_tok_dw_w"].reshape(P, DW)),
        "chan": flat(np.stack([a[f"L0_tok_{m}"] for m in ("dw_b", "gn1_w", "gn1_b", "gn2_w", "gn2_b")], 1)),
        "pw_t": flat(a["L0_tok_pw_w"][:, :, 0].T),
        "w_qkv": flat(np.concatenate([k, v, q], 1)),
        "w_o": flat(a["L0_attn_Wo"].T.reshape(KV, HEADS, D, L)),
        "rope": flat(np.stack([np.cos(angle), turn], 1).astype(np.float32)),
        "a_route": moving(np.concatenate([a["L0_ffn_A"].reshape(ER, L), a["L0_ffn_route_w"]], 0)),
        "bw": flat(a["L0_ffn_Bw"].transpose(0, 2, 1).reshape(ER, L)),
        "experts": all_rows(np.arange(EXPERTS, dtype=np.float32)),
        "dft_fwd": packed(fwd),
        "dft_inv": packed(inv),
        "lag_cos": packed(inv[:HALF, 1:HALF + 1]),
        "lags": all_rows(np.arange(L, dtype=np.float32)),
        "w_t": moving(a["L1_ffn_W"]),
        "qka_t": moving(np.concatenate([a["L1_ffn_Wq"], a["L1_ffn_Wk"], a["L1_ffn_A"].reshape(ER, L)], 0)),
        "bm_t": flat(a["L1_ffn_Bm"].transpose(0, 2, 1).reshape(ER, L)),
        "bias": all_rows(a["L1_ffn_b"]),
    }


def kernel(**inputs):
    import numpy as _np
    import concourse.bacc as _bacc
    from concourse import mybir as _mybir
    from concourse.bass_utils import run_bass_kernel_spmd as _run

    nc = _bacc.Bacc("TRN2", target_bir_lowering=False, num_devices=1)
    arrays, args = {}, []
    for name, a in _layout({k: _np.asarray(v) for k, v in inputs.items()}).items():
        arrays[f"in_{name}_dram"] = a
        args.append(nc.dram_tensor(f"in_{name}_dram", a.shape, _mybir.dt.from_np(a.dtype), kind="ExternalInput").ap())
    out = nc.dram_tensor("out_dram", (NB, P, L), _mybir.dt.float32, kind="ExternalOutput").ap()
    audio_tower(nc, *args, out)
    r = _run(nc, [arrays], core_ids=[0])
    return r.results[0]["out_dram"]
```

```python
from contextlib import ExitStack

import concourse.bass as bass
from concourse import mybir

F32 = mybir.dt.float32
F32R = mybir.dt.float32r
I32 = mybir.dt.int32
ALU = mybir.AluOpType
ACT = mybir.ActivationFunctionType
AX = mybir.AxisListType

P = 128
NB = 16
C_IN = 64
T_IN = 2048
L = 1024
KT = L // P
BANK = 512
EPS = 1e-5
TAPS, PAD = 7, 3
PAIRS = (TAPS + 1) // 2
DW, DW_PAD = 5, 2
RSQRT_SEED = 0x5F3759DF
NEWTON = 3
RSQRT_LINKS = 3 + NEWTON * 3


class Links:

    def __init__(self, engine, sem, base):
        self.engine, self.sem, self.base, self.n = engine, sem, base, 0

    def __call__(self, ins):
        self.n += 1
        ins.then_inc(self.sem, 1)
        self.engine.wait_ge(self.sem, self.base + self.n)


def rsqrt(e, y, v, t, link):
    link(e.tensor_scalar(t.bitcast(I32), v.bitcast(I32), 1, None, ALU.logical_shift_right))
    link(e.tensor_scalar(y.bitcast(I32), t.bitcast(I32), -1.0, float(RSQRT_SEED), ALU.mult, ALU.add))
    link(e.tensor_scalar(v, v, -0.5, None, ALU.mult))
    for _ in range(NEWTON):
        link(e.tensor_tensor(t, y, y, ALU.mult))
        link(e.tensor_tensor(t, t, v, ALU.mult))
        link(e.scalar_tensor_tensor(out=y, in0=t, scalar=1.5, in1=y, op0=ALU.add, op1=ALU.mult))


def row(ap3, i):
    return ap3[:, bass.ds(i, 1), :].rearrange("p a n -> p (a n)")


def landing(nc, ctx, name, shape):
    with nc.sbuf_tensor(f"{name}_raw", shape, F32) as raw:
        pass
    return raw, ctx.enter_context(nc.sbuf_tensor(name, shape, F32R))


def early(i, n):
    return isinstance(i, int) and i < n


def prime(nc, sems):
    with nc.Block() as block:

        @block.sync
        def _(sp):
            for s in sems:
                sp.sem_inc(s, 1)


def after(engine, sem, count):
    if not early(count, 1):
        engine.wait_ge(sem, count + 1)


def setup_constants(nc, ctx, ident, ones_mean):
    filled = ctx.enter_context(nc.semaphore("const_filled"))
    with nc.Block() as block:

        @block.gpsimd
        def _(pool):
            pool.memset(ident[:, :], 1.0).then_inc(filled, 1)
            pool.memset(ones_mean[:, :], 1.0 / P)
            pool.wait_ge(filled, 1)
            pool.affine_select(out=ident[:, :], in_=ident[:, :], compare_op=ALU.is_equal, fill=0.0,
                               base=0, pattern=[[-1, P]], channel_multiplier=1).then_inc(filled, 1)
            pool.wait_ge(filled, 2)


HEADS = 4
KV = 8
D = 128
QUARTERS = 4
QB = NB // QUARTERS
QT = QB * P
TILES = 2 + HEADS
SCALE = float(D) ** -0.5


class WeightStage:

    def __init__(self, nc, ctx, w_qkv):
        self.w_qkv = w_qkv
        self.buffers = [ctx.enter_context(nc.sbuf_tensor(f"at_wstage{i}", [P, L], F32)) for i in range(2)]
        self.landed = [ctx.enter_context(nc.semaphore(f"at_w_staged{i}")) for i in range(2)]

    def load(self, sp, g, j):
        src = self.w_qkv[bass.ds(g, 1), j, :, :].rearrange("a p n -> (a p) n")
        sp.dma_start(self.buffers[j % 2][:, :], src).then_inc(self.landed[j % 2], 16)


class QuarterRows:

    LINKS = 3 * QB + 1 + RSQRT_LINKS + 1
    UNITS = 2 * QB

    def __init__(self, nc, ctx, h, ident):
        def sb(n, shape, dt=F32):
            return ctx.enter_context(nc.sbuf_tensor(f"qr_{n}", shape, dt))

        def sem(n):
            return ctx.enter_context(nc.semaphore(f"qr_{n}"))

        self.h, self.ident = h, ident
        self.x_hi, self.x_lo = (sb(n, [P, KT, QT], F32R) for n in ("xhi", "xlo"))
        self.xn = [sb(f"xn{i}", [P, L]) for i in range(2)]
        self.st, self.mv = sb("st", [P, QB, 2, 6]), sb("mv", [P, QB, 2])
        self.var, self.tmp, self.root, self.rstd, self.shift = (
            sb(n, [P, QB]) for n in ("var", "tmp", "root", "rstd", "shift"))
        self.dummy = sb("dummy", [P, 1])
        self.norm = sem("norm")
        self.normed = sem("normed")
        self.turned = sem("turned")
        self.hi_done, self.lo_done = sem("xhi_done"), sem("xlo_done")
        prime(nc, [self.norm, self.normed, self.turned, self.hi_done, self.lo_done])

    def stats(self, dve, qt, link, b):
        for c in range(2):
            link(dve.bn_stats(self.st[:, b, c, :], row(self.h, qt * QB + b)[:, c * BANK:(c + 1) * BANK]))

    def coefficients(self, dve, link):
        for b in range(QB):
            dve.memset(self.dummy[:, :], 0.0)
            link(dve.bn_aggr(self.mv[:, b, :], self.st[:, b, :, :]))
        link(dve.tensor_scalar(self.var[:, :], self.mv[:, :, 1], EPS, None, ALU.add))
        rsqrt(dve, self.root[:, :], self.var[:, :], self.tmp[:, :], link)

    def keep(self, dve, link, rstd, shift):
        dve.tensor_scalar(rstd, self.root[:, :], 1.0, None, ALU.mult)
        link(dve.scalar_tensor_tensor(out=shift, in0=self.mv[:, :, 0], scalar=-1.0, in1=self.root[:, :],
                                      op0=ALU.mult, op1=ALU.mult))
        assert link.n == self.LINKS

    def normalize(self, act, qt, b):
        after(act, self.norm, (qt + 1) * self.LINKS)
        if b >= 2:
            after(act, self.turned, qt * self.UNITS + 2 * b - 2)
        act.activation(self.xn[b % 2][:, :], row(self.h, qt * QB + b), ACT.Identity,
                       bias=self.shift[:, b:b + 1], scale=self.rstd[:, b:b + 1]).then_inc(self.normed, 1)

    def turn(self, pe, qt, banks, *batches):
        for b in batches:
            after(pe, self.normed, qt * QB + b + 1)
            for c in range(2):
                if b > 0:
                    after(pe, self.lo_done, qt * self.UNITS + 2 * b + c - 1)
                for k in range(KT // 2):
                    at = (c * KT // 2 + k) * P
                    last = pe.transpose(banks[:, c, k * P:(k + 1) * P], self.xn[b % 2][:, at:at + P],
                                        self.ident[:, :])
                last.then_inc(self.turned, 1)

    def high(self, act, qt, banks, b):
        for c in range(2):
            after(act, self.turned, qt * self.UNITS + 2 * b + c + 1)
            act.copy(self.x_hi[:, c * KT // 2:(c + 1) * KT // 2, b * P:(b + 1) * P],
                     banks[:, c, :].rearrange("p (k t) -> p k t", t=P)).then_inc(self.hi_done, 1)

    def low(self, dve, qt, banks, b):
        for c in range(2):
            after(dve, self.hi_done, qt * self.UNITS + 2 * b + c + 1)
            tiles, cols = slice(c * KT // 2, (c + 1) * KT // 2), slice(b * P, (b + 1) * P)
            dve.tensor_tensor(self.x_lo[:, tiles, cols], banks[:, c, :].rearrange("p (k t) -> p k t", t=P),
                              self.x_hi[:, tiles, cols].bitcast(F32), ALU.subtract).then_inc(self.lo_done, 1)


def conv_stage(nc, h, ident, ones_mean, x, conv_w, dw_w, chan, pw_wT, rows, w_stage):
    XW = T_IN + 2 * PAD + 2
    GW = T_IN + 2 * DW_PAD
    NCH = T_IN // BANK
    T2 = T_IN // 2
    LAST = NB + 3
    with ExitStack() as ctx:
        def sb(name, shape, dt=F32):
            return ctx.enter_context(nc.sbuf_tensor(name, shape, dt))

        def sem(name):
            return ctx.enter_context(nc.semaphore(name))

        x_in = [sb(f"cv_x{i}", [P, XW]) for i in range(2)]
        x_hi = [sb(f"cv_xhi{i}", [P, XW], F32R) for i in range(2)]
        x_lo = [sb(f"cv_xlo{i}", [P, XW], F32R) for i in range(2)]
        raw = [sb(f"cv_raw{i}", [P, T_IN]) for i in range(2)]
        g = sb("cv_g", [P, GW])
        tap_0 = sb("cv_tap0", [P, T2])
        y = sb("cv_y", [P, T2])
        y_hi = sb("cv_yhi", [P, T2], F32R)
        y_lo = sb("cv_ylo", [P, T2], F32R)
        cw_hi = sb("cv_whi", [P, PAIRS * P], F32R)
        cw, cw_lo = landing(nc, ctx, "cv_wlo", [P, PAIRS * P])
        pw_hi = sb("cv_pwhi", [P, P], F32R)
        pw, pw_lo = landing(nc, ctx, "cv_pwlo", [P, P])
        dww = sb("cv_dww", [P, DW])
        ch = sb("cv_ch", [P, 5])
        dummy = sb("cv_dummy", [P, 1])
        carrier = sb("cv_carrier", [P, 1])
        st = [sb(f"cv_st{n}", [P, 4, 6]) for n in range(2)]
        mv = sb("cv_mv", [P, 2, 2])
        mean, dev, var, tmp, rstd, scale, shift = (
            sb(f"cv_{n}", [P, 2]) for n in ("mean", "dev", "var", "tmp", "rstd", "scale", "shift"))
        cp = ctx.enter_context(nc.psum_tensor("cv_cp", [P, NCH, BANK], F32))
        pp = ctx.enter_context(nc.psum_tensor("cv_pp", [P, 2, BANK], F32))
        sp = ctx.enter_context(nc.psum_tensor("cv_sp", [P, BANK], F32))

        w_loaded, pads, w_hi_done, w_lo_done = sem("cv_w_loaded"), sem("cv_pads"), sem("cv_whi_d"), sem("cv_wlo_d")
        x_loaded = [sem(f"cv_x_loaded{i}") for i in range(2)]
        xhi_done, xlo_done = sem("cv_xhi_done"), sem("cv_xlo_done")
        conv_done, raw_done = sem("cv_conv_done"), sem("cv_raw_done")
        head_done = [sem(f"cv_head_done{n}") for n in range(2)]
        chain = sem("cv_chain")
        mean_mm = sem("cv_mean_mm")
        coef = sem("cv_coef")
        gelu1, tap_done, dw_acc = sem("cv_gelu1"), sem("cv_tap_done"), sem("cv_dw_acc")
        yhi_done, ylo_done = sem("cv_yhi"), sem("cv_ylo")
        pw_done, gelu2 = sem("cv_pw_done"), sem("cv_gelu2")

        HEAD_LINKS = 2
        MIDDLE_LINKS = 3
        CHAIN_LINKS = MIDDLE_LINKS + 1 + RSQRT_LINKS + 2
        DW_LINKS = DW - 1

        def from_end(it):
            return LAST - it if isinstance(it, int) else 0

        def steps(e, body):
            def peeled(it):
                body(it, it % 2, lambda k: 0 <= it - k < NB)
            for it in range(4):
                peeled(it)
            with e.Fori(2, NB // 2 - 1) as pair:
                body(pair * 2, 0, lambda k: True)
                body(pair * 2 + 1, 1, lambda k: True)
            for it in range(NB - 2, LAST):
                peeled(it)

        gv = g[:, :].rearrange("p (t s) -> p t s", s=2)

        with nc.Block() as block:

            @block.sync
            def _(sp_):
                for dst, src in ((cw, conv_w), (pw, pw_wT), (dww, dw_w), (ch, chan)):
                    sp_.dma_start(dst[:, :], src).then_inc(w_loaded, 16)
                sp_.wait_ge(pads, 1)

                def body(it, par, on):
                    if not on(0):
                        return
                    if not early(it, 2):
                        sp_.wait_ge(xlo_done, it - 1)
                    src = x[bass.ds(it, 1), :, :].rearrange("b c t -> (b c) t")
                    sp_.dma_start(x_in[par][0:C_IN, PAD:PAD + T_IN], src).then_inc(x_loaded[par], 16)
                    sp_.dma_start(x_in[par][C_IN:P, PAD - 1:PAD - 1 + T_IN], src).then_inc(x_loaded[par], 16)
                steps(sp_, body)
                w_stage.load(sp_, 0, 0)
                w_stage.load(sp_, 0, 1)

            @block.gpsimd
            def _(pool):
                for par in range(2):
                    pool.memset(x_in[par][:, 0:PAD], 0.0)
                    pool.memset(x_in[par][:, XW - PAD - 3:XW], 0.0)
                pool.memset(g[:, 0:DW_PAD], 0.0)
                pool.memset(g[:, GW - DW_PAD:GW], 0.0).then_inc(pads, 1)

                def split_in(i, par):
                    pool.wait_ge(xhi_done, i + 1)
                    if not early(i, 2):
                        pool.wait_ge(conv_done, (i - 1) * NCH)
                    pool.tensor_tensor(x_lo[par][:, :], x_in[par][:, :], x_hi[par][:, :].bitcast(F32),
                                       ALU.subtract).then_inc(xlo_done, 1)

                def body(it, par, on):
                    if early(it, 1):
                        split_in(0, 0)
                    if on(-1):
                        split_in(it + 1, 1 - par)
                    if on(2):
                        pool.wait_ge(yhi_done, it - 1)
                        if not early(it, 3):
                            pool.wait_ge(pw_done, it - 2)
                        pool.tensor_tensor(y_lo[:, :], y[:, :], y_hi[:, :].bitcast(F32),
                                           ALU.subtract).then_inc(ylo_done, 1)
                    if on(1):
                        pool.wait_ge(gelu1, it)
                        if not early(it, 2):
                            pool.wait_ge(dw_acc, (it - 1) * DW_LINKS)
                        pool.tensor_tensor(carrier[:, :], ch[:, 0:1], ch[:, 0:1], ALU.add)
                        pool.tensor_scalar(tap_0[:, :], gv[:, 0:T2, 0], dww[:, 0:1], ch[:, 0:1],
                                           ALU.mult, ALU.add).then_inc(tap_done, 1)
                steps(pool, body)

            @block.scalar
            def _(act):
                act.wait_ge(w_loaded, 64)
                act.copy(cw_hi[:, :], cw[:, :])
                act.copy(pw_hi[:, :], pw[:, :]).then_inc(w_hi_done, 1)

                def split_in(i, par):
                    act.wait_ge(x_loaded[par], (i // 2 + 1) * 32)
                    if not early(i, 2):
                        act.wait_ge(conv_done, (i - 1) * NCH)
                    act.copy(x_hi[par][:, :], x_in[par][:, :]).then_inc(xhi_done, 1)

                def body(it, par, on):
                    if early(it, 1):
                        act.wait_ge(pads, 1)
                        split_in(0, 0)

                    def evacuate(c):
                        act.wait_ge(conv_done, it * NCH + c + 1)
                        if c == 0 and not early(it, 2):
                            act.wait_ge(gelu1, it - 1)
                        act.copy(raw[par][:, c * BANK:(c + 1) * BANK], cp[:, c, :]).then_inc(raw_done, 1)

                    if on(0):
                        evacuate(0)
                    if on(-1):
                        split_in(it + 1, 1 - par)
                    if on(0):
                        for c in range(1, NCH - 1):
                            evacuate(c)
                    if on(2):
                        act.wait_ge(dw_acc, (it - 1) * DW_LINKS)
                        if not early(it, 3):
                            act.wait_ge(pw_done, it - 2)
                        act.copy(y_hi[:, :], y[:, :]).then_inc(yhi_done, 1)
                    if on(0):
                        evacuate(NCH - 1)
                    if from_end(it) == 1:
                        rows.high(act, 0, cp, 0)
                        rows.normalize(act, 0, 2)
                        rows.high(act, 0, cp, 1)
                        rows.normalize(act, 0, 3)
                        rows.high(act, 0, cp, 2)
                    if on(1) or on(3):
                        act.wait_ge(coef, it)
                    if on(3):
                        act.activation(row(h, it - 3), pp[:, :, :], ACT.Gelu,
                                       bias=shift[:, 1:2], scale=scale[:, 1:2]).then_inc(gelu2, 1)
                    if from_end(it) == 2:
                        rows.normalize(act, 0, 0)
                        rows.normalize(act, 0, 1)
                    if from_end(it) == 1:
                        rows.high(act, 0, cp, 3)
                    if on(1):
                        act.activation(g[:, DW_PAD:DW_PAD + T_IN], raw[1 - par][:, :], ACT.Gelu,
                                       bias=shift[:, 0:1], scale=scale[:, 0:1]).then_inc(gelu1, 1)
                steps(act, body)

            @block.vector
            def _(dve):
                dve.wait_ge(w_hi_done, 1)
                dve.tensor_tensor(cw_lo[:, :], cw[:, :], cw_hi[:, :].bitcast(F32), ALU.subtract)
                dve.tensor_tensor(pw_lo[:, :], pw[:, :], pw_hi[:, :].bitcast(F32), ALU.subtract).then_inc(w_lo_done, 1)

                dve.memset(mv[:, :, :], 0.0)

                def head(n, i, chunks):
                    link = Links(dve, head_done[n], i * HEAD_LINKS)
                    for c, src in enumerate(chunks):
                        if n == 0:
                            dve.wait_ge(raw_done, i * NCH + c + 1)
                        last = dve.bn_stats(st[n][:, c, :], src)
                    link(last)
                    dve.memset(dummy[:, :], 0.0)
                    link(dve.bn_aggr(mv[:, n, :], st[n][:, 0:len(chunks), :]))
                    assert link.n == HEAD_LINKS

                def middle(it):
                    link = Links(dve, chain, (it - 1) * CHAIN_LINKS)
                    dve.wait_ge(mean_mm, 2 * it - 1)
                    dve.tensor_copy(mean[:, :], sp[:, 0:2])
                    link(dve.tensor_tensor(dev[:, :], mv[:, :, 0], sp[:, 0:2], ALU.subtract))
                    link(dve.tensor_tensor(dev[:, :], dev[:, :], dev[:, :], ALU.mult))
                    link(dve.tensor_tensor(dev[:, :], dev[:, :], mv[:, :, 1], ALU.add))
                    assert link.n == MIDDLE_LINKS

                def tail(it):
                    link = Links(dve, chain, (it - 1) * CHAIN_LINKS + MIDDLE_LINKS)
                    gamma_beta = ch[:, 1:5].rearrange("p (n c) -> p n c", c=2)
                    dve.wait_ge(mean_mm, 2 * it)
                    link(dve.tensor_scalar(var[:, :], sp[:, 0:2], EPS, None, ALU.add))
                    rsqrt(dve, rstd[:, :], var[:, :], tmp[:, :], link)
                    link(dve.tensor_tensor(scale[:, :], gamma_beta[:, :, 0], rstd[:, :], ALU.mult))
                    link(dve.tensor_tensor(tmp[:, :], mean[:, :], scale[:, :], ALU.mult))
                    assert link.n == CHAIN_LINKS - MIDDLE_LINKS
                    dve.tensor_tensor(shift[:, :], gamma_beta[:, :, 1], tmp[:, :], ALU.subtract).then_inc(coef, 1)

                def taps(i, which):
                    link = Links(dve, dw_acc, i * DW_LINKS + which[0] - 1)
                    if which[0] == 1:
                        dve.wait_ge(tap_done, i + 1)
                        if not early(i, 1):
                            dve.wait_ge(ylo_done, i)
                    for k in which:
                        link(dve.scalar_tensor_tensor(out=y[:, :], in0=gv[:, k // 2:k // 2 + T2, k % 2],
                                                      scalar=dww[:, k:k + 1], in1=(tap_0 if k == 1 else y)[:, :],
                                                      op0=ALU.mult, op1=ALU.add))

                def body(it, par, on):
                    if on(1):
                        head(0, it - 1, [raw[1 - par][:, c * BANK:(c + 1) * BANK] for c in range(NCH)])
                    if on(3):
                        dve.wait_ge(pw_done, it - 2)
                        head(1, it - 3, [pp[:, c, :] for c in range(2)])
                    if on(2):
                        taps(it - 2, (1, 2))
                    last = from_end(it) == 1
                    if last:
                        rows.low(dve, 0, cp, 0)
                    if not early(it, 1):
                        middle(it)
                    if on(2):
                        taps(it - 2, (3, 4))
                    if last:
                        rows.low(dve, 0, cp, 1)
                        rows.low(dve, 0, cp, 2)
                    if not early(it, 1):
                        tail(it)
                    if from_end(it) == 3:
                        dve.wait_ge(gelu2, QB)
                        for b in range(QB):
                            rows.stats(dve, 0, rows_link, b)
                    if from_end(it) == 2:
                        rows.coefficients(dve, rows_link)
                        rows.keep(dve, rows_link, rows.rstd[:, :], rows.shift[:, :])
                    if last:
                        rows.low(dve, 0, cp, 3)
                rows_link = Links(dve, rows.norm, 1)
                steps(dve, body)

            @block.tensor
            def _(pe):
                pe.wait_ge(w_lo_done, 1)

                def conv(i, par, c):
                    if not early(i, 1):
                        pe.wait_ge(raw_done, (i - 1) * NCH + c + 1)
                    if c == 0:
                        pe.wait_ge(xhi_done, i + 1)
                    for q in range(PAIRS):
                        w = slice(q * P, (q + 1) * P)
                        cols = slice(c * BANK + 2 * q, (c + 1) * BANK + 2 * q)
                        pe.matmul(cp[:, c, :], cw_hi[:, w], x_hi[par][:, cols], start=(q == 0), stop=False)
                        pe.matmul(cp[:, c, :], cw_lo[:, w], x_hi[par][:, cols], start=False, stop=False)
                    if c == 0:
                        pe.wait_ge(xlo_done, i + 1)
                    for q in range(PAIRS):
                        w = slice(q * P, (q + 1) * P)
                        cols = slice(c * BANK + 2 * q, (c + 1) * BANK + 2 * q)
                        last = pe.matmul(cp[:, c, :], cw_hi[:, w], x_lo[par][:, cols], start=False,
                                         stop=(q == PAIRS - 1))
                    last.then_inc(conv_done, 1)

                def average(it, on, which):
                    if early(it, 1):
                        return
                    if which == 0:
                        if on(1):
                            pe.wait_ge(head_done[0], it * HEAD_LINKS)
                        if on(3):
                            pe.wait_ge(head_done[1], (it - 2) * HEAD_LINKS)
                        if not early(it, 2):
                            pe.wait_ge(chain, (it - 1) * CHAIN_LINKS)
                    else:
                        pe.wait_ge(chain, (it - 1) * CHAIN_LINKS + MIDDLE_LINKS)
                    src = mv[:, :, 0] if which == 0 else dev[:, :]
                    pe.matmul(sp[:, 0:2], ones_mean[:, :], src, start=True, stop=True).then_inc(mean_mm, 1)

                def pointwise(i):
                    pe.wait_ge(ylo_done, i + 1)
                    if not early(i, 1):
                        pe.wait_ge(gelu2, i)
                    for c in range(2):
                        cols = slice(c * BANK, (c + 1) * BANK)
                        pe.matmul(pp[:, c, :], pw_hi[:, :], y_hi[:, cols], start=True, stop=False)
                        pe.matmul(pp[:, c, :], pw_hi[:, :], y_lo[:, cols], start=False, stop=False)
                        last = pe.matmul(pp[:, c, :], pw_lo[:, :], y_hi[:, cols], start=False, stop=True)
                    last.then_inc(pw_done, 1)

                def body(it, par, on):
                    last = from_end(it) == 1
                    if on(0):
                        conv(it, par, 0)
                    if on(3):
                        pointwise(it - 3)
                    if last:
                        pe.wait_ge(raw_done, NB * NCH)
                        rows.turn(pe, 0, cp, 0)
                    if on(0):
                        conv(it, par, 1)
                    average(it, on, 0)
                    if on(0):
                        conv(it, par, 2)
                    if last:
                        rows.turn(pe, 0, cp, 1)
                        rows.turn(pe, 0, cp, 2)
                    average(it, on, 1)
                    if on(0):
                        conv(it, par, 3)
                    if last:
                        rows.turn(pe, 0, cp, 3)
                steps(pe, body)


def attention_stage(nc, h, ident, w_o, rope, rows, w_stage, next_rstd, next_shift):
    ROPED = TILES - 1
    with ExitStack() as ctx:
        def sb(name, shape, dt=F32):
            return ctx.enter_context(nc.sbuf_tensor(name, shape, dt))

        def sem(name):
            return ctx.enter_context(nc.semaphore(name))

        def psum(name):
            return ctx.enter_context(nc.psum_tensor(name, [P, BANK], F32))

        x_hi, x_lo = rows.x_hi, rows.x_lo
        o_stage = [sb(f"at_ostage{i}", [P, L]) for i in range(2)]
        w_hi = [sb(f"at_whi{i}", [P, L], F32R) for i in range(2)]
        w_lo = [sb(f"at_wlo{i}", [P, L], F32R) for i in range(2)]
        wo_hi = sb("at_wohi", [P, HEADS, L], F32R)
        wo_lo = sb("at_wolo", [P, HEADS, L], F32R)
        qT = [sb(f"at_q{i}", [P, HEADS, QT]) for i in range(2)]
        kT = [sb(f"at_k{i}", [P, QT]) for i in range(2)]
        vT = sb("at_vT", [P, QT])
        v = [sb(f"at_v{i}", [P, QB, D]) for i in range(2)]
        probs = sb("at_probs", [P, HEADS, P])
        pT = sb("at_pT", [P, HEADS * P])
        o_hi = sb("at_ohi", [P, HEADS * P], F32R)
        o_lo = sb("at_olo", [P, HEADS * P], F32R)
        cs = sb("at_cs", [P, 2, P])
        turned = sb("at_turned", [P, QT])
        top = sb("at_top", [P, HEADS])
        ntop = sb("at_ntop", [P, HEADS])
        total = sb("at_total", [P, HEADS])
        rtotal = sb("at_rtotal", [P, HEADS])
        proj = ctx.enter_context(nc.psum_tensor("at_proj", [P, 2, BANK], F32))
        sc = [psum(f"at_sc{i}") for i in range(2)]
        tp = psum("at_tp")
        ov = psum("at_ov")
        out = ctx.enter_context(nc.psum_tensor("at_out", [P, 2, BANK], F32))

        rope_in = sem("at_rope_in")
        o_staged = [sem(f"at_o_staged{i}") for i in range(2)]
        whi_done, wlo_done = sem("at_whi_done"), sem("at_wlo_done")
        wohi_done, wolo_done = sem("at_wohi_done"), sem("at_wolo_done")
        wolo_dve = sem("at_wolo_dve")
        ahead = sem("at_ahead")
        proj_done, roped, vT_done = sem("at_proj_done"), sem("at_roped"), sem("at_vT_done")
        rope_mul = sem("at_rope_mul")
        v_turned, v_done = sem("at_v_turned"), sem("at_v_done")
        sc_done, top_done, ntop_done = sem("at_sc_done"), sem("at_top_done"), sem("at_ntop_done")
        exp_done, rtotal_done, probs_done = sem("at_exp_done"), sem("at_rtotal_done"), sem("at_probs_done")
        pT_mm, pT_done, ov_mm = sem("at_pT_mm"), sem("at_pT_done"), sem("at_ov_mm")
        ohi_done, olo_done = sem("at_ohi_done"), sem("at_olo_done")
        out_mm, added = sem("at_out_mm"), sem("at_added")

        prime(nc, [whi_done, wlo_done, wohi_done, wolo_done, ahead,
                   proj_done, roped, vT_done, rope_mul, v_turned, v_done, sc_done, top_done, ntop_done, exp_done,
                   rtotal_done, probs_done, pT_mm, pT_done, ov_mm, ohi_done, olo_done, out_mm, added])

        def steps(e, first, step):
            first()
            step(0, -1, 1, False, 2, False)

            def quarter(qt, more):
                with e.Fori(0, KV // 2 - 1) as pair:
                    step(qt, pair * 2, 0, True, 2, False)
                    step(qt, pair * 2 + 1, 1, True, 2, False)
                step(qt, KV - 2, 0, True, 2 if more else 1, False)
                step(qt, KV - 1, 1, True, 2 if more else 0, more)
            quarter(0, True)
            with e.Fori(1, QUARTERS - 1) as qt:
                quarter(qt, True)
            quarter(QUARTERS - 1, False)

        def head_at(qt, g):
            return qt * KV + g

        def tile_at(s, j):
            return s * TILES + j

        def wrapped(g):
            return g % KV if isinstance(g, int) else g

        def splits(att, nxt):
            order = []
            if nxt:
                order.append(("w", 1, 1))
            if att:
                order += [("o", 0), ("o", 1)]
            if nxt:
                order.append(("w", 1, 2))
            if att:
                order += [("o", 2), ("o", 3)]
            if nxt:
                order += [("w", 1, 3), ("w", 1, 4), ("w", 1, 5)]
            if nxt > 1:
                order.append(("w", 2, 0))
            return order

        def before_turn(g, nxt):
            return isinstance(g, int) and g == KV - 2 and nxt == 2

        assert TILES % 2 == 0 and HEADS % 2 == 0

        with nc.Block() as block:

            def out_banks(b, nxt):
                return proj if not nxt and b % 2 else out

            @block.sync
            def _(sp):
                def load_o(s, g, r):
                    src = w_o[bass.ds(wrapped(g), 1), r, :, :].rearrange("a p n -> (a p) n")
                    sp.dma_start(o_stage[r % 2][:, :], src).then_inc(o_staged[r % 2], 16)

                def first():
                    sp.dma_start(cs[:, :, :], rope).then_inc(rope_in, 16)
                    load_o(0, 0, 0)
                    load_o(0, 0, 1)
                    after(sp, wlo_done, 1)
                    w_stage.load(sp, 0, 2)

                def step(qt, g, par, att, nxt, turn):
                    s = head_at(qt, g)
                    for what in splits(att, nxt):
                        if what[0] == "w":
                            ahead, j = what[1] + (what[2] + 2) // TILES, (what[2] + 2) % TILES
                            if ahead <= nxt:
                                after(sp, wlo_done, tile_at(s + what[1], what[2]) + 1)
                                w_stage.load(sp, wrapped(g + ahead), j)
                        else:
                            r, ahead = (what[1] + 2) % HEADS, (what[1] + 2) // HEADS
                            if nxt:
                                after(sp, wolo_done, s * HEADS + what[1] + 1)
                            elif what[1] == 0:
                                after(sp, wolo_done, s * HEADS + 1)
                            elif what[1] == 1:
                                sp.wait_ge(wolo_dve, 1)
                            if ahead == 0 or nxt:
                                load_o(s + ahead, g + ahead, r)
                steps(sp, first, step)

            def low_o(e, s, r, done):
                after(e, wohi_done, s * HEADS + r + 1)
                e.tensor_tensor(wo_lo[:, r, :], o_stage[r % 2][:, :], wo_hi[:, r, :].bitcast(F32), ALU.subtract)\
                 .then_inc(done, 1)

            @block.gpsimd
            def _(pool):
                def split_w(n, j):
                    after(pool, whi_done, n + 1)
                    pool.tensor_tensor(w_lo[j % 2][:, :], w_stage.buffers[j % 2][:, :], w_hi[j % 2][:, :].bitcast(F32),
                                       ALU.subtract).then_inc(wlo_done, 1)

                def first():
                    split_w(0, 0)

                def step(qt, g, par, att, nxt, turn):
                    s = head_at(qt, g)
                    for what in splits(att, nxt):
                        if what[0] == "w":
                            split_w(tile_at(s + what[1], what[2]), what[2])
                        elif nxt or what[1] % 2 == 0:
                            low_o(pool, s, what[1], wolo_done)
                steps(pool, first, step)

            @block.scalar
            def _(act):

                def split_w(s, j):
                    act.wait_ge(w_stage.landed[j % 2], (s * (TILES // 2) + j // 2 + 1) * 16)
                    if not (isinstance(s, int) and s == 0 and j < 2):
                        after(act, proj_done, tile_at(s, j) - 1)
                    act.copy(w_hi[j % 2][:, :], w_stage.buffers[j % 2][:, :]).then_inc(whi_done, 1)

                def split_o(s, r):
                    act.wait_ge(o_staged[r % 2], (s * (HEADS // 2) + r // 2 + 1) * 16)
                    if r == 0:
                        after(act, out_mm, s * QB)
                    act.copy(wo_hi[:, r, :], o_stage[r % 2][:, :]).then_inc(wohi_done, 1)

                def first():
                    split_w(0, 0)

                def soft(n, b):
                    after(act, ntop_done, n + 1)
                    after(act, pT_mm, n)
                    for r in range(HEADS):
                        last = act.activation(probs[:, r, :], sc[b % 2][:, r * P:(r + 1) * P], ACT.Exp,
                                              bias=ntop[:, r:r + 1], scale=SCALE, accum_out=total[:, r:r + 1])
                    last.then_inc(exp_done, 1)

                def pT_out(n):
                    after(act, pT_mm, n + 1)
                    after(act, ov_mm, n)
                    act.copy(pT[:, :], tp[:, :]).then_inc(pT_done, 1)

                def o_split(n):
                    after(act, ov_mm, n + 1)
                    after(act, out_mm, n)
                    act.copy(o_hi[:, :], ov[:, :]).then_inc(ohi_done, 1)

                def v_out(s):
                    after(act, proj_done, tile_at(s, 1) + 1)
                    act.copy(vT[:, :], proj[:, 1, :]).then_inc(vT_done, 1)

                def v_rows(s, par):
                    after(act, v_turned, s + 1)
                    act.copy(v[par][:, :, :], tp[:, :].rearrange("p (b d) -> p b d", d=D)).then_inc(v_done, 1)

                def step(qt, g, par, att, nxt, turn):
                    s = head_at(qt, g)
                    n = s * QB
                    order = splits(att, nxt)

                    def split(*which):
                        for what in which:
                            if what in order:
                                if what[0] == "w":
                                    split_w(s + what[1], what[2])
                                else:
                                    split_o(s, what[1])
                    if att:
                        v_rows(s, par)
                    if turn:
                        rows.high(act, qt + 1, proj, 0)
                        soft(n, 0)
                        rows.normalize(act, qt + 1, 2)
                        rows.high(act, qt + 1, proj, 1)
                        pT_out(n)
                        soft(n + 1, 1)
                        rows.normalize(act, qt + 1, 3)
                        rows.high(act, qt + 1, proj, 2)
                        pT_out(n + 1)
                        rows.high(act, qt + 1, proj, 3)
                        split(("w", 1, 1), ("o", 0), ("o", 1))
                    elif att:
                        soft(n, 0)
                        split(("w", 1, 1), ("o", 0), ("o", 1))
                        pT_out(n)
                        soft(n + 1, 1)
                    else:
                        split(("w", 1, 1))
                    split(("w", 1, 2), ("o", 2))
                    if nxt:
                        v_out(s + 1)
                    if att:
                        if not turn:
                            pT_out(n + 1)
                        o_split(n)
                    split(("o", 3),)
                    if att:
                        soft(n + 2, 2)
                    split(("w", 1, 3),)
                    if att:
                        pT_out(n + 2)
                        o_split(n + 1)
                        soft(n + 3, 3)
                    split(("w", 1, 4),)
                    if att:
                        pT_out(n + 3)
                        o_split(n + 2)
                    split(("w", 1, 5))
                    if att:
                        o_split(n + 3)
                    split(("w", 2, 0))
                    if before_turn(g, nxt):
                        rows.normalize(act, qt + 1, 0)
                        rows.normalize(act, qt + 1, 1)
                steps(act, first, step)

            @block.vector
            def _(dve):
                def rope_out(s, par, j):
                    n = s * ROPED + (j if j == 0 else j - 1)
                    src = proj[:, j % 2, :]
                    dst = kT[par][:, :] if j == 0 else qT[par][:, j - 2, :]
                    HD = D // 2

                    def cols(ap):
                        return ap.rearrange("p (b t) -> p b t", t=P)

                    def table(which, rows):
                        return cs[rows, which:which + 1, :].to_broadcast([HD if rows != slice(0, P) else P, QB, P])
                    after(dve, proj_done, tile_at(s, j) + 1)
                    after(dve, roped, n)
                    dve.tensor_tensor(cols(dst), cols(src), table(0, slice(0, P)), ALU.mult)\
                       .then_inc(rope_mul, 1)
                    low, high = slice(0, HD), slice(HD, P)
                    dve.tensor_tensor(cols(turned[low, :]), cols(src[high, :]), table(1, high), ALU.mult)\
                       .then_inc(rope_mul, 1)
                    dve.tensor_tensor(cols(turned[high, :]), cols(src[low, :]), table(1, low), ALU.mult)\
                       .then_inc(rope_mul, 1)
                    after(dve, rope_mul, n * 3 + 3)
                    dve.tensor_tensor(dst, dst, turned[:, :], ALU.add).then_inc(roped, 1)

                def top_of(n, b):
                    after(dve, sc_done, n + 1)
                    dve.tensor_reduce(top[:, :], sc[b % 2][:, :].rearrange("p (r k) -> p r k", k=P),
                                      AX.X, ALU.max).then_inc(top_done, 1)
                    after(dve, top_done, n + 1)
                    dve.tensor_scalar(ntop[:, :], top[:, :], -SCALE, None, ALU.mult).then_inc(ntop_done, 1)

                def normalize(n):
                    after(dve, exp_done, n + 1)
                    dve.reciprocal(rtotal[:, :], total[:, :]).then_inc(rtotal_done, 1)
                    after(dve, rtotal_done, n + 1)
                    dve.tensor_tensor(probs[:, :, :], probs[:, :, :],
                                      rtotal[:, :].rearrange("p (r a) -> p r a", a=1).to_broadcast([P, HEADS, P]),
                                      ALU.mult).then_inc(probs_done, 1)

                def o_split(n):
                    after(dve, ohi_done, n + 1)
                    dve.tensor_tensor(o_lo[:, :], ov[:, :], o_hi[:, :].bitcast(F32), ALU.subtract).then_inc(olo_done, 1)

                def add(qt, n, b, nxt):
                    after(dve, out_mm, n + 1)
                    hb = row(h, qt * QB + b)
                    part = out_banks(b, nxt)[:, :, :].rearrange("p a n -> p (a n)")
                    dve.tensor_tensor(hb, hb, part, ALU.add).then_inc(added, 1)

                def step(qt, g, par, att, nxt, turn):
                    s = head_at(qt, g)
                    n = s * QB
                    turn_next = before_turn(g, nxt)
                    for_next_stage = isinstance(g, int) and g == KV - 1 and not early(qt, 1)
                    if turn_next:
                        stats_of, link = qt + 1, Links(dve, rows.norm, (qt + 1) * rows.LINKS + 1)
                    elif for_next_stage:
                        stats_of, link = qt - 1, Links(dve, ahead, (qt - 1) * rows.LINKS + 1)
                        after(dve, added, qt * (KV * QB))
                    stats = turn_next or for_next_stage
                    if turn:
                        top_of(n, 0)
                        rows.low(dve, qt + 1, proj, 0)
                        normalize(n)
                        top_of(n + 1, 1)
                        rows.low(dve, qt + 1, proj, 1)
                        normalize(n + 1)
                        rows.low(dve, qt + 1, proj, 2)
                        rows.low(dve, qt + 1, proj, 3)
                    elif att:
                        top_of(n, 0)
                        normalize(n)
                    if nxt:
                        rope_out(s + 1, 1 - par, 0)
                    if att:
                        if not turn:
                            top_of(n + 1, 1)
                            if not nxt:
                                low_o(dve, s, 1, wolo_dve)
                            normalize(n + 1)
                        top_of(n + 2, 2)
                        o_split(n)
                        normalize(n + 2)
                    if nxt:
                        rope_out(s + 1, 1 - par, 2)
                    if att:
                        if not nxt:
                            low_o(dve, s, 3, wolo_dve)
                        top_of(n + 3, 3)
                        o_split(n + 1)
                        add(qt, n, 0, nxt)
                        normalize(n + 3)
                    if stats:
                        rows.stats(dve, stats_of, link, 0)
                    if nxt:
                        rope_out(s + 1, 1 - par, 3)
                    if stats:
                        rows.stats(dve, stats_of, link, 1)
                    if att:
                        o_split(n + 2)
                        add(qt, n + 1, 1, nxt)
                    if stats:
                        rows.stats(dve, stats_of, link, 2)
                    if nxt:
                        rope_out(s + 1, 1 - par, 4)
                    if stats:
                        rows.stats(dve, stats_of, link, 3)
                    if att:
                        o_split(n + 3)
                        add(qt, n + 2, 2, nxt)
                    if nxt:
                        rope_out(s + 1, 1 - par, 5)
                    if stats:
                        rows.coefficients(dve, link)
                    if turn_next:
                        after(dve, rows.normed, (qt + 1) * QB)
                        rows.keep(dve, link, rows.rstd[:, :], rows.shift[:, :])
                    elif for_next_stage:
                        these = bass.ds(stats_of * QB, QB)
                        rows.keep(dve, link, next_rstd[:, these], next_shift[:, these])
                    if att:
                        add(qt, n + 3, 3, nxt)
                dve.wait_ge(rope_in, 16)
                steps(dve, lambda: None, step)

            @block.tensor
            def _(pe):
                def project(qt, s, g, j):
                    after(pe, wlo_done, tile_at(s, j) + 1)
                    if j == 0:
                        after(pe, rows.lo_done, (qt + 1) * rows.UNITS)
                    if j == 3:
                        after(pe, vT_done, s + 1)
                    else:
                        after(pe, roped, s * ROPED + {0: -1, 1: 0, 2: 1, 4: 2, 5: 3}[j])
                    hi, lo = w_hi[j % 2], w_lo[j % 2]
                    for k in range(KT):
                        w = slice(k * P, (k + 1) * P)
                        pe.matmul(proj[:, j % 2, :], hi[:, w], x_hi[:, k, :], start=(k == 0), stop=False)
                        pe.matmul(proj[:, j % 2, :], hi[:, w], x_lo[:, k, :], start=False, stop=False)
                        last = pe.matmul(proj[:, j % 2, :], lo[:, w], x_hi[:, k, :], start=False, stop=(k == KT - 1))
                    last.then_inc(proj_done, 1)

                def scores(s, n, par, b):
                    if b == 0:
                        after(pe, roped, (s + 1) * ROPED)
                    cols = slice(b * P, (b + 1) * P)
                    for r in range(HEADS):
                        last = pe.matmul(sc[b % 2][:, r * P:(r + 1) * P], qT[par][:, r, cols], kT[par][:, cols],
                                         start=True, stop=True)
                    last.then_inc(sc_done, 1)

                def turn_probs(s, n, b):
                    after(pe, probs_done, n + 1)
                    if b == 0:
                        after(pe, v_done, s + 1)
                    else:
                        after(pe, pT_done, n)
                    for r in range(HEADS):
                        last = pe.transpose(tp[:, r * P:(r + 1) * P], probs[:, r, :], ident[:, :])
                    last.then_inc(pT_mm, 1)

                def values(n, par, b):
                    after(pe, pT_done, n + 1)
                    after(pe, olo_done, n)
                    pe.matmul(ov[:, :], v[par][:, b, :], pT[:, :], start=True, stop=True).then_inc(ov_mm, 1)

                def outputs(s, n, b, nxt):
                    after(pe, olo_done, n + 1)
                    if nxt or b == 0:
                        after(pe, added, n)
                    elif b >= 2:
                        after(pe, added, n - 1)
                    banks = out_banks(b, nxt)
                    if b == 0 and nxt:
                        after(pe, wolo_done, (s + 1) * HEADS)
                    elif b == 0:
                        after(pe, wolo_done, s * HEADS + HEADS // 2)
                        pe.wait_ge(wolo_dve, HEADS // 2)
                    for r in range(HEADS):
                        rows = slice(r * P, (r + 1) * P)
                        for a, w, first, end in ((o_hi, wo_hi, r == 0, False), (o_hi, wo_lo, False, False),
                                                 (o_lo, wo_hi, False, r == HEADS - 1)):
                            for c in range(2):
                                last = pe.matmul(banks[:, c, :], a[:, rows], w[:, r, c * BANK:(c + 1) * BANK],
                                                 start=first, stop=end)
                    last.then_inc(out_mm, 1)

                def turn_v(s):
                    after(pe, vT_done, s + 1)
                    after(pe, pT_done, s * QB)
                    for b in range(QB):
                        last = pe.transpose(tp[:, b * D:(b + 1) * D], vT[:, b * P:(b + 1) * P], ident[:, :])
                    last.then_inc(v_turned, 1)

                def step(qt, g, par, att, nxt, turn):
                    s = head_at(qt, g)
                    n = s * QB
                    if turn:
                        scores(s, n, par, 0)
                        rows.turn(pe, qt + 1, proj, 0)
                        scores(s, n + 1, par, 1)
                        turn_probs(s, n, 0)
                        rows.turn(pe, qt + 1, proj, 1)
                        values(n, par, 0)
                        turn_probs(s, n + 1, 1)
                        rows.turn(pe, qt + 1, proj, 2, 3)
                    for j in range(TILES):
                        if att:
                            if 3 <= j:
                                outputs(s, n + j - 3, j - 3, nxt)
                            if 2 <= j and not (turn and j == 2):
                                values(n + j - 2, par, j - 2)
                            if j < QB and not (turn and j < 2):
                                scores(s, n + j, par, j)
                            if 1 <= j <= QB and not (turn and j <= 2):
                                turn_probs(s, n + j - 1, j - 1)
                        if nxt:
                            project(qt + 1 if turn else qt, s + 1, g + 1, j)
                    if att:
                        outputs(s, n + QB - 1, QB - 1, nxt)
                    if nxt:
                        turn_v(s + 1)
                steps(pe, lambda: None, step)


GROUP = 4


class Rows:

    LINKS = 3 + RSQRT_LINKS + 1

    def __init__(self, nc, ctx, name, h, ident):
        def sb(n, shape, dt=F32):
            return ctx.enter_context(nc.sbuf_tensor(f"{name}_{n}", shape, dt))

        def sem(n):
            return ctx.enter_context(nc.semaphore(f"{name}_{n}"))

        self.h, self.ident = h, ident
        self.xn = sb("xn", [P, L])
        self.x_hi = [sb(f"xhi{i}", [P, KT, P], F32R) for i in range(2)]
        self.x_lo = [sb(f"xlo{i}", [P, KT, P], F32R) for i in range(2)]
        self.st = sb("st", [P, GROUP, 2, 6])
        self.mv = sb("mv", [P, GROUP, 2])
        self.var, self.tmp, self.root = (sb(n, [P, GROUP]) for n in ("var", "tmp", "root"))
        self.rstd, self.shift = sb("rstd", [P, GROUP]), sb("shift", [P, GROUP])
        self.dummy = sb("dummy", [P, 1])
        self.tp = ctx.enter_context(nc.psum_tensor(f"{name}_tp", [P, 2, BANK], F32))
        self.norm = sem("norm")
        self.normed = sem("normed")
        self.turned = sem("turned")
        self.hi_done = sem("xhi_done")
        self.lo_done = sem("xlo_done")
        self.sems = [self.norm, self.normed, self.turned, self.hi_done, self.lo_done]

    def stats(self, dve, group, tiles):
        for i in tiles:
            hb = row(self.h, group * GROUP + i)
            for c in range(2):
                last = dve.bn_stats(self.st[:, i, c, :], hb[:, c * BANK:(c + 1) * BANK])
        if GROUP - 1 in tiles:
            self.coefficients(dve, group, last)

    def coefficients(self, dve, group, last):
        link = Links(dve, self.norm, group * self.LINKS + 1)
        link(last)
        dve.memset(self.dummy[:, :], 0.0)
        for i in range(GROUP):
            last = dve.bn_aggr(self.mv[:, i, :], self.st[:, i, :, :])
        link(last)
        link(dve.tensor_scalar(self.var[:, :], self.mv[:, :, 1], EPS, None, ALU.add))
        rsqrt(dve, self.root[:, :], self.var[:, :], self.tmp[:, :], link)
        after(dve, self.normed, group * GROUP)
        dve.tensor_copy(self.rstd[:, :], self.root[:, :])
        link(dve.scalar_tensor_tensor(out=self.shift[:, :], in0=self.mv[:, :, 0], scalar=-1.0,
                                      in1=self.root[:, :], op0=ALU.mult, op1=ALU.mult))
        assert link.n == self.LINKS

    def normalize(self, act, group, i):
        t = group * GROUP + i
        after(act, self.norm, (group + 1) * self.LINKS)
        after(act, self.turned, t)
        act.activation(self.xn[:, :], row(self.h, t), ACT.Identity,
                       bias=self.shift[:, i:i + 1], scale=self.rstd[:, i:i + 1]).then_inc(self.normed, 1)

    def turn(self, pe, t):
        after(pe, self.normed, t + 1)
        after(pe, self.lo_done, t)
        for k in range(KT):
            last = pe.transpose(self.tp[:, k // 4, (k % 4) * P:(k % 4 + 1) * P],
                                self.xn[:, k * P:(k + 1) * P], self.ident[:, :])
        last.then_inc(self.turned, 1)

    def high(self, act, t, par, used, count):
        after(act, self.turned, t + 1)
        after(act, used, count)
        act.copy(self.x_hi[par][:, :, :], self.tp[:, :, :].rearrange("p a (k t) -> p (a k) t", t=P))\
           .then_inc(self.hi_done, 1)

    def low(self, dve, t, par):
        after(dve, self.hi_done, t + 1)
        dve.tensor_tensor(self.x_lo[par][:, :, :], self.tp[:, :, :].rearrange("p a (k t) -> p (a k) t", t=P),
                          self.x_hi[par][:, :, :].bitcast(F32), ALU.subtract).then_inc(self.lo_done, 1)


def tile_steps(e, before, body, finish):
    GROUPS = NB // GROUP

    def group(g, first, last):
        for i in range(GROUP):
            body(g, i, g * GROUP + i, lambda k: not (first and i + k < 0 or last and i + k >= GROUP))
    before()
    group(0, True, False)
    with e.Fori(1, GROUPS - 1) as g:
        group(g, False, False)
    group(GROUPS - 1, False, True)
    finish()


class RowsAhead(Rows):

    def __init__(self, nc, ctx, name, h, ident, rstd, shift):
        super().__init__(nc, ctx, name, h, ident)
        self.all_rstd, self.all_shift = rstd, shift
        last = slice(NB - GROUP, NB)
        self.rstd, self.shift = rstd[:, last], shift[:, last]

    def last_stats(self, dve, tiles):
        for i in tiles:
            for c in range(2):
                last = dve.bn_stats(self.st[:, i, c, :], self.h[:, NB - GROUP + i, c * BANK:(c + 1) * BANK])
        if GROUP - 1 in tiles:
            self.coefficients(dve, 0, last)

    def normalize(self, act, group, i):
        t = group * GROUP + i
        if not early(group, NB // GROUP - 1):
            after(act, self.norm, self.LINKS)
        after(act, self.turned, t)
        act.activation(self.xn[:, :], row(self.h, t), ACT.Identity, bias=self.all_shift[:, bass.ds(t, 1)],
                       scale=self.all_rstd[:, bass.ds(t, 1)]).then_inc(self.normed, 1)


class Weight:

    CHUNK = 1024

    def __init__(self, nc, ctx, name, src):
        self.name, self.src, self.n = name, src, src.shape[1]
        self.chunks = -(-self.n // self.CHUNK)
        self.raw, self.lo = landing(nc, ctx, f"{name}_lo", [P, self.n])
        self.landed = [ctx.enter_context(nc.semaphore(f"{name}_landed{c}")) for c in range(self.chunks)]

    def add_high(self, nc, ctx):
        self.hi = ctx.enter_context(nc.sbuf_tensor(f"{self.name}_hi", [P, self.n], F32R))
        self.hi_done = ctx.enter_context(nc.semaphore(f"{self.name}_hi_done"))
        self.lo_done = ctx.enter_context(nc.semaphore(f"{self.name}_lo_done"))
        return self

    def cols(self, c):
        return slice(c * self.CHUNK, min(self.n, (c + 1) * self.CHUNK))

    def load(self, sp):
        for c in range(self.chunks):
            sp.dma_start(self.raw[:, self.cols(c)], self.src[:, self.cols(c)]).then_inc(self.landed[c], 16)

    def high(self, act):
        for c in range(self.chunks):
            act.wait_ge(self.landed[c], 16)
            act.copy(self.hi[:, self.cols(c)], self.raw[:, self.cols(c)]).then_inc(self.hi_done, 1)

    def low(self, e, chunks=None):
        for c in range(self.chunks) if chunks is None else chunks:
            e.wait_ge(self.hi_done, c + 1)
            cols = self.cols(c)
            e.tensor_tensor(self.lo[:, cols], self.raw[:, cols], self.hi[:, cols].bitcast(F32), ALU.subtract)\
             .then_inc(self.lo_done, 1)

    def ready(self, pe):
        pe.wait_ge(self.lo_done, self.chunks)


EXPERTS = 8
RANK = 16
ER = EXPERTS * RANK
ROUTED = ER + EXPERTS


class ScreenTables:

    def __init__(self, nc, ctx, f_dram, c_dram):
        f_raw, self.f_hi = landing(nc, ctx, "sc_fhi", [P, KT // 2, L])
        c_raw, self.c_hi = landing(nc, ctx, "sc_chi", [P, KT // 2, HALF])
        self.landed = ctx.enter_context(nc.semaphore("sc_tables_landed"))
        self.rounded = ctx.enter_context(nc.semaphore("sc_tables_rounded"))

        def pair(ap, k):
            return ap[:, k:k + 2, :].rearrange("p k n -> p (k n)")
        self.chunks = [(self.f_hi[:, k, :], f_raw[:, k, :], f_dram[:, k * L:(k + 1) * L])
                       for k in range(KT // 2)]
        self.chunks += [(pair(self.c_hi, k), pair(c_raw, k), c_dram[:, k * HALF:(k + 2) * HALF])
                        for k in range(0, KT // 2, 2)]

    def load(self, sp):
        for _, raw, src in self.chunks:
            sp.dma_start(raw, src).then_inc(self.landed, 16)

    def round(self, pool):
        pool.wait_ge(self.landed, 16 * len(self.chunks))
        for hi, raw, _ in self.chunks:
            pool.tensor_copy(hi, raw).then_inc(self.rounded, 1)


class ScreenStats:

    LINKS = 3 + RSQRT_LINKS + 1

    def __init__(self, nc, ctx, h, rstd, shift):
        def sb(n, shape):
            return ctx.enter_context(nc.sbuf_tensor(f"ss_{n}", shape, F32))

        self.h, self.rstd, self.shift = h, rstd, shift
        self.st, self.mv = sb("st", [P, QB, 2, 6]), sb("mv", [P, NB, 2])
        self.var, self.tmp = sb("var", [P, QB]), sb("tmp", [P, QB])
        self.norm = ctx.enter_context(nc.semaphore("ss_norm"))

    def take(self, dve, qt, b):
        for c in range(2):
            last = dve.bn_stats(self.st[:, b, c, :], self.h[:, qt * QB + b, c * BANK:(c + 1) * BANK])
        if b < QB - 1:
            return
        link = Links(dve, self.norm, qt * self.LINKS)
        these = slice(qt * QB, (qt + 1) * QB)
        mv, rstd, var, tmp = self.mv[:, these, :], self.rstd[:, these], self.var[:, :], self.tmp[:, :]
        link(last)
        for b in range(QB):
            last = dve.bn_aggr(mv[:, b, :], self.st[:, b, :, :])
        link(last)
        link(dve.tensor_scalar(var, mv[:, :, 1], EPS, None, ALU.add))
        rsqrt(dve, rstd, var, tmp, link)
        link(dve.scalar_tensor_tensor(out=self.shift[:, these], in0=mv[:, :, 0], scalar=-1.0, in1=rstd,
                                      op0=ALU.mult, op1=ALU.mult))
        assert link.n == self.LINKS


def mixture_stage(nc, h, ident, a_route, bw, experts, tables, stats, rstd, shift):
    with ExitStack() as ctx:
        def sb(name, shape, dt=F32):
            return ctx.enter_context(nc.sbuf_tensor(name, shape, dt))

        def sem(name):
            return ctx.enter_context(nc.semaphore(name))

        ar = Weight(nc, ctx, "mx_ar", a_route).add_high(nc, ctx)
        b = Weight(nc, ctx, "mx_b", bw).add_high(nc, ctx)
        rows = RowsAhead(nc, ctx, "mx", h, ident, rstd, shift)
        logits = sb("mx_logits", [P, EXPERTS])
        best = sb("mx_best", [P, 8])
        at = sb("mx_at", [P, 8], mybir.dt.uint32)
        atf = sb("mx_atf", [P, 1])
        weight = sb("mx_weight", [P, EXPERTS])
        numbers = sb("mx_numbers", [P, EXPERTS])
        wh = sb("mx_wh", [P, ER])
        wt_hi = sb("mx_wthi", [P, P], F32R)
        wt_lo = sb("mx_wtlo", [P, P], F32R)
        pj = ctx.enter_context(nc.psum_tensor("mx_pj", [P, BANK], F32))
        wt = ctx.enter_context(nc.psum_tensor("mx_wt", [P, BANK], F32))
        out = ctx.enter_context(nc.psum_tensor("mx_out", [P, 2, BANK], F32))
        numbers_in, pj_done, route = sem("mx_numbers_in"), sem("mx_pj_done"), sem("mx_route")
        wh_done, wt_mm, wthi_done, wtlo_done = sem("mx_wh_done"), sem("mx_wt_mm"), sem("mx_wthi"), sem("mx_wtlo")
        out_mm, added = sem("mx_out_mm"), sem("mx_added")
        prime(nc, rows.sems + [pj_done, route, wh_done, wt_mm, wthi_done, wtlo_done, out_mm, added])
        ROUTE_LINKS = 5

        with nc.Block() as block:

            @block.sync
            def _(sp):
                ar.load(sp)
                sp.dma_start(numbers[:, :], experts).then_inc(numbers_in, 16)
                b.load(sp)
                tables.load(sp)

            @block.gpsimd
            def _(pool):
                tables.round(pool)

            @block.scalar
            def _(act):
                def before():
                    ar.high(act)
                    rows.normalize(act, 0, 0)
                    rows.high(act, 0, 0, pj_done, 0)
                    rows.normalize(act, 0, 1)
                    b.high(act)

                def body(g, i, t, on):
                    if on(1):
                        rows.high(act, t + 1, (i + 1) % 2, pj_done, t)
                    if on(2):
                        rows.normalize(act, g + (i + 2) // GROUP, (i + 2) % GROUP)
                    after(act, wt_mm, t + 1)
                    after(act, out_mm, t)
                    act.copy(wt_hi[:, :], wt[:, 0:P]).then_inc(wthi_done, 1)
                tile_steps(act, before, body, lambda: None)

            @block.vector
            def _(dve):
                def before():
                    ar.low(dve)
                    rows.low(dve, 0, 0)
                    b.low(dve)
                    dve.wait_ge(numbers_in, 16)

                def route_of(t):
                    after(dve, pj_done, t + 1)
                    link = Links(dve, route, t * ROUTE_LINKS + 1)
                    link(dve.tensor_copy(logits[:, :], pj[:, ER:ROUTED]))
                    dve.memset(rows.dummy[:, :], 0.0)
                    link(dve.max(best[:, :], logits[:, :]))
                    dve.memset(rows.dummy[:, :], 0.0)
                    link(dve.max_index(at[:, :], best[:, :], logits[:, :]))
                    link(dve.tensor_copy(atf[:, :], at[:, 0:1]))
                    link(dve.tensor_scalar(weight[:, :], numbers[:, :], atf[:, :], best[:, 0:1],
                                           ALU.is_equal, ALU.mult))
                    assert link.n == ROUTE_LINKS
                    after(dve, wt_mm, t)
                    dve.tensor_tensor(wh[:, :].rearrange("p (e r) -> p e r", r=RANK),
                                      pj[:, 0:ER].rearrange("p (e r) -> p e r", r=RANK),
                                      weight[:, :].rearrange("p (e a) -> p e a", a=1).to_broadcast([P, EXPERTS, RANK]),
                                      ALU.mult).then_inc(wh_done, 1)

                def add(t):
                    after(dve, out_mm, t + 1)
                    hb = row(h, t)
                    dve.tensor_tensor(hb, hb, out[:, :, :].rearrange("p a n -> p (a n)"), ALU.add).then_inc(added, 1)

                def body(g, i, t, on):
                    if on(1):
                        rows.low(dve, t + 1, (i + 1) % 2)
                    route_of(t)
                    if on(-1):
                        add(t - 1)
                    after(dve, wthi_done, t + 1)
                    dve.tensor_tensor(wt_lo[:, :], wt[:, 0:P], wt_hi[:, :].bitcast(F32), ALU.subtract)\
                       .then_inc(wtlo_done, 1)
                    if early(g, 1):
                        rows.last_stats(dve, (i,))
                    if not on(GROUP):
                        if i == 0:
                            after(dve, added, GROUP)
                        stats.take(dve, 0, i)
                tile_steps(dve, before, body, lambda: add(NB - 1))

            @block.tensor
            def _(pe):
                def before():
                    rows.turn(pe, 0)
                    ar.ready(pe)
                    b.ready(pe)

                def outputs(t):
                    after(pe, wtlo_done, t + 1)
                    after(pe, added, t)
                    for c in range(2):
                        w = slice(c * BANK, (c + 1) * BANK)
                        pe.matmul(out[:, c, :], wt_hi[:, :], b.hi[:, w], start=True, stop=False)
                        pe.matmul(out[:, c, :], wt_hi[:, :], b.lo[:, w], start=False, stop=False)
                        mm = pe.matmul(out[:, c, :], wt_lo[:, :], b.hi[:, w], start=False, stop=True)
                    mm.then_inc(out_mm, 1)

                def body(g, i, t, on):
                    after(pe, rows.lo_done, t + 1)
                    if on(1):
                        rows.turn(pe, t + 1)
                    after(pe, wh_done, t)
                    xh, xl = rows.x_hi[i % 2], rows.x_lo[i % 2]
                    for k in range(KT):
                        w = slice(k * ROUTED, (k + 1) * ROUTED)
                        pe.matmul(pj[:, 0:ROUTED], xh[:, k, :], ar.hi[:, w], start=(k == 0), stop=False)
                        pe.matmul(pj[:, 0:ROUTED], xh[:, k, :], ar.lo[:, w], start=False, stop=False)
                        mm = pe.matmul(pj[:, 0:ROUTED], xl[:, k, :], ar.hi[:, w], start=False, stop=(k == KT - 1))
                    mm.then_inc(pj_done, 1)
                    if on(-1):
                        outputs(t - 1)
                    after(pe, wh_done, t + 1)
                    after(pe, wtlo_done, t)
                    pe.transpose(wt[:, 0:P], wh[:, :], ident[:, :]).then_inc(wt_mm, 1)
                tile_steps(pe, before, body, lambda: outputs(NB - 1))


TOP_K = 6
HALF = L // 2
NO_WEIGHT = 150.0


def screen(nc, h, ident, tables, stats, flag, weights):
    with ExitStack() as ctx:
        def sb(name, shape, dt=F32):
            return ctx.enter_context(nc.sbuf_tensor(name, shape, dt))

        def sem(name):
            return ctx.enter_context(nc.semaphore(name))

        f_hi, c_hi = tables.f_hi, tables.c_hi
        xn = [sb(f"sc_xn{i}", [P, L]) for i in range(2)]
        folded = [sb(f"sc_folded{i}", [P, 2, BANK]) for i in range(2)]
        x_hi = [sb(f"sc_xhi{i}", [P, KT, QT], F32R) for i in range(2)]
        squares = [sb(f"sc_sq{i}", [P, 2, BANK]) for i in range(2)]
        power = [sb(f"sc_pw{i}", [P, KT // 2, QT], F32R) for i in range(2)]
        mv, rstd, shift = stats.mv, stats.rstd, stats.shift
        top = sb("sc_top", [P, NB])
        lead = sb("sc_lead", [P, NB])
        least = sb("sc_least", [P, 1])
        least_row = sb("sc_least_row", [1, 1])
        tp = ctx.enter_context(nc.psum_tensor("sc_tp", [P, 2, BANK], F32))
        ri = ctx.enter_context(nc.psum_tensor("sc_ri", [P, 2, 2, BANK], F32))
        co = ctx.enter_context(nc.psum_tensor("sc_co", [P, 2, BANK], F32))
        normed, turned, hi_done = sem("sc_normed"), sem("sc_turned"), sem("sc_hi_done")
        fold_done = sem("sc_fold_done")
        spectrum, squared, powered = sem("sc_spectrum"), sem("sc_squared"), sem("sc_powered")
        corr_mm, topped, leads, least_t = sem("sc_corr_mm"), sem("sc_topped"), sem("sc_leads"), sem("sc_least_t")
        FT = KT // 2

        with nc.Block() as block:

            @block.sync
            def _(sp):
                for weight in weights:
                    weight.load(sp)

            @block.vector
            def _(dve):
                def fold(qt, b):
                    t = qt * QB + b
                    dve.wait_ge(normed, t + 1)
                    if t >= 2:
                        dve.wait_ge(turned, t - 1)
                    halves = [xn[t % 2][:, c * BANK:(c + 1) * BANK] for c in range(2)]
                    dve.tensor_tensor(folded[t % 2][:, 0, :], *halves, ALU.add)
                    dve.tensor_tensor(folded[t % 2][:, 1, :], *halves, ALU.subtract).then_inc(fold_done, 1)

                def tops(qt):
                    for b in range(QB):
                        t = qt * QB + b
                        dve.wait_ge(corr_mm, t + 1)
                        dve.tensor_reduce(top[:, t:t + 1], co[:, t % 2, :], AX.X, ALU.max).then_inc(topped, 1)

                for qt in range(-1, QUARTERS):
                    for i in range(QB):
                        if qt + 1 < QUARTERS:
                            fold(qt + 1, i)
                        if i == 0 and qt >= 1:
                            tops(qt - 1)
                        if qt + 2 < QUARTERS:
                            for b in ((0,), (1, 2), (3,), ())[i]:
                                stats.take(dve, qt + 2, b)
                tops(QUARTERS - 1)
                link = Links(dve, leads, 0)
                dve.wait_ge(topped, NB)
                link(dve.tensor_tensor(lead[:, :], mv[:, :, 1], rstd[:, :], ALU.mult))
                link(dve.tensor_tensor(lead[:, :], lead[:, :], rstd[:, :], ALU.mult))
                link(dve.scalar_tensor_tensor(out=lead[:, :], in0=lead[:, :], scalar=float(L), in1=top[:, :],
                                              op0=ALU.mult, op1=ALU.subtract))
                link(dve.tensor_reduce(least[:, :], lead[:, :], AX.X, ALU.min))
                dve.wait_ge(least_t, 1)
                link(dve.tensor_reduce(least_row[:, :], tp[0:1, 0, 0:P], AX.X, ALU.min))
                link(dve.tensor_scalar(flag[:, :], least_row[:, :], NO_WEIGHT, None, ALU.is_ge))

            @block.scalar
            def _(act):
                def rows(qt, b):
                    t = qt * QB + b
                    act.wait_ge(stats.norm, (qt + 1) * stats.LINKS)
                    if t >= 2:
                        act.wait_ge(fold_done, t - 1)
                    act.activation(xn[t % 2][:, :], h[:, t, :], ACT.Identity,
                                   bias=shift[:, t:t + 1], scale=rstd[:, t:t + 1]).then_inc(normed, 1)

                def high(qt, b):
                    t = qt * QB + b
                    act.wait_ge(turned, t + 1)
                    if qt >= 2 and b == 0:
                        act.wait_ge(spectrum, (qt - 1) * FT)
                    act.copy(x_hi[qt % 2][:, :, b * P:(b + 1) * P],
                             tp[:, :, :].rearrange("p a (k t) -> p (a k) t", t=P)).then_inc(hi_done, 1)

                def square(qt, i):
                    n = qt * FT + i
                    act.wait_ge(spectrum, n + 1)
                    if n >= 2:
                        act.wait_ge(powered, n - 1)
                    act.activation(squares[n % 2][:, :, :], ri[:, n % 2, :, :], ACT.Square).then_inc(squared, 1)

                rows(0, 0)
                rows(0, 1)
                for n in range(NB + FT):
                    if n < NB:
                        high(*divmod(n, QB))
                    if n >= FT:
                        square(*divmod(n - FT, FT))
                    if n + 2 < NB:
                        rows(*divmod(n + 2, QB))

            @block.gpsimd
            def _(pool):
                for n in range(QUARTERS * FT):
                    qt, i = n // FT, n % FT
                    pool.wait_ge(squared, n + 1)
                    if qt >= 2 and i == 0:
                        pool.wait_ge(corr_mm, (qt - 1) * QB)
                    sq = squares[n % 2]
                    pool.tensor_tensor(power[qt % 2][:, i, :], sq[:, 0, :], sq[:, 1, :], ALU.add).then_inc(powered, 1)

            @block.tensor
            def _(pe):
                def turn(qt, b):
                    t = qt * QB + b
                    pe.wait_ge(fold_done, t + 1)
                    if t:
                        pe.wait_ge(hi_done, t)
                    for k in range(KT):
                        part, cols = k // 4, slice(k % 4 * P, (k % 4 + 1) * P)
                        last = pe.transpose(tp[:, part, cols], folded[t % 2][:, part, cols], ident[:, :])
                    last.then_inc(turned, 1)

                def dft(qt, i):
                    n = qt * FT + i
                    if i == 0:
                        pe.wait_ge(hi_done, (qt + 1) * QB)
                    if n >= 2:
                        pe.wait_ge(squared, n - 1)
                    odd, at = i // 2, i % 2 * 2 * P
                    for part in range(2):
                        cols = slice(part * HALF + at + odd, part * HALF + at + 2 * P, 2)
                        for k in range(KT // 2):
                            last = pe.matmul(ri[:, n % 2, part, :], f_hi[:, k, cols],
                                             x_hi[qt % 2][:, odd * (KT // 2) + k, :],
                                             start=(k == 0), stop=(k == KT // 2 - 1))
                    last.then_inc(spectrum, 1)

                def correlate(qt):
                    pe.wait_ge(powered, (qt + 1) * FT)
                    for b in range(QB):
                        t = qt * QB + b
                        if t >= 2:
                            pe.wait_ge(topped, t - 1)
                        for k in range(FT):
                            last = pe.matmul(co[:, t % 2, :], power[qt % 2][:, k, b * P:(b + 1) * P], c_hi[:, k, :],
                                             start=(k == 0), stop=(k == FT - 1))
                        last.then_inc(corr_mm, 1)

                for b in range(QB):
                    turn(0, b)
                pe.wait_ge(tables.rounded, len(tables.chunks))
                for qt in range(QUARTERS):
                    for i in range(FT):
                        dft(qt, i)
                        if qt + 1 < QUARTERS:
                            turn(qt + 1, i)
                        if i == 0 and qt:
                            correlate(qt - 1)
                correlate(QUARTERS - 1)
                pe.wait_ge(leads, 4)
                pe.transpose(tp[0:1, 0, 0:P], least[:, :], ident[:, :]).then_inc(least_t, 1)


TURNS = (["xn", "x_turned", "xT", "x_dft", "x_spectrum", "re2", "im2", "power", "power_0", "power_512",
          "power_turned", "powerT", "corr_mm", "corr", "best", "at", "at_f", "minus", "exp", "rtotal", "weights",
          "spread_0"] + [f"{what}_{j}" for j in range(1, TOP_K) for what in ("one", "spread")] +
         ["w_turned", "wT", "w_dft", "w_spectrum", "rr", "ii", "re", "ir", "ri", "im", "re_0", "re_512",
          "a_turned", "aT", "agg", "added"])


def delay_average(nc, ctx, h, ident, f_dram, g_dram, lags, rstd, shift):
    def sb(name, shape, dt=F32):
        return ctx.enter_context(nc.sbuf_tensor(name, shape, dt))

    fwd, inv = sb("da_fwd", [P, KT, L]), sb("da_inv", [P, KT, L])
    lag_row = sb("da_lags", [P, L])
    xn, corr, spread, one = (sb(f"da_{n}", [P, L]) for n in ("xn", "corr", "spread", "one"))
    xT = sb("da_xT", [P, KT, P])
    xs, ws, sq, am = (sb(f"da_{n}", [P, 2, HALF]) for n in ("xs", "ws", "sq", "am"))
    power = sb("da_power", [P, KT // 2 + 1, P])
    best, at_f, weights = (sb(f"da_{n}", [P, 8]) for n in ("best", "at_f", "weights"))
    at = sb("da_at", [P, 8], mybir.dt.uint32)
    minus, total, rtotal, dummy = (sb(f"da_{n}", [P, 1]) for n in ("minus", "total", "rtotal", "dummy"))
    tp = ctx.enter_context(nc.psum_tensor("da_tp", [P, KT, P], F32))
    mm = ctx.enter_context(nc.psum_tensor("da_mm", [P, 2, BANK], F32))
    tables = ctx.enter_context(nc.semaphore("da_tables"))
    cleared = ctx.enter_context(nc.semaphore("da_cleared"))
    done = ctx.enter_context(nc.semaphore("da_done"))
    prime(nc, [done])
    S = len(TURNS)
    flat = power[:, :, :].rearrange("p k n -> p (k n)")


    def turn(e, t, name, ins):
        after(e, done, t * S + TURNS.index(name))
        ins().then_inc(done, 1)

    def sync(sp):
        sp.dma_start(fwd[:, :, :].rearrange("p k n -> p (k n)"), f_dram).then_inc(tables, 16)
        sp.dma_start(inv[:, :, :].rearrange("p k n -> p (k n)"), g_dram).then_inc(tables, 16)
        sp.dma_start(lag_row[:, :], lags).then_inc(tables, 16)

    def scalar(act):
        act.wait_ge(cleared, 1)
        with act.Fori(0, NB) as t:
            turn(act, t, "xn", lambda: act.activation(
                xn[:, :], row(h, t), ACT.Identity,
                bias=shift[:, bass.ds(t, 1)], scale=rstd[:, bass.ds(t, 1)]))
            turn(act, t, "xT", lambda: act.copy(xT[:, :, :], tp[:, :, :]))
            turn(act, t, "x_spectrum", lambda: act.copy(xs[:, :, :], mm[:, :, :]))
            turn(act, t, "powerT", lambda: act.copy(xT[:, 0:5, :], tp[:, 0:5, :]))
            turn(act, t, "corr", lambda: act.copy(corr[:, :], mm[:, :, :].rearrange("p a n -> p (a n)")))
            turn(act, t, "exp", lambda: act.activation(
                weights[:, 0:TOP_K], best[:, 0:TOP_K], ACT.Exp, bias=minus[:, :], accum_out=total[:, :]))
            turn(act, t, "wT", lambda: act.copy(xT[:, :, :], tp[:, :, :]))
            turn(act, t, "w_spectrum", lambda: act.copy(ws[:, :, :], mm[:, :, :]))
            turn(act, t, "aT", lambda: act.copy(xT[:, :, :], tp[:, :, :]))

    def vector(dve):
        dve.wait_ge(tables, 48)
        dve.memset(power[:, KT // 2, :], 0.0).then_inc(cleared, 1)

        def product(out, a, b):
            return lambda: dve.tensor_tensor(out, a, b, ALU.mult)
        with dve.Fori(0, NB) as t:
            turn(dve, t, "re2", product(sq[:, 0, :], xs[:, 0, :], xs[:, 0, :]))
            turn(dve, t, "im2", product(sq[:, 1, :], xs[:, 1, :], xs[:, 1, :]))
            turn(dve, t, "power", lambda: dve.tensor_tensor(flat[:, 0:HALF], sq[:, 0, :], sq[:, 1, :], ALU.add))
            turn(dve, t, "power_0", lambda: dve.tensor_copy(flat[:, 0:1], sq[:, 0, 0:1]))
            turn(dve, t, "power_512", lambda: dve.tensor_copy(flat[:, HALF:HALF + 1], sq[:, 1, 0:1]))
            after(dve, done, t * S + TURNS.index("best"))
            dve.memset(dummy[:, :], 0.0)
            dve.max(best[:, :], corr[:, :]).then_inc(done, 1)
            after(dve, done, t * S + TURNS.index("at"))
            dve.memset(dummy[:, :], 0.0)
            dve.max_index(at[:, :], best[:, :], corr[:, :]).then_inc(done, 1)
            turn(dve, t, "at_f", lambda: dve.tensor_copy(at_f[:, :], at[:, :]))
            turn(dve, t, "minus", lambda: dve.tensor_scalar(minus[:, :], best[:, 0:1], -1.0, None, ALU.mult))
            turn(dve, t, "rtotal", lambda: dve.reciprocal(rtotal[:, :], total[:, :]))
            turn(dve, t, "weights", lambda: dve.tensor_scalar(
                weights[:, 0:TOP_K], weights[:, 0:TOP_K], rtotal[:, :], None, ALU.mult))
            for j in range(TOP_K):
                dst = spread if j == 0 else one
                turn(dve, t, "spread_0" if j == 0 else f"one_{j}", lambda: dve.tensor_scalar(
                    dst[:, :], lag_row[:, :], at_f[:, j:j + 1], weights[:, j:j + 1], ALU.is_equal, ALU.mult))
                if j:
                    turn(dve, t, f"spread_{j}", lambda: dve.tensor_tensor(
                        spread[:, :], spread[:, :], one[:, :], ALU.add))
            turn(dve, t, "rr", product(sq[:, 0, :], xs[:, 0, :], ws[:, 0, :]))
            turn(dve, t, "ii", product(sq[:, 1, :], xs[:, 1, :], ws[:, 1, :]))
            turn(dve, t, "re", lambda: dve.tensor_tensor(am[:, 0, :], sq[:, 0, :], sq[:, 1, :], ALU.add))
            turn(dve, t, "ir", product(sq[:, 0, :], xs[:, 1, :], ws[:, 0, :]))
            turn(dve, t, "ri", product(sq[:, 1, :], xs[:, 0, :], ws[:, 1, :]))
            turn(dve, t, "im", lambda: dve.tensor_tensor(am[:, 1, :], sq[:, 0, :], sq[:, 1, :], ALU.subtract))
            turn(dve, t, "re_0", product(am[:, 0, 0:1], xs[:, 0, 0:1], ws[:, 0, 0:1]))
            turn(dve, t, "re_512", product(am[:, 1, 0:1], xs[:, 1, 0:1], ws[:, 1, 0:1]))
            turn(dve, t, "added", lambda: dve.tensor_tensor(
                row(h, t), row(h, t), mm[:, :, :].rearrange("p a n -> p (a n)"), ALU.add))

    def tensor(pe):
        pe.wait_ge(tables, 48)

        def turned(t, name, src, tiles):
            after(pe, done, t * S + TURNS.index(name))
            for k in range(tiles):
                last = pe.transpose(tp[:, k, :], src[:, k * P:(k + 1) * P], ident[:, :])
            last.then_inc(done, 1)

        def transform(t, name, table, tiles):
            after(pe, done, t * S + TURNS.index(name))
            for c in range(2):
                for k in range(tiles):
                    last = pe.matmul(mm[:, c, :], xT[:, k, :], table[:, k, c * BANK:(c + 1) * BANK],
                                     start=(k == 0), stop=(k == tiles - 1))
            last.then_inc(done, 1)

        with pe.Fori(0, NB) as t:
            turned(t, "x_turned", xn, KT)
            transform(t, "x_dft", fwd, KT)
            turned(t, "power_turned", flat, KT // 2 + 1)
            transform(t, "corr_mm", inv, KT // 2 + 1)
            turned(t, "w_turned", spread, KT)
            transform(t, "w_dft", fwd, KT)
            turned(t, "a_turned", am[:, :, :].rearrange("p a n -> p (a n)"), KT)
            transform(t, "agg", inv, KT)

    return sync, scalar, vector, tensor


def delay_stage(nc, h, ident, f_dram, g_dram, lags, rstd, shift, flag):
    with ExitStack() as ctx:
        def sb(name, shape, dt=F32):
            return ctx.enter_context(nc.sbuf_tensor(name, shape, dt))

        gain = sb("dl_gain", [P, NB])
        gained = ctx.enter_context(nc.semaphore("dl_gained"))
        sync, scalar, vector, tensor = delay_average(nc, ctx, h, ident, f_dram, g_dram, lags, rstd, shift)
        ACT_TILES = 6

        with nc.Block() as block:

            def only_zero(e):
                return e.value_load(flag[0:1, 0:1], min_val=0, max_val=1)

            @block.sync
            def _(sp):
                with sp.If(only_zero(sp) < 1):
                    sync(sp)

            @block.tensor
            def _(pe):
                with pe.If(only_zero(pe) < 1):
                    tensor(pe)

            @block.vector
            def _(dve):
                with dve.If(only_zero(dve) < 1):
                    vector(dve)
                with dve.Else():
                    dve.tensor_scalar(gain[:, :], rstd[:, :], 1.0, None, ALU.add).then_inc(gained, 1)
                    dve.wait_ge(gained, 1)
                    for t in range(ACT_TILES, NB):
                        dve.tensor_scalar(h[:, t, :], h[:, t, :], gain[:, t:t + 1], shift[:, t:t + 1],
                                          ALU.mult, ALU.add)

            @block.scalar
            def _(act):
                with act.If(only_zero(act) < 1):
                    scalar(act)
                with act.Else():
                    act.wait_ge(gained, 1)
                    for t in range(ACT_TILES):
                        act.activation(h[:, t, :], h[:, t, :], ACT.Identity,
                                       bias=shift[:, t:t + 1], scale=gain[:, t:t + 1])


DK = 32
QK = EXPERTS * DK
QKA = 2 * QK + ER


def final_stage(nc, h, ident, w_t, qka, bm, bias, out_dram):
    SC = float(DK) ** -0.5
    with ExitStack() as ctx:
        def sb(name, shape, dt=F32):
            return ctx.enter_context(nc.sbuf_tensor(name, shape, dt))

        def sem(name):
            return ctx.enter_context(nc.semaphore(name))

        w = Weight(nc, ctx, "fn_w", w_t).add_high(nc, ctx)
        qka.add_high(nc, ctx)
        bm.add_high(nc, ctx)
        rows = Rows(nc, ctx, "fn", h, ident)
        bias_row = sb("fn_bias", [P, L])
        q = sb("fn_q", [P, QK])
        qk = sb("fn_qk", [P, QK])
        s8, w8 = sb("fn_s8", [P, EXPERTS]), sb("fn_w8", [P, EXPERTS])
        col = {n: sb(f"fn_{n}", [P, 1]) for n in ("top", "ntop", "total", "rtotal")}
        wh = sb("fn_wh", [P, ER])
        wt_hi, wt_lo = sb("fn_wthi", [P, P], F32R), sb("fn_wtlo", [P, P], F32R)
        ka = ctx.enter_context(nc.psum_tensor("fn_ka", [P, BANK], F32))
        qp = ctx.enter_context(nc.psum_tensor("fn_qp", [P, BANK], F32))
        out = ctx.enter_context(nc.psum_tensor("fn_out", [P, 2, 2, BANK], F32))
        bias_in, ka_done, q_done, gate = sem("fn_bias_in"), sem("fn_ka_done"), sem("fn_q_done"), sem("fn_gate")
        exp_done, biased = sem("fn_exp_done"), sem("fn_biased")
        wh_done, wt_mm, wthi_done, wtlo_done = sem("fn_wh_done"), sem("fn_wt_mm"), sem("fn_wthi"), sem("fn_wtlo")
        out_mm, added = sem("fn_out_mm"), sem("fn_added")
        stored = sem("fn_stored")
        prime(nc, rows.sems + [ka_done, q_done, gate, exp_done, biased, wh_done, wt_mm, wthi_done, wtlo_done,
                               out_mm, added])
        GATE_LINKS = 6

        with nc.Block() as block:

            @block.sync
            def _(sp):
                w.load(sp)
                sp.dma_start(bias_row[:, :], bias).then_inc(bias_in, 16)
                with sp.Fori(0, NB) as t:
                    after(sp, added, t + 1)
                    sp.dma_start(out_dram[bass.ds(t, 1), :, :].rearrange("b p l -> (b p) l"), row(h, t))\
                      .then_inc(stored, 16)
                sp.wait_ge(stored, 16 * NB)

            @block.gpsimd
            def _(pool):
                qka.low(pool)
                w.low(pool, range(KT // 2))
                pool.wait_ge(bias_in, 16)
                with pool.Fori(0, NB) as t:
                    after(pool, rows.normed, t + 1)
                    pool.tensor_tensor(row(h, t), row(h, t), bias_row[:, :], ALU.add).then_inc(biased, 1)

            @block.scalar
            def _(act):
                def before():
                    qka.high(act)
                    rows.normalize(act, 0, 0)
                    rows.high(act, 0, 0, out_mm, 0)
                    rows.normalize(act, 0, 1)
                    w.high(act)
                    bm.high(act)

                def body(g, i, t, on):
                    after(act, q_done, t + 1)
                    after(act, gate, t * GATE_LINKS)
                    act.copy(q[:, :], qp[:, 0:QK]).then_inc(exp_done, 1)
                    if on(1):
                        rows.high(act, t + 1, (i + 1) % 2, out_mm, t)
                    after(act, gate, t * GATE_LINKS + 4)
                    act.activation(s8[:, :], s8[:, :], ACT.Exp, bias=col["ntop"][:, :], scale=SC,
                                   accum_out=col["total"][:, :]).then_inc(exp_done, 1)
                    if on(2):
                        rows.normalize(act, g + (i + 2) // GROUP, (i + 2) % GROUP)
                    after(act, wt_mm, t + 1)
                    act.copy(wt_hi[:, :], qp[:, 0:P]).then_inc(wthi_done, 1)
                tile_steps(act, before, body, lambda: None)

            @block.vector
            def _(dve):
                def before():
                    rows.stats(dve, 0, range(GROUP))
                    rows.low(dve, 0, 0)
                    w.low(dve, range(KT // 2, KT))
                    bm.low(dve)

                def gate_of(t):
                    link = Links(dve, gate, t * GATE_LINKS + 1)
                    after(dve, ka_done, t + 1)
                    after(dve, exp_done, 2 * t + 1)
                    link(dve.tensor_tensor(qk[:, :], ka[:, 0:QK], q[:, :], ALU.mult))
                    link(dve.tensor_reduce(s8[:, :], qk[:, :].rearrange("p (e d) -> p e d", d=DK), AX.X, ALU.add))
                    link(dve.tensor_reduce(col["top"][:, :], s8[:, :], AX.X, ALU.max))
                    link(dve.tensor_scalar(col["ntop"][:, :], col["top"][:, :], -SC, None, ALU.mult))
                    after(dve, exp_done, 2 * t + 2)
                    link(dve.reciprocal(col["rtotal"][:, :], col["total"][:, :]))
                    link(dve.tensor_scalar(w8[:, :], s8[:, :], col["rtotal"][:, :], None, ALU.mult))
                    assert link.n == GATE_LINKS
                    after(dve, wt_mm, t)
                    dve.tensor_tensor(wh[:, :].rearrange("p (e r) -> p e r", r=RANK),
                                      ka[:, QK:QK + ER].rearrange("p (e r) -> p e r", r=RANK),
                                      w8[:, :].rearrange("p (e a) -> p e a", a=1).to_broadcast([P, EXPERTS, RANK]),
                                      ALU.mult).then_inc(wh_done, 1)

                def add(t, par):
                    after(dve, out_mm, t + 1)
                    after(dve, biased, t + 1)
                    hb = row(h, t)
                    dve.tensor_tensor(hb, hb, out[:, par, :, :].rearrange("p a n -> p (a n)"), ALU.add)\
                       .then_inc(added, 1)

                def body(g, i, t, on):
                    gate_of(t)
                    if on(1):
                        rows.low(dve, t + 1, (i + 1) % 2)
                    if i < 2 and on(GROUP):
                        rows.stats(dve, g + 1, (2 * i, 2 * i + 1))
                    after(dve, wthi_done, t + 1)
                    dve.tensor_tensor(wt_lo[:, :], qp[:, 0:P], wt_hi[:, :].bitcast(F32), ALU.subtract)\
                       .then_inc(wtlo_done, 1)
                    add(t, i % 2)
                tile_steps(dve, before, body, lambda: None)

            @block.tensor
            def _(pe):
                def group(par, dst, weight, width, lo, hi, final=True):
                    xh, xl = rows.x_hi[par], rows.x_lo[par]
                    for k in range(KT):
                        cols = slice(k * width + lo, k * width + hi)
                        pe.matmul(dst, xh[:, k, :], weight.hi[:, cols], start=(k == 0), stop=False)
                        pe.matmul(dst, xh[:, k, :], weight.lo[:, cols], start=False, stop=False)
                        mm = pe.matmul(dst, xl[:, k, :], weight.hi[:, cols], start=False,
                                       stop=(final and k == KT - 1))
                    return mm

                def body(g, i, t, on):
                    par = i % 2
                    after(pe, rows.lo_done, t + 1)
                    if early(t, 1):
                        qka.ready(pe)
                    after(pe, wtlo_done, t)
                    group(par, qp[:, 0:QK], qka, QKA, 0, QK).then_inc(q_done, 1)
                    after(pe, wh_done, t)
                    group(par, ka[:, 0:QK + ER], qka, QKA, QK, QKA).then_inc(ka_done, 1)
                    if on(1):
                        rows.turn(pe, t + 1)
                    if early(t, 1):
                        w.ready(pe)
                        bm.ready(pe)
                    else:
                        after(pe, added, t - 1)
                    group(par, out[:, par, 0, :], w, L, 0, BANK, final=False)
                    after(pe, wh_done, t + 1)
                    pe.transpose(qp[:, 0:P], wh[:, :], ident[:, :]).then_inc(wt_mm, 1)
                    group(par, out[:, par, 1, :], w, L, BANK, L, final=False)
                    after(pe, wtlo_done, t + 1)
                    for c in range(2):
                        cols = slice(c * BANK, (c + 1) * BANK)
                        dst = out[:, par, c, :]
                        pe.matmul(dst, wt_hi[:, :], bm.hi[:, cols], start=False, stop=False)
                        pe.matmul(dst, wt_hi[:, :], bm.lo[:, cols], start=False, stop=False)
                        mm = pe.matmul(dst, wt_lo[:, :], bm.hi[:, cols], start=False, stop=True)
                    mm.then_inc(out_mm, 1)
                tile_steps(pe, lambda: rows.turn(pe, 0), body, lambda: None)


def audio_tower(nc, x, conv_w, dw_w, chan, pw_t, w_qkv, w_o, rope, a_route, bw, experts, dft_fwd, dft_inv,
                lag_cos, lags, w_t, qka_t, bm_t, bias, out):
    with ExitStack() as ctx:
        h = ctx.enter_context(nc.sbuf_tensor("h", [P, NB, L], F32))
        ident = ctx.enter_context(nc.sbuf_tensor("ident", [P, P], F32))
        ones_mean = ctx.enter_context(nc.sbuf_tensor("ones_mean", [P, P], F32))
        setup_constants(nc, ctx, ident, ones_mean)
        rstd, shift = (ctx.enter_context(nc.sbuf_tensor(n, [P, NB], F32)) for n in ("rstd", "shift"))
        with ExitStack() as inner:
            rows = QuarterRows(nc, inner, h, ident)
            w_stage = WeightStage(nc, inner, w_qkv)
            conv_stage(nc, h, ident, ones_mean, x, conv_w, dw_w, chan, pw_t, rows, w_stage)
            attention_stage(nc, h, ident, w_o, rope, rows, w_stage, rstd, shift)
        middle_stages(nc, h, ident, rstd, shift, (a_route, bw, experts), (dft_fwd, dft_inv, lag_cos, lags),
                      (w_t, qka_t, bm_t, bias), out)


def middle_stages(nc, h, ident, rstd, shift, mixture, delay, final, out):
    dft_fwd, dft_inv, lag_cos, lags = delay
    w_t, qka_t, bm_t, bias = final
    with ExitStack() as ctx:
        flag = ctx.enter_context(nc.sbuf_tensor("dl_flag", [1, 1], I32))
        qka, bm = Weight(nc, ctx, "fn_qka", qka_t), Weight(nc, ctx, "fn_bm", bm_t)
        with ExitStack() as inner:
            tables = ScreenTables(nc, inner, dft_fwd, lag_cos)
            stats = ScreenStats(nc, inner, h, rstd, shift)
            mixture_stage(nc, h, ident, *mixture, tables, stats, rstd, shift)
            screen(nc, h, ident, tables, stats, flag, (qka, bm))
        delay_stage(nc, h, ident, dft_fwd, dft_inv, lags, rstd, shift, flag)
        final_stage(nc, h, ident, w_t, qka, bm, bias, out)


def _layout(a):
    import numpy as np

    def flat(m):
        return np.ascontiguousarray(m)

    def moving(w):
        return flat(w.reshape(w.shape[0], KT, P).transpose(2, 1, 0).reshape(P, KT * w.shape[0]))

    def head_tiles(w):
        n = w.shape[0] // P
        return w.reshape(n, P, KT, P).transpose(0, 3, 2, 1).reshape(n, P, L)

    def packed(m):
        return flat(m.reshape(-1, P, m.shape[1]).transpose(1, 0, 2).reshape(P, -1).astype(np.float32))

    taps = np.zeros((P, C_IN, 2 * PAIRS), np.float32)
    taps[:, :, :TAPS] = a["L0_tok_conv_in_w"]
    q = head_tiles(a["L0_attn_Wq"]).reshape(KV, HEADS, P, L)
    k, v = (head_tiles(a[f"L0_attn_{n}"])[:, None] for n in ("Wk", "Wv"))
    inv_freq = (1.0 / np.power(np.float32(500000.0), np.arange(0, D, 2, dtype=np.float32) / np.float32(D)))
    angle = np.arange(P, dtype=np.float32)[:, None] * inv_freq.astype(np.float32)[None]
    angle = np.concatenate([angle, angle], 1).astype(np.float64).T
    turn = np.sin(angle)
    turn[D // 2:] *= -1.0
    n = np.arange(L)
    w = 2 * np.pi * (n[:, None] * n[None, :] % L) / L
    cos, sin = np.cos(w), np.sin(w)
    fwd = np.concatenate([cos[:, :HALF], cos[:, HALF:HALF + 1], -sin[:, 1:HALF]], 1)
    twice = np.where(n[:HALF, None] == 0, 1.0, 2.0)
    inv = np.concatenate([cos[:HALF] * twice, cos[HALF:HALF + 1], -2 * sin[1:HALF]], 0) / L

    def all_rows(r):
        return flat(np.broadcast_to(r, (P, r.shape[0])))

    return {
        "x": flat(a["x"]),
        "conv_w": flat(taps.reshape(P, C_IN, PAIRS, 2).transpose(3, 1, 2, 0).reshape(P, PAIRS * P)),
        "dw_w": flat(a["L0_tok_dw_w"].reshape(P, DW)),
        "chan": flat(np.stack([a[f"L0_tok_{m}"] for m in ("dw_b", "gn1_w", "gn1_b", "gn2_w", "gn2_b")], 1)),
        "pw_t": flat(a["L0_tok_pw_w"][:, :, 0].T),
        "w_qkv": flat(np.concatenate([k, v, q], 1)),
        "w_o": flat(a["L0_attn_Wo"].T.reshape(KV, HEADS, D, L)),
        "rope": flat(np.stack([np.cos(angle), turn], 1).astype(np.float32)),
        "a_route": moving(np.concatenate([a["L0_ffn_A"].reshape(ER, L), a["L0_ffn_route_w"]], 0)),
        "bw": flat(a["L0_ffn_Bw"].transpose(0, 2, 1).reshape(ER, L)),
        "experts": all_rows(np.arange(EXPERTS, dtype=np.float32)),
        "dft_fwd": packed(fwd),
        "dft_inv": packed(inv),
        "lag_cos": packed(inv[:HALF, 1:HALF + 1][np.r_[0:HALF:2, 1:HALF:2]]),
        "lags": all_rows(np.arange(L, dtype=np.float32)),
        "w_t": moving(a["L1_ffn_W"]),
        "qka_t": moving(np.concatenate([a["L1_ffn_Wq"], a["L1_ffn_Wk"], a["L1_ffn_A"].reshape(ER, L)], 0)),
        "bm_t": flat(a["L1_ffn_Bm"].transpose(0, 2, 1).reshape(ER, L)),
        "bias": all_rows(a["L1_ffn_b"]),
    }


def kernel(**inputs):
    import numpy as _np
    import concourse.bacc as _bacc
    from concourse import mybir as _mybir
    from concourse.bass_utils import run_bass_kernel_spmd as _run

    nc = _bacc.Bacc("TRN2", target_bir_lowering=False, num_devices=1)
    arrays, args = {}, []
    for name, a in _layout({k: _np.asarray(v) for k, v in inputs.items()}).items():
        arrays[f"in_{name}_dram"] = a
        args.append(nc.dram_tensor(f"in_{name}_dram", a.shape, _mybir.dt.from_np(a.dtype), kind="ExternalInput").ap())
    out = nc.dram_tensor("out_dram", (NB, P, L), _mybir.dt.float32, kind="ExternalOutput").ap()
    audio_tower(nc, *args, out)
    r = _run(nc, [arrays], core_ids=[0])
    return r.results[0]["out_dram"]
```
